# Optimizing a Trainium2 kernel written in Bass

```python
import numpy as np
import jax
import jax.numpy as jnp

def _softmax(x, axis=-1):
    return jax.nn.softmax(x, axis=axis)

def _gelu(x):
    return jax.nn.gelu(x, approximate=True)

def _silu(x):
    return jax.nn.silu(x)

def _sigmoid(x):
    return jax.nn.sigmoid(x)

def _layernorm(x, axis=-1, eps=1e-05):
    m = jnp.mean(x, axis=axis, keepdims=True)
    v = jnp.var(x, axis=axis, keepdims=True)
    return (x - m) / jnp.sqrt(v + eps)

def _scatter_add(tgt, idx, src, axis=0):
    return tgt.at[idx].add(src)

def _segment_sum(src, seg, n):
    return jax.ops.segment_sum(src, seg, n)
kernel_name = 'mk_xattn_seq_d2_seqx_r4_b61659'

def setup_inputs(seed: int=0):
    np.random.seed(seed)
    _w = jnp.asarray

    def _rec_inputs():
        import jax
        import jax.numpy as jnp
        _rk = jax.random.key(seed)
        x = -0.000125 + 0.9999 * jax.random.normal(jax.random.fold_in(_rk, 1), (32, 112, 512), jnp.float32)
        _lenS = 112 - jax.random.randint(jax.random.fold_in(_rk, 7), (32,), 0, max(1, 112 // 4) + 1, jnp.int32)
        _lenS2 = 375 - jax.random.randint(jax.random.fold_in(_rk, 8), (32,), 0, max(1, 375 // 4) + 1, jnp.int32)
        _ctx_1024P = jax.random.normal(jax.random.fold_in(_rk, 11), (32, 16, 256), jnp.float32)
        _ctx_1024c = jax.random.dirichlet(jax.random.fold_in(_rk, 511), 0.3 * jnp.ones((16,), jnp.float32), (32, 375))
        _ctx_1024t = jnp.einsum('bsk,bkd->bsd', _ctx_1024c, _ctx_1024P)
        _ctx_1024t = _ctx_1024t * jax.lax.rsqrt(jnp.mean(jnp.square(_ctx_1024t)) + 1e-12) * 0.953939
        ctx_1024 = 4.13588e-05 + 0.999923 * (_ctx_1024t + 0.3 * jax.random.normal(jax.random.fold_in(_rk, 611), (32, 375, 256), jnp.float32))
        pos_1xS = jnp.broadcast_to(jnp.arange(112, dtype=jnp.int32), (1, 112))
        _validS = jnp.arange(112)[None, :] < _lenS[:, None]
        _validS2 = jnp.arange(375)[None, :] < _lenS2[:, None]
        _causal = jnp.tril(jnp.ones((112, 112), dtype=bool))
        mask_BxS_ik0 = jnp.where(jnp.broadcast_to(_validS[:, :], (32, 112)), 0, 1).astype(jnp.int32)
        return (x, ctx_1024, pos_1xS, mask_BxS_ik0)
    x, ctx_1024, pos_1xS, mask_BxS_ik0 = _rec_inputs()

    def _L0_xattn_setup():
        import jax, jax.numpy as jnp
        import numpy as np
        EPS = 1e-06

        def _rmsnorm(x, w):
            var = jnp.mean(jnp.square(x), axis=-1, keepdims=True)
            return x * jax.lax.rsqrt(var + EPS) * w
        key = jax.random.key(seed)
        ks = jax.random.split(key, 6)
        B, N, M = (4, 1024, 512)
        d_model, memory_dim = (512, 256)
        hidden_states = jax.random.normal(ks[0], (B, N, d_model), dtype=jnp.float32)
        memory = jax.random.normal(ks[1], (B, M, memory_dim), dtype=jnp.float32)
        W_mem = jax.random.normal(ks[2], (d_model, memory_dim), dtype=jnp.float32) / np.sqrt(memory_dim)
        W_gate = jax.random.normal(ks[3], (d_model, 2 * d_model), dtype=jnp.float32) / np.sqrt(2 * d_model)
        b_gate = jax.random.normal(ks[4], (d_model,), dtype=jnp.float32) * 0.01
        norm_w = jnp.ones((d_model,), dtype=jnp.float32)
        return {'hidden_states': hidden_states, 'memory': memory, 'W_mem': W_mem, 'W_gate': W_gate, 'b_gate': b_gate, 'norm_w': norm_w}
    _L0_xattn_all = _L0_xattn_setup()
    _L0_xattn_in = {k: v for k, v in _L0_xattn_all.items() if k in ('W_mem', 'W_gate', 'b_gate', 'norm_w')}
    del _L0_xattn_all

    def _L1_xattn_setup():
        import jax, jax.numpy as jnp
        import numpy as np
        H = 512
        NH = 16
        HD = H // NH
        CH = 256
        CC = 256
        CHD = CC // NH
        I = 1376
        B = 2
        L = 512
        LE = 256
        EPS = 1e-06

        def rms_norm(x, w):
            xf = x.astype(jnp.float32)
            var = jnp.mean(xf * xf, axis=-1, keepdims=True)
            return (w * (xf * jax.lax.rsqrt(var + EPS))).astype(x.dtype)

        def expert_mask(tt):
            vm = jnp.zeros(tt.shape, dtype=bool)
            vm = vm.at[:, :-1].set((tt[:, :-1] == 1) & (tt[:, 1:] == 1))
            return vm

        def rotate_half(x):
            d = x.shape[-1] // 2
            return jnp.concatenate([-x[..., d:], x[..., :d]], axis=-1)

        def apply_rotary(q, k, position_ids, seq_len):
            inv = 1.0 / 10000.0 ** (jnp.arange(0, HD, 2, dtype=jnp.float32) / HD)
            t = jnp.arange(seq_len, dtype=jnp.float32)
            freqs = jnp.outer(t, inv)
            emb = jnp.concatenate([freqs, freqs], axis=-1)
            cos = jnp.cos(emb)[position_ids][:, None].astype(q.dtype)
            sin = jnp.sin(emb)[position_ids][:, None].astype(q.dtype)
            return (q * cos + rotate_half(q) * sin, k * cos + rotate_half(k) * sin)

        def sdpa(q, k, v, causal):
            scale = 1.0 / np.sqrt(q.shape[-1])
            scores = jnp.einsum('bhqd,bhkd->bhqk', q * scale, k)
            if causal:
                mask = jnp.tril(jnp.ones((q.shape[-2], k.shape[-2]), dtype=bool))
                scores = jnp.where(mask, scores, jnp.finfo(jnp.float32).min)
            p = jax.nn.softmax(scores.astype(jnp.float32), axis=-1).astype(q.dtype)
            return jnp.einsum('bhqk,bhkd->bhqd', p, v)

        def heads(x, nh, hd):
            b, l, _ = x.shape
            return x.reshape(b, l, nh, hd).transpose(0, 2, 1, 3)
        key = jax.random.key(seed)
        ks = jax.random.split(key, 20)
        s = 0.02
        f32 = jnp.float32
        return {'hidden_states': jax.random.normal(ks[0], (B, L, H), f32), 'encoder_outputs': jax.random.normal(ks[1], (B, LE, CH), f32), 'token_type_ids': jax.random.randint(ks[2], (B, L), 0, 2, jnp.int32), 'position_ids': jnp.arange(L, dtype=jnp.int32)[None, :], 'ln_in_w': jnp.ones((H,), f32), 'ln_post_attn_w': jnp.ones((H,), f32), 'ln_post_cross_w': jnp.ones((H,), f32), 'v_qkv': jax.random.normal(ks[3], (H, 3 * H), f32) * s, 'l_qkv': jax.random.normal(ks[4], (H, 3 * H), f32) * s, 'v_dense': jax.random.normal(ks[5], (H, H), f32) * s, 'l_dense': jax.random.normal(ks[6], (H, H), f32) * s, 'cq_w': jax.random.normal(ks[7], (H, CC), f32) * s, 'ckv_w': jax.random.normal(ks[8], (CH, 2 * CC), f32) * s, 'cdense_w': jax.random.normal(ks[9], (CC, H), f32) * s, 'v_gate': jax.random.normal(ks[10], (H, I), f32) * s, 'v_up': jax.random.normal(ks[11], (H, I), f32) * s, 'v_down': jax.random.normal(ks[12], (I, H), f32) * s, 'l_gate': jax.random.normal(ks[13], (H, I), f32) * s, 'l_up': jax.random.normal(ks[14], (H, I), f32) * s, 'l_down': jax.random.normal(ks[15], (I, H), f32) * s}
    _L1_xattn_all = _L1_xattn_setup()
    _L1_xattn_in = {k: v for k, v in _L1_xattn_all.items() if k in ('ln_in_w', 'ln_post_attn_w', 'ln_post_cross_w', 'v_qkv', 'l_qkv', 'v_dense', 'l_dense', 'cq_w', 'ckv_w', 'cdense_w', 'v_gate', 'v_up', 'v_down', 'l_gate', 'l_up', 'l_down')}
    del _L1_xattn_all
    return {'x': x, 'ctx_1024': ctx_1024, 'pos_1xS': pos_1xS, 'mask_BxS_ik0': mask_BxS_ik0, 'L0_xattn_W_mem': _L0_xattn_in['W_mem'], 'L0_xattn_W_gate': _L0_xattn_in['W_gate'], 'L0_xattn_b_gate': _L0_xattn_in['b_gate'], 'L0_xattn_norm_w': _L0_xattn_in['norm_w'], 'L1_xattn_ln_in_w': _L1_xattn_in['ln_in_w'], 'L1_xattn_ln_post_attn_w': _L1_xattn_in['ln_post_attn_w'], 'L1_xattn_ln_post_cross_w': _L1_xattn_in['ln_post_cross_w'], 'L1_xattn_v_qkv': _L1_xattn_in['v_qkv'], 'L1_xattn_l_qkv': _L1_xattn_in['l_qkv'], 'L1_xattn_v_dense': _L1_xattn_in['v_dense'], 'L1_xattn_l_dense': _L1_xattn_in['l_dense'], 'L1_xattn_cq_w': _L1_xattn_in['cq_w'], 'L1_xattn_ckv_w': _L1_xattn_in['ckv_w'], 'L1_xattn_cdense_w': _L1_xattn_in['cdense_w'], 'L1_xattn_v_gate': _L1_xattn_in['v_gate'], 'L1_xattn_v_up': _L1_xattn_in['v_up'], 'L1_xattn_v_down': _L1_xattn_in['v_down'], 'L1_xattn_l_gate': _L1_xattn_in['l_gate'], 'L1_xattn_l_up': _L1_xattn_in['l_up'], 'L1_xattn_l_down': _L1_xattn_in['l_down']}

def reference(x, ctx_1024, pos_1xS, mask_BxS_ik0, L0_xattn_W_mem, L0_xattn_W_gate, L0_xattn_b_gate, L0_xattn_norm_w, L1_xattn_ln_in_w, L1_xattn_ln_post_attn_w, L1_xattn_ln_post_cross_w, L1_xattn_v_qkv, L1_xattn_l_qkv, L1_xattn_v_dense, L1_xattn_l_dense, L1_xattn_cq_w, L1_xattn_ckv_w, L1_xattn_cdense_w, L1_xattn_v_gate, L1_xattn_v_up, L1_xattn_v_down, L1_xattn_l_gate, L1_xattn_l_up, L1_xattn_l_down):
    import jax
    import jax.numpy as jnp

    def _L0_xattn_ref(hidden_states, memory, W_mem, W_gate, b_gate, norm_w):
        import jax, jax.numpy as jnp
        import numpy as np
        EPS = 1e-06

        def _rmsnorm(x, w):
            var = jnp.mean(jnp.square(x), axis=-1, keepdims=True)
            return x * jax.lax.rsqrt(var + EPS) * w
        D = hidden_states.shape[-1]
        memory_proj = jnp.einsum('bme,de->bmd', memory, W_mem)
        scores = jnp.einsum('bnd,bmd->bnm', hidden_states, memory_proj) / jnp.sqrt(jnp.float32(D))
        attn = jax.nn.softmax(scores, axis=-1)
        memory_context = jnp.einsum('bnm,bmd->bnd', attn, memory_proj)
        gate_input = jnp.concatenate([hidden_states, memory_context], axis=-1)
        gate = jax.nn.sigmoid(jnp.einsum('bnf,df->bnd', gate_input, W_gate) + b_gate)
        fused = hidden_states + gate * memory_context
        return _rmsnorm(fused, norm_w)

    def _L1_xattn_ref(hidden_states, encoder_outputs, token_type_ids, position_ids, ln_in_w, ln_post_attn_w, ln_post_cross_w, v_qkv, l_qkv, v_dense, l_dense, cq_w, ckv_w, cdense_w, v_gate, v_up, v_down, l_gate, l_up, l_down):
        import jax, jax.numpy as jnp
        import numpy as np
        H = 512
        NH = 16
        HD = H // NH
        CH = 256
        CC = 256
        CHD = CC // NH
        I = 1376
        B = 2
        L = 512
        LE = 256
        EPS = 1e-06

        def rms_norm(x, w):
            xf = x.astype(jnp.float32)
            var = jnp.mean(xf * xf, axis=-1, keepdims=True)
            return (w * (xf * jax.lax.rsqrt(var + EPS))).astype(x.dtype)

        def expert_mask(tt):
            vm = jnp.zeros(tt.shape, dtype=bool)
            vm = vm.at[:, :-1].set((tt[:, :-1] == 1) & (tt[:, 1:] == 1))
            return vm

        def rotate_half(x):
            d = x.shape[-1] // 2
            return jnp.concatenate([-x[..., d:], x[..., :d]], axis=-1)

        def apply_rotary(q, k, position_ids, seq_len):
            inv = 1.0 / 10000.0 ** (jnp.arange(0, HD, 2, dtype=jnp.float32) / HD)
            t = jnp.arange(seq_len, dtype=jnp.float32)
            freqs = jnp.outer(t, inv)
            emb = jnp.concatenate([freqs, freqs], axis=-1)
            cos = jnp.cos(emb)[position_ids][:, None].astype(q.dtype)
            sin = jnp.sin(emb)[position_ids][:, None].astype(q.dtype)
            return (q * cos + rotate_half(q) * sin, k * cos + rotate_half(k) * sin)

        def sdpa(q, k, v, causal):
            scale = 1.0 / np.sqrt(q.shape[-1])
            scores = jnp.einsum('bhqd,bhkd->bhqk', q * scale, k)
            if causal:
                mask = jnp.tril(jnp.ones((q.shape[-2], k.shape[-2]), dtype=bool))
                scores = jnp.where(mask, scores, jnp.finfo(jnp.float32).min)
            p = jax.nn.softmax(scores.astype(jnp.float32), axis=-1).astype(q.dtype)
            return jnp.einsum('bhqk,bhkd->bhqd', p, v)

        def heads(x, nh, hd):
            b, l, _ = x.shape
            return x.reshape(b, l, nh, hd).transpose(0, 2, 1, 3)
        b, l, _ = hidden_states.shape
        vm = expert_mask(token_type_ids)[..., None]
        residual = hidden_states
        x = rms_norm(hidden_states, ln_in_w)
        mixed = jnp.where(vm, x @ v_qkv, x @ l_qkv)
        q, k, v = jnp.split(mixed, 3, axis=-1)
        q, k, v = (heads(q, NH, HD), heads(k, NH, HD), heads(v, NH, HD))
        q, k = apply_rotary(q, k, position_ids, l)
        ctx = sdpa(q, k, v, causal=True)
        ctx = ctx.transpose(0, 2, 1, 3).reshape(b, l, H)
        attn_out = jnp.where(vm, ctx @ v_dense, ctx @ l_dense)
        hidden_states = residual + attn_out
        ci = rms_norm(hidden_states, ln_post_cross_w)
        cq = heads(ci @ cq_w, NH, CHD)
        ckv = encoder_outputs @ ckv_w
        ck, cv = jnp.split(ckv, 2, axis=-1)
        ck, cv = (heads(ck, NH, CHD), heads(cv, NH, CHD))
        cctx = sdpa(cq, ck, cv, causal=False)
        cctx = cctx.transpose(0, 2, 1, 3).reshape(b, l, CC)
        hidden_states = hidden_states + cctx @ cdense_w
        mi = rms_norm(hidden_states, ln_post_attn_w)
        v_out = jax.nn.silu(mi @ v_gate) * (mi @ v_up) @ v_down
        l_out = jax.nn.silu(mi @ l_gate) * (mi @ l_up) @ l_down
        hidden_states = hidden_states + jnp.where(vm, v_out, l_out)
        return hidden_states
    x = _L0_xattn_ref(x, ctx_1024, L0_xattn_W_mem, L0_xattn_W_gate, L0_xattn_b_gate, L0_xattn_norm_w)
    x = _L1_xattn_ref(x, ctx_1024, mask_BxS_ik0, pos_1xS, L1_xattn_ln_in_w, L1_xattn_ln_post_attn_w, L1_xattn_ln_post_cross_w, L1_xattn_v_qkv, L1_xattn_l_qkv, L1_xattn_v_dense, L1_xattn_l_dense, L1_xattn_cq_w, L1_xattn_ckv_w, L1_xattn_cdense_w, L1_xattn_v_gate, L1_xattn_v_up, L1_xattn_v_down, L1_xattn_l_gate, L1_xattn_l_up, L1_xattn_l_down)
    return x

_drawn_inputs = setup_inputs


def setup_inputs(seed=0):
    import zlib

    import numpy as np

    out = dict(_drawn_inputs(seed))
    spreads = {'L0_xattn_norm_w': (1.0, 0.2),
     'L1_xattn_ln_in_w': (1.0, 0.6),
     'L1_xattn_ln_post_attn_w': (1.0, 0.6),
     'L1_xattn_ln_post_cross_w': (1.0, 0.6)}
    factors = {'L0_xattn_b_gate': 8.0,
     'L1_xattn_v_qkv': 8.0,
     'L1_xattn_v_dense': 3.241,
     'L1_xattn_cq_w': 33.48,
     'L1_xattn_v_gate': 2.722}
    for name, (base, spread) in spreads.items():
        noise = np.random.default_rng([zlib.crc32(name.encode()), seed]).standard_normal(out[name].shape)
        drawn = base * np.exp(spread * noise) if base else spread * noise
        out[name] = jnp.asarray(drawn.astype(out[name].dtype))
    for name, factor in factors.items():
        out[name] = (out[name] * factor).astype(out[name].dtype)
    return out
```

```python
from contextlib import ExitStack

import concourse.bass as bass
from concourse import mybir

F32 = mybir.dt.float32
F32R = mybir.dt.float32r
BF16 = mybir.dt.bfloat16
I32 = mybir.dt.int32
ALU = mybir.AluOpType
ACT = mybir.ActivationFunctionType
AX_X = mybir.AxisListType.X

P = 128
BATCHES, SEQ, DIM = 32, 112, 512
CTX, CDIM = 375, 256
NB = 4
GROUPS = BATCHES // NB
NT = NB * SEQ
KT = DIM // P
CT = CDIM // P
HEADS, HD = 16, 32
CHD = 16
QUADS = HEADS // 4
KC, NKC = 125, 3
CPAD = NB * CTX + 4
CEVEN = CTX + 1
INTER = 1376
FT = -(-INTER // P)
EXPERTS = 2
EPS = 1e-6
MASKED = -3.0e38

C_U = 0
C_MC = C_U + CT
C_GATE = C_MC + KT // 2
C_QK = C_GATE + KT
C_V = C_QK + 2 * KT * EXPERTS
C_DENSE = C_V + KT * EXPERTS
C_CK = C_DENSE + KT * EXPERTS
C_CV = C_CK + 1
C_CQ = C_CV + 1
C_CDENSE = C_CQ + CT
C_MLP = C_CDENSE + KT // 2
STEPS = EXPERTS * FT
CHUNKS = C_MLP + 3 * STEPS
RING = 7
assert CHUNKS % RING == 0
CV_BANKS = (4, 5, 2, 3, 4, 5)
PE_SET, ACT_SET, DVE_SET = CT + 1, KT + CT + 4, 18
DVE_STEPS = 120


def c_glu(step):
    return C_MLP + (3 * step - 1 if step else 0)


def c_down(step):
    return C_MLP + (3 * step + 4 if step < STEPS - 1 else 3 * STEPS - 1)


class Signal:

    def __init__(self, ctx, nc, name, per_group=0, first=0):
        self.sem = ctx.enter_context(nc.semaphore(name))
        self.name, self.per_group, self.first = name, per_group, first


class Engine:

    def __init__(self, eng, group):
        self.eng, self.group, self.last, self.count = eng, group, None, {}

    def wait(self, signal, events):
        self.eng.wait_ge(signal.sem, self.group * signal.per_group + (signal.first + events))

    def done(self, instruction, signal):
        instruction.then_inc(signal.sem, 1)
        self.count[signal] = self.count.get(signal, 0) + 1
        self.last = signal

    def fence(self):
        self.wait(self.last, self.count[self.last])

    def close(self):
        wrong = {s.name: n for s, n in self.count.items() if n != s.per_group}
        assert not wrong, wrong


def split_products(pe, out, w_hi, w_lo, x_hi, x_lo, start, stop):
    first = pe.matmul(out, w_hi, x_hi, start=start, stop=False)
    pe.matmul(out, w_hi, x_lo, start=False, stop=False)
    return first, pe.matmul(out, w_lo, x_hi, start=False, stop=stop)


def cross_heads(pair):
    h = 4 * (pair // 2) + pair % 2
    return h, h + 2


def build_xattn(nc, x_t, mem_t, mem_n, weights, w_gate_mem, w_mem, b_gate, norms, pos, mask,
                rope_tables, identity_in, causal_in, head_parity, out_t):
    with ExitStack() as ctx:
        def sb(name, shape, dt=F32):
            return ctx.enter_context(nc.sbuf_tensor(name, shape, dt))

        def signal(name, per_group=0, first=0):
            return Signal(ctx, nc, name, per_group, first)

        ps = ctx.enter_context(nc.psum_tensor("ps", [P, 8, 512], F32))

        w_raw = sb("w_raw", [P, RING, 512])
        w_hi, w_lo = sb("w_hi", [P, RING, 512], F32R), sb("w_lo", [P, RING, 512], F32R)
        v_hi, v_lo = sb("v_hi", [P, KT, NT], F32R), sb("v_lo", [P, KT, NT], F32R)
        l_hi, l_lo = sb("l_hi", [P, KT, NT], F32R), sb("l_lo", [P, KT, NT], F32R)
        m_hi, m_lo = sb("m_hi", [P, CT, CPAD], F32R), sb("m_lo", [P, CT, CPAD], F32R)
        wc_hi, wc_lo = sb("wc_hi", [P, CT, DIM], F32R), sb("wc_lo", [P, CT, DIM], F32R)
        h_hi, h_lo = sb("h_hi", [P, 2, NT], F32R), sb("h_lo", [P, 2, NT], F32R)
        x_in, res = sb("x_in", [P, KT, NT]), sb("res", [P, KT, NT])
        tt_in = sb("tt_in", [P, NB, SEQ], I32)
        is_pad, is_v, is_l = (sb(n, [P, NB, SEQ]) for n in ("is_pad", "is_v", "is_l"))
        rstd_v, rstd_l = sb("rstd_v", [P, NT]), sb("rstd_l", [P, NT])
        mean_sq, rstd_t = sb("mean_sq", [SEQ, NB]), sb("rstd_t", [SEQ, NB])
        minus_half = sb("minus_half", [SEQ, NB])
        ident = sb("ident", [P, P])
        ident_b = sb("ident_b", [P, P], BF16)
        causal = sb("causal", [SEQ, NB, SEQ], BF16)
        ones_col = sb("ones_col", [P, 1])
        cos_t, sin_t = sb("cos_t", [P, SEQ]), sb("sin_t", [P, SEQ])
        norm_w = sb("norm_w", [P, 4, KT])
        gate_b, half_b = sb("gate_b", [P, KT]), sb("half_b", [P, KT])
        parity = sb("parity", [P, 2])
        max0, sum0, rsum0 = (sb(n, [SEQ, NB]) for n in ("max0", "sum0", "rsum0"))
        max_s, rsum_s = sb("max_s", [SEQ, HEADS]), sb("rsum_s", [SEQ, HEADS])
        max_c, rsum_c = sb("max_c", [SEQ, 2, 2]), sb("rsum_c", [SEQ, HEADS])
        ARENA = 15936
        arena = sb("arena", [P, ARENA])

        def view(at, shape, parts=P):
            n = 1
            for s in shape:
                n *= s
            assert at + n <= ARENA
            flat = arena[0:parts, at:at + n]
            if len(shape) == 1:
                return flat
            names = "abcd"[:len(shape)]
            sizes = {c: s for c, s in zip(names[1:], shape[1:])}
            return flat.rearrange(f"p ({' '.join(names)}) -> p {' '.join(names)}", **sizes)

        memn = view(0, (NB * NKC, CDIM), KC)
        memt = view(3072, (CT, NB * CTX))
        p0 = view(6072, (NB, CTX), SEQ)
        pt0 = view(7572, (2, NKC * SEQ), KC)
        mc = view(8244, (KT, NT))
        gate_t = view(10036, (KT, NT))
        fused = view(11828, (KT, NT))
        q_t, k_t = view(0, (KT, NT)), view(1792, (KT, NT))
        rot, roc = view(3584, (2, NT)), view(4480, (2, NT))
        ctx_v, ctx_l = view(3584, (2, KT, SEQ)), view(4480, (2, KT, SEQ))
        v_n = view(5376, (NB, HEADS, HD + 1), SEQ)
        prob = view(7488, (2, HEADS, SEQ), SEQ)
        prob_t = view(11072, (2, HEADS, SEQ), SEQ)
        ctx_n = view(14656, (DIM,), SEQ)
        cq = view(0, (2, CT, NT))
        ck = view(1792, (CT, NB * CTX))
        cv = view(4792, (NB * NKC, HEADS, CHD + 1), KC)
        cp = view(8056, (2, 2, CTX), SEQ)
        cpt = view(9556, (2, 2, NKC * SEQ), KC)
        cctx = view(10900, (CDIM,), SEQ)
        cctx_t = view(11156, (2, CT, SEQ))
        act_t, act_a, act_h = view(11448, (2, NT)), view(12344, (2, NT)), view(13240, (2, NT))
        y_out = view(14136, (KT, NT))
        squares = [view(at, (KT, NT)) for at in (13620, 7488, 12162, 6072)]
        norm_v = [None, view(9280, (KT, NT)), view(13954, (KT, NT)), view(7864, (KT, NT))]
        norm_l = [None, view(11072, (KT, NT)), None, view(9656, (KT, NT))]
        wm_raw, wg_raw = view(0, (KT, CDIM)), view(1024, (KT, DIM))
        table_sb, onehot = view(3072, (2, P), SEQ), view(3328, (SEQ,), SEQ)
        pos_i, row_i = view(3440, (SEQ,), SEQ).bitcast(I32), view(3552, (SEQ,), SEQ).bitcast(I32)
        pos_f, pos_neg, row_f = (view(at, (SEQ,), SEQ) for at in (3664, 3776, 3888))
        causal_raw = view(4000, (NB, SEQ), SEQ)
        wm_hi, wm_lo = v_hi[:, :, 0:CDIM], v_lo[:, :, 0:CDIM]

        def gate_part(t, k):
            return t[:, k // 2, (k % 2) * DIM:(k % 2 + 1) * DIM]

        const_loaded, setup_loaded = signal("const_loaded"), signal("setup_loaded")
        x_loaded, mask_loaded = signal("x_loaded", 16), signal("mask_loaded", 16)
        memt_loaded, memn_loaded = signal("memt_loaded", 16), signal("memn_loaded", 16)
        w_loaded = [signal(f"w_loaded{i}", 16 * CHUNKS // RING) for i in range(RING)]
        w_hi_made, w_lo_made = signal("w_hi_made", CHUNKS), signal("w_lo_made", CHUNKS, first=1)
        product = signal("product", CHUNKS, first=RING)
        stored = signal("stored", 16, first=1)
        dve_set, pe_set, act_set, pool_set = (signal(n) for n in (
            "dve_set", "pe_set", "act_set", "pool_set"))
        s0_done, pt0_done, am_done = (signal(n, NB) for n in ("s0_done", "pt0_done", "am_done"))
        sumsq_done, rstd_done = signal("sumsq_done", 4), signal("rstd_done", 4)
        s_done, pt_done = signal("s_done", NB), signal("pt_done", NB * QUADS)
        ctx_done, ctxt_done = signal("ctx_done", NB), signal("ctxt_done", NB)
        ck_done, cv_done = signal("ck_done", 6), signal("cv_done", 6)
        PAIRS = NB * HEADS // 2
        cs_done, cpt_done = signal("cs_done", PAIRS), signal("cpt_done", PAIRS)
        co_done, cctxt_done = signal("co_done", NB), signal("cctxt_done", NB)
        x_hi_made, m_hi_made, u_hi_made = (signal("x_hi_made", 1), signal("m_hi_made", CT),
                                           signal("u_hi_made", CT))
        p0_made, am_hi_made, mc_made = (signal("p0_made", NB), signal("am_hi_made", NB),
                                        signal("mc_made", KT))
        tanh_gate, squared = signal("tanh_gate", KT), signal("squared", 4)
        norm_hi_made, ctx_hi_made = signal("norm_hi_made", 5), signal("ctx_hi_made", 2 * NB)
        v_made, exp_done, pt_made = (signal("v_made", NB), signal("exp_done", NB),
                                     signal("pt_made", NB * QUADS))
        ck_made, cq_made, cexp_done = (signal("ck_made", 6), signal("cq_made", 2 * CT),
                                       signal("cexp_done", 2 * PAIRS))
        cctx_hi_made = signal("cctx_hi_made", NB)
        tanh_mlp, h_hi_made = signal("tanh_mlp", STEPS), signal("h_hi_made", STEPS)
        step = signal("step", DVE_STEPS)
        masks_made, ones_set = signal("masks_made", 1, first=1), signal("ones_set", 1)
        x_lo_made, m_lo_made, u_lo_made = (signal("x_lo_made", 1), signal("m_lo_made", CT),
                                           signal("u_lo_made", CT))
        max0_made, p0_normed, pt0_made = (signal(n, NB) for n in (
            "max0_made", "p0_normed", "pt0_made"))
        am_lo_made, fused_made = signal("am_lo_made", NB), signal("fused_made", KT, first=1)
        sq_summed, mean_made = signal("sq_summed", 4), signal("mean_made", 4)
        res_made, normed = signal("res_made", 3 * KT), signal("normed", 5, first=1)
        norm_lo_made, ctx_lo_made = signal("norm_lo_made", 5), signal("ctx_lo_made", 2 * NB)
        rotated, roped = signal("rotated", 2 * KT), signal("roped", 2 * KT)
        s_shifted, ctx_normed, ctx_split = (signal("s_shifted", NB), signal("ctx_normed", NB),
                                            signal("ctx_split", 2 * NB))
        cones_set, cv_made = signal("cones_set", 1), signal("cv_made", 6)
        cmax_made, cpt_made = signal("cmax_made", PAIRS), signal("cpt_made", PAIRS)
        cctx_normed, cctx_made, cctx_lo_made = (signal(n, NB) for n in (
            "cctx_normed", "cctx_made", "cctx_lo_made"))
        glu_made, h_lo_made = signal("glu_made", STEPS), signal("h_lo_made", STEPS)
        y_made = signal("y_made", KT, first=1)
        powered = signal("powered", 4)

        loads = [(ident, identity_in), (norm_w, norms), (gate_b, b_gate), (parity, head_parity)]
        setups = [(wm_raw, w_mem), (wg_raw, w_gate_mem), (table_sb, rope_tables),
                  (causal_raw, causal_in),
                  (pos_i, pos.broadcast_to([SEQ, SEQ]))]
        block = ctx.enter_context(nc.Block())

        def batch(b):
            return slice(b * SEQ, (b + 1) * SEQ)

        turns = []
        for b in range(NB):
            turns += [("p", b, j) for j in range(QUADS)] + ([("c", b - 1, 0)] if b else [])
        turns.append(("c", NB - 1, 0))

        def turn_bank(kind, b, j):
            return 4 + turns.index((kind, b, j)) % 2

        @block.sync
        def _(sp):
            sp.sem_inc(stored.sem, stored.first)
            for dst, src in loads:
                sp.dma_start(dst[:], src).then_inc(const_loaded.sem, 16)
            for dst, src in setups:
                sp.dma_start(dst, src).then_inc(setup_loaded.sem, 16)
            sp.wait_ge(pe_set.sem, PE_SET)
            sp.wait_ge(act_set.sem, ACT_SET)
            sp.wait_ge(dve_set.sem, DVE_SET)
            with sp.Fori(0, GROUPS) as g:
                e = Engine(sp, g)
                e.wait(masks_made, 0)
                sp.dma_start(tt_in[:].rearrange("p b s -> p (b s)"),
                             mask[g].broadcast_to([P, NT])).then_inc(mask_loaded.sem, 16)
                e.wait(fused_made, 0)
                sp.dma_start(x_in[:], x_t[g]).then_inc(x_loaded.sem, 16)
                e.wait(normed, 0)
                sp.dma_start(memt, mem_t[g]).then_inc(memt_loaded.sem, 16)
                sp.dma_start(memn, mem_n[g]).then_inc(memn_loaded.sem, 16)
                for c in range(CHUNKS):
                    e.wait(w_lo_made, max(c - RING + 1, 0))
                    sp.dma_start(w_raw[:, c % RING, :], weights[c]).then_inc(w_loaded[c % RING].sem, 16)
                e.wait(y_made, KT)
                sp.dma_start(out_t[g], y_out).then_inc(stored.sem, 16)
            sp.wait_ge(stored.sem, stored.first + 16 * GROUPS)

        @block.gpsimd
        def _(pool):
            pool.sem_inc(w_lo_made.sem, w_lo_made.first)
            pool.memset(minus_half[:], -0.5).then_inc(pool_set.sem, 1)
            pool.iota(row_i, pattern=[[0, SEQ]], base=0, channel_multiplier=1).then_inc(pool_set.sem, 1)
            pool.wait_ge(pool_set.sem, 2)
            with pool.Fori(0, GROUPS) as g:
                e = Engine(pool, g)

                def low_parts(first, end):
                    for c in range(first, end):
                        slot = c % RING
                        e.wait(w_hi_made, c + 1)
                        e.done(pool.tensor_tensor(w_lo[:, slot, :], w_raw[:, slot, :],
                                                  w_hi[:, slot, :].bitcast(F32), ALU.subtract), w_lo_made)

                def power(n):
                    e.wait(mean_made, n + 1)
                    e.done(pool.tensor_tensor(rstd_t[:], mean_sq[:], minus_half[:], ALU.pow), powered)

                low_parts(0, C_QK)
                power(0)
                power(1)
                low_parts(C_QK, C_CK)
                low_parts(C_CK, C_CQ)
                power(2)
                low_parts(C_CQ, C_MLP)
                power(3)
                low_parts(C_MLP, CHUNKS)
                e.close()

        @block.scalar
        def _(act):
            act.wait_ge(setup_loaded.sem, 16 * len(setups))
            act.copy(wm_hi, wm_raw).then_inc(act_set.sem, 1)
            for k in range(KT):
                act.copy(gate_part(m_hi, k), wg_raw[:, k, :]).then_inc(act_set.sem, 1)
            for t in range(CT):
                act.wait_ge(pe_set.sem, t + 1)
                act.copy(wc_hi[:, t, :], ps[:, t, :]).then_inc(act_set.sem, 1)
            act.wait_ge(const_loaded.sem, 16 * len(loads))
            act.mul(half_b[:], gate_b[:], 0.5).then_inc(act_set.sem, 1)
            act.copy(ident_b[:], ident[:]).then_inc(act_set.sem, 1)
            act.copy(causal[:], causal_raw).then_inc(act_set.sem, 1)
            act.wait_ge(act_set.sem, ACT_SET)
            act.wait_ge(dve_set.sem, DVE_SET)
            with act.Fori(0, GROUPS) as g:
                e = Engine(act, g)
                made = [0]

                def high_parts(end):
                    for c in range(made[0], min(end, CHUNKS)):
                        slot = c % RING
                        act.wait_ge(w_loaded[slot].sem, g * w_loaded[slot].per_group + 16 * (c // RING + 1))
                        act.wait_ge(product.sem, g * CHUNKS + (c + 1))
                        e.done(act.copy(w_hi[:, slot, :], w_raw[:, slot, :]), w_hi_made)
                    made[0] = max(made[0], end)

                def product_of(chunk):
                    high_parts(chunk + RING)
                    e.wait(product, chunk + 1)

                high_parts(2)
                e.wait(x_loaded, 16)
                e.done(act.copy(v_hi[:], x_in[:]), x_hi_made)
                e.wait(memt_loaded, 16)
                for t in range(CT):
                    e.done(act.copy(m_hi[:, t, 0:NB * CTX], memt[:, t, :]), m_hi_made)
                for t in range(CT):
                    product_of(C_U + t)
                    e.done(act.activation(l_hi[:, t, :], ps[:, t, 0:NT], ACT.Copy,
                                          scale=float(DIM) ** -0.5), u_hi_made)
                for b in range(NB):
                    e.wait(max0_made, b + 1)
                    e.done(act.activation(p0[:, b, :], ps[0:SEQ, 2 + b, 0:CTX], ACT.Exp,
                                          bias=max0[:, b:b + 1], accum_out=sum0[:, b:b + 1]), p0_made)
                for b in range(NB):
                    e.wait(am_done, b + 1)
                    e.done(act.copy(l_hi[:, CT:2 * CT, batch(b)], ps[:, b % 2, 0:CT * SEQ].rearrange(
                        "p (t s) -> p t s", t=CT)), am_hi_made)
                for t in range(KT):
                    product_of(C_MC + t // 2)
                    e.done(act.copy(mc[:, t, :], ps[:, 2 + t, 0:NT]), mc_made)
                for t in range(KT):
                    product_of(C_GATE + t)
                    e.done(act.activation(gate_t[:, t, :], ps[:, (6 + t) % 8, 0:NT], ACT.Tanh,
                                          bias=half_b[:, t:t + 1], scale=0.5), tanh_gate)

                def square(n, source):
                    e.done(act.activation(squares[n], source, ACT.Square, scale=float(DIM) ** -0.5), squared)

                e.wait(fused_made, KT)
                e.wait(stored, 0)
                square(0, fused)
                e.wait(res_made, KT)
                e.wait(sq_summed, 1)
                square(1, res[:])
                e.wait(normed, 1)
                e.done(act.copy(v_hi[:], norm_v[1]), norm_hi_made)
                e.wait(normed, 2)
                e.done(act.copy(l_hi[:], norm_l[1]), norm_hi_made)
                for j in range(2 * KT):
                    product_of(C_QK + 2 * j + 1)
                product_of(C_V + KT * EXPERTS - 1)
                for b in range(NB):
                    if b == 0:
                        e.wait(ones_set, 1)
                    e.done(act.copy(v_n[:, b, :, 0:HD], ps[0:SEQ, 4 + b, 0:DIM].rearrange(
                        "p (h d) -> p h d", h=HEADS)), v_made)

                def exponents(b):
                    e.wait(s_shifted, b + 1)
                    e.done(act.activation(prob[:, b % 2], prob[:, b % 2], ACT.Exp,
                                          scale=float(HD) ** -0.5), exp_done)

                def context_high(b):
                    e.wait(ctx_split, 2 * b + 2)
                    e.done(act.copy(v_hi[:, :, batch(b)], ctx_v[:, b % 2]), ctx_hi_made)
                    e.done(act.copy(l_hi[:, :, batch(b)], ctx_l[:, b % 2]), ctx_hi_made)

                exponents(0)
                for b in range(NB):
                    if b >= 2:
                        e.wait(ctx_done, b - 1)
                    for j in range(QUADS):
                        e.wait(pt_done, b * QUADS + j + 1)
                        e.done(act.copy(prob_t[:, b % 2, 4 * j:4 * j + 4, :],
                                        ps[0:SEQ, turn_bank("p", b, j), 0:NT].rearrange(
                                            "p (h s) -> p h s", h=4)), pt_made)
                    if b + 1 < NB:
                        exponents(b + 1)
                    if b:
                        context_high(b - 1)
                context_high(NB - 1)
                for t in range(KT):
                    product_of(C_DENSE + 2 * t + 1)
                high_parts(C_CQ + 2)
                for n in range(6):
                    e.wait(ck_done, n + 1)
                    t, c = divmod(n, 3)
                    e.done(act.copy(ck[:, t, c * 500:(c + 1) * 500], ps[:, 2 + n % 4, 0:500]), ck_made)
                e.wait(res_made, 2 * KT)
                square(2, res[:])
                e.wait(normed, 3)
                e.done(act.copy(l_hi[:], norm_v[2]), norm_hi_made)
                for t in range(CT):
                    product_of(C_CQ + t)
                    for odd in range(2):
                        e.done(act.activation(cq[:, odd, t, :], ps[:, t, 0:NT], ACT.Copy,
                                              scale=parity[:, odd:odd + 1]), cq_made)
                high_parts(C_CDENSE + RING - 3)
                for u in range(PAIRS):
                    e.wait(cmax_made, u + 1)
                    if u >= 2:
                        e.wait(cpt_done, u - 1)
                    for i in range(2):
                        e.done(act.activation(cp[:, u % 2, i, :], ps[0:SEQ, 2 * (u % 2) + i, 0:CTX], ACT.Exp,
                                              bias=max_c[:, u % 2, i:i + 1], scale=float(CHD) ** -0.5), cexp_done)
                    b, p = divmod(u, HEADS // 2)
                    if b and p == 6:
                        e.wait(cctx_made, b)
                        e.done(act.copy(v_hi[:, 0:CT, batch(b - 1)], cctx_t[:, (b - 1) % 2]), cctx_hi_made)
                e.wait(cctx_made, NB)
                e.done(act.copy(v_hi[:, 0:CT, batch(NB - 1)], cctx_t[:, (NB - 1) % 2]), cctx_hi_made)
                for t in range(KT // 2):
                    product_of(C_CDENSE + t)
                e.wait(res_made, 3 * KT)
                square(3, res[:])
                e.wait(normed, 4)
                e.done(act.copy(v_hi[:], norm_v[3]), norm_hi_made)
                e.wait(normed, 5)
                e.done(act.copy(l_hi[:], norm_l[3]), norm_hi_made)
                for i in range(STEPS):
                    product_of(c_glu(i) + 1)
                    e.done(act.activation(act_t[:, i % 2, :], ps[:, 4 + 2 * (i % 2), 0:NT], ACT.Tanh,
                                          scale=0.5), tanh_mlp)
                    e.wait(glu_made, i + 1)
                    if i >= 2:
                        e.wait(product, c_down(i - 2) + 1)
                    e.done(act.copy(h_hi[:, i % 2, :], act_h[:, i % 2, :]), h_hi_made)
                product_of(c_down(STEPS - 1))
                e.close()

        @block.tensor
        def _(pe):
            pe.sem_inc(product.sem, product.first)
            pe.wait_ge(act_set.sem, KT + 1)
            pe.wait_ge(dve_set.sem, KT + 1)
            for t in range(CT):
                for k in range(KT):
                    w = slice(t * P, (t + 1) * P)
                    _, last = split_products(pe, ps[:, t, :], wm_hi[:, k, w], wm_lo[:, k, w],
                                             gate_part(m_hi, k), gate_part(m_lo, k), k == 0, k == KT - 1)
                last.then_inc(pe_set.sem, 1)
            pe.wait_ge(dve_set.sem, KT + 1 + 6)
            pe.matmul(ps[:, 2, 0:SEQ], table_sb[:, 0, :], onehot, start=True, stop=True)
            pe.matmul(ps[:, 3, 0:SEQ], table_sb[:, 1, :], onehot, start=True, stop=True).then_inc(pe_set.sem, 1)
            pe.wait_ge(pool_set.sem, 1)
            pe.wait_ge(act_set.sem, ACT_SET)
            pe.wait_ge(dve_set.sem, DVE_SET)
            with pe.Fori(0, GROUPS) as g:
                e = Engine(pe, g)

                def chunk(c):
                    e.wait(w_lo_made, c + 1)
                    slot = c % RING
                    return w_hi[:, slot, :], w_lo[:, slot, :]

                def project(out, c, at, stride, tiles, x_hi, x_lo, start=True, stop=True):
                    whi, wlo = chunk(c)
                    for k in range(tiles):
                        w = slice(at + k * stride, at + k * stride + P)
                        first, last = split_products(pe, out, whi[:, w], wlo[:, w], x_hi[:, k, :], x_lo[:, k, :],
                                                     start and k == 0, stop and k == tiles - 1)
                    return last

                e.wait(x_lo_made, 1)
                for t in range(CT):
                    e.done(project(ps[:, t, 0:NT], C_U + t, 0, P, KT, v_hi, v_lo), product)
                e.wait(m_lo_made, CT)
                e.wait(u_lo_made, CT)
                for b in range(NB):
                    out = ps[0:SEQ, 2 + b, 0:CEVEN]
                    for t in range(CT):
                        m = slice(b * CTX, b * CTX + CEVEN)
                        _, last = split_products(pe, out, l_hi[:, t, batch(b)], l_lo[:, t, batch(b)],
                                                 m_hi[:, t, m], m_lo[:, t, m], t == 0, t == CT - 1)
                    e.done(last, s0_done)
                for b in range(NB):
                    e.wait(p0_normed, b + 1)
                    if b >= 2:
                        e.wait(pt0_made, b - 1)
                    for c in range(NKC):
                        last = pe.transpose(ps[0:KC, 6 + b % 2, c * SEQ:(c + 1) * SEQ],
                                            p0[:, b, c * KC:(c + 1) * KC], ident[0:SEQ, 0:SEQ])
                    e.done(last, pt0_done)
                e.wait(memn_loaded, 16)
                for b in range(NB):
                    e.wait(pt0_made, b + 1)
                    if b >= 2:
                        e.wait(am_lo_made, b - 1)
                    for t in range(CT):
                        for c in range(NKC):
                            last = pe.matmul(ps[:, b % 2, t * SEQ:(t + 1) * SEQ],
                                             memn[:, b * NKC + c, t * P:(t + 1) * P],
                                             pt0[:, b % 2, c * SEQ:(c + 1) * SEQ],
                                             start=c == 0, stop=c == NKC - 1)
                    e.done(last, am_done)
                e.wait(am_lo_made, NB)
                for t in range(KT):
                    last = project(ps[:, 2 + t, 0:NT], C_MC + t // 2, (t % 2) * CT * P, P, CT,
                                   l_hi[:, CT:], l_lo[:, CT:])
                    if t % 2:
                        e.done(last, product)
                for t in range(KT):
                    out = ps[:, (6 + t) % 8, 0:NT]
                    for k in range(CT):
                        w = slice(t * P, (t + 1) * P)
                        split_products(pe, out, wc_hi[:, k, w], wc_lo[:, k, w], l_hi[:, CT + k, :],
                                       l_lo[:, CT + k, :], k == 0, False)
                    e.done(project(out, C_GATE + t, 0, P, KT, v_hi, v_lo, start=False), product)

                def norm(n):
                    e.wait(sq_summed, n + 1)
                    for b in range(NB):
                        last = pe.matmul(ps[0:SEQ, 6, b:b + 1], squares[n][:, 0, batch(b)], ones_col[:],
                                         start=True, stop=True)
                    e.done(last, sumsq_done)

                def norm_row(n):
                    e.wait(powered, n + 1)
                    for b in range(NB):
                        last = pe.matmul(ps[:, 7, batch(b)], rstd_t[:, b:b + 1].to_broadcast([SEQ, P]),
                                         ident[0:SEQ, 0:SEQ], start=True, stop=True)
                    e.done(last, rstd_done)

                e.wait(tanh_gate, KT)
                norm(0)
                norm_row(0)
                norm(1)
                e.wait(res_made, KT)
                norm_row(1)
                for j in range(2 * KT):
                    if j >= 4:
                        e.wait(roped, j - 3)
                    e.wait(norm_lo_made, 1)
                    e.done(project(ps[:, j % 4, 0:NT], C_QK + 2 * j, 0, P, KT, v_hi, v_lo, stop=False), product)
                    e.wait(norm_lo_made, 2)
                    e.done(project(ps[:, j % 4, 0:NT], C_QK + 2 * j + 1, 0, P, KT, l_hi, l_lo, start=False), product)
                for c in range(KT * EXPERTS):
                    whi, wlo = chunk(C_V + c)
                    k, expert = divmod(c, EXPERTS)
                    xh, xl = ((v_hi, v_lo), (l_hi, l_lo))[expert]
                    for b in range(NB):
                        out = ps[0:SEQ, 4 + b, :]
                        pe.matmul(out, xh[:, k, batch(b)], whi, start=c == 0, stop=False)
                        pe.matmul(out, xh[:, k, batch(b)], wlo, start=False, stop=False)
                        last = pe.matmul(out, xl[:, k, batch(b)], whi, start=False, stop=c == KT * EXPERTS - 1)
                    e.done(last, product)

                def scores(b):
                    for j in range(4):
                        pe.matmul(ps[0:SEQ, j, 0:NT], ident_b[0:SEQ, 0:SEQ],
                                  causal[:].rearrange("p m s -> p (m s)"), start=True, stop=False,
                                  skip_group_check=True)
                    for m in range(KT):
                        for j in range(4):
                            r = slice(32 * j, 32 * j + 32)
                            last = pe.matmul(ps[0:SEQ, j, m * SEQ:(m + 1) * SEQ], q_t[r, m, batch(b)],
                                             k_t[r, m, batch(b)], start=False, stop=m == KT - 1,
                                             skip_group_check=True)
                    e.done(last, s_done)

                def turn(kind, b, j):
                    n = turns.index((kind, b, j)) - 2
                    if n >= 0:
                        before, bb, jj = turns[n]
                        if before == "p":
                            e.wait(pt_made, bb * QUADS + jj + 1)
                        else:
                            e.wait(ctx_split, 2 * bb + 2)

                def context_transposes(b):
                    e.wait(ctx_normed, b + 1)
                    turn("c", b, 0)
                    for t in range(KT):
                        last = pe.transpose(ps[:, turn_bank("c", b, 0), batch(t)],
                                            ctx_n[:, t * P:(t + 1) * P], ident[0:SEQ, 0:SEQ])
                    e.done(last, ctxt_done)

                e.wait(roped, 2 * KT)
                scores(0)
                e.wait(v_made, NB)
                for b in range(NB):
                    if b + 1 < NB:
                        e.wait(s_shifted, b + 1)
                        scores(b + 1)
                    e.wait(exp_done, b + 1)
                    for j in range(QUADS):
                        turn("p", b, j)
                        for i in range(4):
                            last = pe.transpose(ps[0:SEQ, turn_bank("p", b, j), batch(i)],
                                                prob[:, b % 2, 4 * j + i, :], ident[0:SEQ, 0:SEQ])
                        e.done(last, pt_done)
                    if b:
                        context_transposes(b - 1)
                    for j in range(QUADS):
                        e.wait(pt_made, b * QUADS + j + 1)
                        for i in range(4):
                            h = 4 * i + j
                            last = pe.matmul(ps[0:SEQ, 6 + h // 8, (h % 8) * (HD + 1):(h % 8 + 1) * (HD + 1)],
                                             prob_t[:, b % 2, 4 * j + i, :], v_n[:, b, h, :],
                                             start=True, stop=True)
                    e.done(last, ctx_done)
                context_transposes(NB - 1)
                e.wait(ctx_lo_made, 2 * NB)
                for t in range(KT):
                    e.done(project(ps[:, t, 0:NT], C_DENSE + 2 * t, 0, P, KT, v_hi, v_lo, stop=False), product)
                    e.done(project(ps[:, t, 0:NT], C_DENSE + 2 * t + 1, 0, P, KT, l_hi, l_lo, start=False), product)

                whi, wlo = chunk(C_CK)
                for n in range(6):
                    t, c = divmod(n, 3)
                    if n < 2:
                        e.wait(res_made, KT + n + 3)
                    if n >= 4:
                        e.wait(ck_made, n - 3)
                    for k in range(CT):
                        w = slice((t * CT + k) * P, (t * CT + k + 1) * P)
                        m = slice(c * 500, (c + 1) * 500)
                        _, last = split_products(pe, ps[:, 2 + n % 4, 0:500], whi[:, w], wlo[:, w],
                                                 m_hi[:, k, m], m_lo[:, k, m], k == 0, k == CT - 1)
                    e.done(last, ck_done)
                norm(2)
                vhi, vlo = chunk(C_CV)
                for n in range(6):
                    if n < 4:
                        e.wait(ck_made, n + 3)
                    else:
                        e.wait(cv_made, n - 3)
                    for i in range(2):
                        m = slice((2 * n + i) * KC, (2 * n + i + 1) * KC)
                        out = ps[0:KC, CV_BANKS[n], i * CDIM:(i + 1) * CDIM]
                        for k in range(CT):
                            w = slice(k * CDIM, (k + 1) * CDIM)
                            first = pe.matmul(out, m_hi[:, k, m], vhi[:, w], start=k == 0, stop=False)
                            if n == 0 and i == 0 and k == 0:
                                e.done(first, product)
                            pe.matmul(out, m_hi[:, k, m], vlo[:, w], start=False, stop=False)
                            last = pe.matmul(out, m_lo[:, k, m], vhi[:, w], start=False, stop=k == CT - 1)
                    e.done(last, cv_done)
                norm_row(2)
                e.wait(norm_lo_made, 3)
                for t in range(CT):
                    whi, wlo = chunk(C_CQ + t)
                    for k in range(KT):
                        w = slice(k * P, (k + 1) * P)
                        first, last = split_products(pe, ps[:, t, 0:NT], whi[:, w], wlo[:, w], l_hi[:, k, :],
                                                     l_lo[:, k, :], k == 0, k == KT - 1)
                        if t == 0 and k == 0:
                            e.done(first, product)
                    e.done(last, product)
                e.wait(cq_made, 2 * CT)
                e.wait(cv_made, 6)

                def pair_scores(u):
                    b, p = divmod(u, HEADS // 2)
                    if u >= 2:
                        e.wait(cexp_done, 2 * (u - 1))
                    for i, h in enumerate(cross_heads(p)):
                        r = slice(32 * (h % 8 // 2), 32 * (h % 8 // 2) + 32)
                        last = pe.matmul(ps[0:SEQ, 2 * (u % 2) + i, 0:CTX], cq[r, h % 2, h // 8, batch(b)],
                                         ck[r, h // 8, b * CTX:(b + 1) * CTX], start=True, stop=True)
                    e.done(last, cs_done)

                def pair_transposes(u):
                    e.wait(cexp_done, 2 * (u + 1))
                    if u:
                        e.wait(cpt_made, u)
                    for i in range(2):
                        for c in range(NKC):
                            last = pe.transpose(ps[0:KC, 4 + i, c * SEQ:(c + 1) * SEQ],
                                                cp[:, u % 2, i, c * KC:(c + 1) * KC], ident[0:SEQ, 0:SEQ])
                    e.done(last, cpt_done)

                def pair_context(u):
                    b, p = divmod(u, HEADS // 2)
                    e.wait(cpt_made, u + 1)
                    if b >= 2 and p == 0:
                        e.wait(cctx_made, b - 1)
                    for i, h in enumerate(cross_heads(p)):
                        for c in range(NKC):
                            last = pe.matmul(ps[0:SEQ, 6 + b % 2, h * (CHD + 1):(h + 1) * (CHD + 1)],
                                             cpt[:, u % 2, i, c * SEQ:(c + 1) * SEQ],
                                             cv[:, b * NKC + c, h, :], start=c == 0, stop=c == NKC - 1)
                    return last

                def cross_transposes(b):
                    e.wait(cctx_normed, b + 1)
                    for t in range(CT):
                        last = pe.transpose(ps[:, 6 + b % 2, 288 + t * SEQ:288 + (t + 1) * SEQ],
                                            cctx[:, t * P:(t + 1) * P], ident[0:SEQ, 0:SEQ])
                    e.done(last, cctxt_done)

                for s in range(PAIRS + 2):
                    if s < PAIRS:
                        pair_scores(s)
                    if s >= 2:
                        last = pair_context(s - 2)
                        if (s - 1) % (HEADS // 2) == 0:
                            e.done(last, co_done)
                    if 1 <= s <= PAIRS:
                        pair_transposes(s - 1)
                    if s > 9 and (s - 4) % (HEADS // 2) == 0:
                        cross_transposes((s - 4) // (HEADS // 2) - 1)
                cross_transposes(NB - 1)
                e.wait(cctx_lo_made, NB)
                for t in range(KT):
                    last = project(ps[:, t, 0:NT], C_CDENSE + t // 2, (t % 2) * CT * P, P, CT,
                                   v_hi, v_lo)
                    if t % 2:
                        e.done(last, product)
                norm(3)
                norm_row(3)

                def glu(i):
                    xh, xl = ((v_hi, v_lo), (l_hi, l_lo))[i // FT]
                    if i >= 2:
                        e.wait(glu_made, i - 1)
                    for up in range(2):
                        e.done(project(ps[:, 4 + 2 * (i % 2) + up, 0:NT], c_glu(i) + up, 0, P, KT, xh, xl), product)

                def down(i):
                    whi, wlo = chunk(c_down(i))
                    e.wait(h_lo_made, i + 1)
                    for t in range(KT):
                        w = slice(t * P, (t + 1) * P)
                        _, last = split_products(pe, ps[:, t, 0:NT], whi[:, w], wlo[:, w], h_hi[:, i % 2, :],
                                                 h_lo[:, i % 2, :], i == 0, i == STEPS - 1)
                    e.done(last, product)

                e.wait(norm_lo_made, 4)
                glu(0)
                for i in range(1, STEPS):
                    if i == FT:
                        e.wait(norm_lo_made, 5)
                    glu(i)
                    down(i - 1)
                down(STEPS - 1)
                e.wait(y_made, KT)
                e.close()

        @block.vector
        def _(dve):
            for begun in (masks_made, fused_made, normed, y_made):
                dve.sem_inc(begun.sem, begun.first)
            made = [0]

            def setup(instruction, wait=True):
                instruction.then_inc(dve_set.sem, 1)
                made[0] += 1
                if wait:
                    dve.wait_ge(dve_set.sem, made[0])

            dve.wait_ge(act_set.sem, KT + 1)
            setup(dve.tensor_tensor(wm_lo, wm_raw, wm_hi.bitcast(F32), ALU.subtract))
            for k in range(KT):
                setup(dve.tensor_tensor(gate_part(m_lo, k), wg_raw[:, k, :],
                                        gate_part(m_hi, k).bitcast(F32), ALU.subtract))
            dve.wait_ge(pool_set.sem, 2)
            setup(dve.tensor_copy(row_f, row_i))
            setup(dve.tensor_copy(pos_f, pos_i))
            setup(dve.tensor_scalar(pos_neg, pos_f, 0.0, float(SEQ), ALU.is_lt, ALU.mult))
            setup(dve.tensor_tensor(pos_f, pos_f, pos_neg, ALU.add))
            setup(dve.tensor_scalar(pos_f, pos_f, 0.0, float(SEQ - 1), ALU.max, ALU.min))
            setup(dve.tensor_tensor(onehot, pos_f, row_f, ALU.is_equal))
            setup(dve.memset(ones_col[:], 1.0))
            dve.wait_ge(pe_set.sem, CT + 1)
            setup(dve.tensor_copy(cos_t[:], ps[:, 2, 0:SEQ]))
            setup(dve.tensor_copy(sin_t[:], ps[:, 3, 0:SEQ]))
            dve.wait_ge(act_set.sem, KT + CT + 1)
            for t in range(CT):
                setup(dve.tensor_tensor(wc_lo[:, t, :], ps[:, t, :], wc_hi[:, t, :].bitcast(F32), ALU.subtract))
            setup(dve.memset(m_hi[:, :, NB * CTX:CPAD].bitcast(F32), 0.0))
            setup(dve.memset(m_lo[:, :, NB * CTX:CPAD].bitcast(F32), 0.0))
            assert made[0] == DVE_SET
            dve.wait_ge(const_loaded.sem, 16 * len(loads))
            with dve.Fori(0, GROUPS) as g:
                e = Engine(dve, g)

                def low(out, source, high, signal):
                    e.done(dve.tensor_tensor(out, source, high.bitcast(F32), ALU.subtract), signal)

                e.wait(mask_loaded, 16)
                e.wait(product, 0)
                e.wait(y_made, 0)
                e.done(dve.tensor_scalar(is_pad[:], tt_in[:], 1, None, ALU.is_equal), masks_made)
                e.fence()
                e.done(dve.memset(is_v[:, :, SEQ - 1:SEQ], 0.0), step)
                e.done(dve.tensor_tensor(is_v[:, :, 0:SEQ - 1], is_pad[:, :, 0:SEQ - 1],
                                         is_pad[:, :, 1:SEQ], ALU.mult), step)
                e.fence()
                e.done(dve.tensor_scalar(is_l[:], is_v[:], -1.0, 1.0, ALU.mult, ALU.add), step)
                e.wait(x_hi_made, 1)
                low(v_lo[:], x_in[:], v_hi[:], x_lo_made)
                for t in range(CT):
                    e.wait(m_hi_made, t + 1)
                    low(m_lo[:, t, 0:NB * CTX], memt[:, t, :], m_hi[:, t, 0:NB * CTX], m_lo_made)
                for t in range(CT):
                    e.wait(u_hi_made, t + 1)
                    e.done(dve.scalar_tensor_tensor(l_lo[:, t, :], ps[:, t, 0:NT], float(DIM) ** -0.5,
                                                    l_hi[:, t, :].bitcast(F32), ALU.mult, ALU.subtract), u_lo_made)
                for b in range(NB):
                    e.wait(s0_done, b + 1)
                    e.done(dve.tensor_reduce(max0[:, b:b + 1], ps[0:SEQ, 2 + b, 0:CTX], AX_X, ALU.max), step)
                    e.fence()
                    e.done(dve.tensor_scalar(max0[:, b:b + 1], max0[:, b:b + 1], -1.0, None, ALU.mult), max0_made)
                for b in range(NB):
                    e.wait(p0_made, b + 1)
                    e.done(dve.reciprocal(rsum0[:, b:b + 1], sum0[:, b:b + 1]), step)
                    e.fence()
                    e.done(dve.tensor_scalar(p0[:, b, :], p0[:, b, :], rsum0[:, b:b + 1], None, ALU.mult), p0_normed)
                for b in range(NB):
                    e.wait(pt0_done, b + 1)
                    if b >= 2:
                        e.wait(am_done, b - 1)
                    e.done(dve.tensor_copy(pt0[:, b % 2, :], ps[0:KC, 6 + b % 2, 0:NKC * SEQ]), pt0_made)
                    if b:
                        e.wait(am_hi_made, b)
                        low(l_lo[:, CT:2 * CT, batch(b - 1)], ps[:, (b - 1) % 2, 0:CT * SEQ].rearrange(
                            "p (t s) -> p t s", t=CT), l_hi[:, CT:2 * CT, batch(b - 1)], am_lo_made)
                e.wait(am_hi_made, NB)
                low(l_lo[:, CT:2 * CT, batch(NB - 1)], ps[:, (NB - 1) % 2, 0:CT * SEQ].rearrange(
                    "p (t s) -> p t s", t=CT), l_hi[:, CT:2 * CT, batch(NB - 1)], am_lo_made)
                for t in range(KT):
                    e.wait(mc_made, t + 1)
                    e.wait(tanh_gate, t + 1)
                    e.done(dve.scalar_tensor_tensor(gate_t[:, t, :], gate_t[:, t, :], 1.0, mc[:, t, :],
                                                    ALU.add, ALU.mult), step)
                    e.fence()
                    e.done(dve.scalar_tensor_tensor(fused[:, t, :], gate_t[:, t, :], 0.5, x_in[:, t, :],
                                                    ALU.mult, ALU.add), fused_made)

                def norm_sum(n):
                    sq = squares[n]
                    e.wait(squared, n + 1)
                    e.done(dve.tensor_tensor(sq[:, 0:2, :], sq[:, 0:2, :], sq[:, 2:4, :], ALU.add), step)
                    e.fence()
                    e.done(dve.tensor_tensor(sq[:, 0, :], sq[:, 0, :], sq[:, 1, :], ALU.add), sq_summed)
                    e.wait(sumsq_done, n + 1)
                    if n:
                        e.wait(powered, n)
                    e.done(dve.tensor_scalar(mean_sq[:], ps[0:SEQ, 6, 0:NB], EPS, None, ALU.add), mean_made)

                def norm_scale(out, source, n, t, row, signal):
                    e.done(dve.scalar_tensor_tensor(out[:, t, :], source[:, t, :], norm_w[:, n, t:t + 1], row,
                                                    ALU.mult, ALU.mult), signal)

                def norm_experts(n, first):
                    e.wait(rstd_done, n + 1)
                    for mask_of, row in ((is_v, rstd_v), (is_l, rstd_l)):
                        e.done(dve.tensor_tensor(row[:], ps[:, 7, 0:NT], mask_of[:].rearrange("p b s -> p (b s)"),
                                                 ALU.mult), step)
                    e.fence()
                    for out, row in ((norm_v[n], rstd_v[:]), (norm_l[n], rstd_l[:])):
                        for t in range(KT):
                            norm_scale(out, res, n, t, row, normed if t == KT - 1 else step)
                    e.wait(norm_hi_made, first)
                    low(v_lo[:], norm_v[n], v_hi[:], norm_lo_made)
                    e.wait(norm_hi_made, first + 1)
                    low(l_lo[:], norm_l[n], l_hi[:], norm_lo_made)

                norm_sum(0)
                e.wait(rstd_done, 1)
                for t in range(KT):
                    norm_scale(res, fused, 0, t, ps[:, 7, 0:NT], res_made)
                norm_sum(1)
                norm_experts(1, 1)
                for j in range(2 * KT):
                    out = (q_t, k_t)[j // KT][:, j % KT, :]
                    now, s = ps[:, j % 4, 0:NT], j % 2
                    e.wait(product, C_QK + 2 * j + 2)
                    if j >= 2:
                        e.fence()
                    e.done(dve.tensor_tensor(roc[:, s, :].rearrange("p (b s) -> p b s", b=NB),
                                             now.rearrange("p (b s) -> p b s", b=NB),
                                             cos_t[:].unsqueeze(1).to_broadcast([P, NB, SEQ]), ALU.mult), step)
                    e.done(dve.stream_shuffle(rot[:, s, :], now, [(i + HD // 2) % HD for i in range(HD)]), rotated)
                    e.fence()
                    e.done(dve.tensor_tensor(rot[:, s, :].rearrange("p (b s) -> p b s", b=NB),
                                             rot[:, s, :].rearrange("p (b s) -> p b s", b=NB),
                                             sin_t[:].unsqueeze(1).to_broadcast([P, NB, SEQ]), ALU.mult), step)
                    e.fence()
                    e.done(dve.tensor_tensor(out, rot[:, s, :], roc[:, s, :], ALU.add), roped)
                def context_split(b):
                    e.wait(ctxt_done, b + 1)
                    now = ps[:, turn_bank("c", b, 0), 0:NT].rearrange("p (t s) -> p t s", t=KT)
                    for out, mask_of in ((ctx_v, is_v), (ctx_l, is_l)):
                        e.done(dve.tensor_tensor(out[:, b % 2], now,
                                                 mask_of[:, b, :].unsqueeze(1).to_broadcast([P, KT, SEQ]),
                                                 ALU.mult), ctx_split)

                def context_low(b):
                    e.wait(ctx_hi_made, 2 * b + 2)
                    low(v_lo[:, :, batch(b)], ctx_v[:, b % 2], v_hi[:, :, batch(b)], ctx_lo_made)
                    low(l_lo[:, :, batch(b)], ctx_l[:, b % 2], l_hi[:, :, batch(b)], ctx_lo_made)

                e.done(dve.memset(v_n[:, :, :, HD:HD + 1], 1.0), ones_set)
                for b in range(NB + 1):
                    if b < NB:
                        e.wait(s_done, b + 1)
                        now = ps[0:SEQ, 0:4, 0:NT].rearrange("p j (m s) -> p j m s", m=KT)
                        if b:
                            e.fence()
                        e.done(dve.tensor_reduce(max_s[:].rearrange("p (j m) -> p j m", j=4), now, AX_X, ALU.max), step)
                        e.fence()
                        if b >= 2:
                            e.wait(pt_done, (b - 1) * QUADS)
                        e.done(dve.tensor_tensor(
                            prob[:, b % 2].rearrange("p (j m) s -> p j m s", j=4), now,
                            max_s[:].rearrange("p (j m) -> p j m", j=4).unsqueeze(3).to_broadcast([SEQ, 4, KT, SEQ]),
                            ALU.subtract), s_shifted)
                    if b >= 2:
                        context_split(b - 2)
                    if b:
                        e.wait(ctx_done, b)
                        now = ps[0:SEQ, 6:8, 0:8 * (HD + 1)].rearrange("p j (h d) -> p j h d", h=8)
                        e.done(dve.reciprocal(rsum_s[:].rearrange("p (j h) -> p j h", j=2).unsqueeze(3),
                                              now[:, :, :, HD:HD + 1]), step)
                        e.fence()
                        if b >= 2:
                            e.wait(ctxt_done, b - 1)
                        e.done(dve.tensor_tensor(
                            ctx_n.rearrange("p (j h d) -> p j h d", j=2, h=8), now[:, :, :, 0:HD],
                            rsum_s[:].rearrange("p (j h) -> p j h", j=2).unsqueeze(3).to_broadcast([SEQ, 2, 8, HD]),
                            ALU.mult), ctx_normed)
                    if b >= 2:
                        context_low(b - 2)
                context_split(NB - 1)
                context_low(NB - 1)
                for t in range(KT):
                    e.wait(product, C_DENSE + 2 * t + 2)
                    e.done(dve.tensor_tensor(res[:, t, :], ps[:, t, 0:NT], res[:, t, :], ALU.add), res_made)
                norm_sum(2)
                e.done(dve.memset(cv[:, :, :, CHD:CHD + 1], 1.0), cones_set)
                for n in range(6):
                    e.wait(cv_done, n + 1)
                    e.done(dve.tensor_copy(cv[:, 2 * n:2 * n + 2, :, 0:CHD], ps[0:KC, CV_BANKS[n], :].rearrange(
                        "p (i h d) -> p i h d", i=2, h=HEADS)), cv_made)
                e.wait(rstd_done, 3)
                for t in range(KT):
                    norm_scale(norm_v[2], res, 2, t, ps[:, 7, 0:NT], normed if t == KT - 1 else step)
                e.wait(norm_hi_made, 3)
                low(l_lo[:], norm_v[2], l_hi[:], norm_lo_made)
                def cross_normalise(b):
                    e.wait(co_done, b + 1)
                    now = ps[0:SEQ, 6 + b % 2, 0:HEADS * (CHD + 1)].rearrange("p (h d) -> p h d", h=HEADS)
                    e.done(dve.reciprocal(rsum_c[:].unsqueeze(2), now[:, :, CHD:CHD + 1]), step)
                    e.fence()
                    if b:
                        e.wait(cctxt_done, b)
                    e.done(dve.tensor_tensor(cctx.rearrange("p (h d) -> p h d", h=HEADS), now[:, :, 0:CHD],
                                             rsum_c[:].unsqueeze(2).to_broadcast([SEQ, HEADS, CHD]),
                                             ALU.mult), cctx_normed)

                def cross_copy(b):
                    e.wait(cctxt_done, b + 1)
                    e.done(dve.tensor_copy(cctx_t[:, b % 2], ps[:, 6 + b % 2, 288:288 + CT * SEQ].rearrange(
                        "p (t s) -> p t s", t=CT)), cctx_made)

                def cross_low(b):
                    e.wait(cctx_hi_made, b + 1)
                    low(v_lo[:, 0:CT, batch(b)], cctx_t[:, b % 2], v_hi[:, 0:CT, batch(b)], cctx_lo_made)

                for u in range(PAIRS + 1):
                    if u < PAIRS:
                        e.wait(cs_done, u + 1)
                        if u >= 2:
                            e.wait(cexp_done, 2 * (u - 1))
                        e.done(dve.tensor_reduce(max_c[:, u % 2, :], ps[0:SEQ, 2 * (u % 2):2 * (u % 2) + 2, 0:CTX],
                                                 AX_X, ALU.max), step)
                        e.fence()
                        e.done(dve.tensor_scalar(max_c[:, u % 2, :], max_c[:, u % 2, :], -float(CHD) ** -0.5, None,
                                                 ALU.mult), cmax_made)
                    if u:
                        e.wait(cpt_done, u)
                        e.done(dve.tensor_copy(cpt[:, (u - 1) % 2], ps[0:KC, 4:6, 0:NKC * SEQ]), cpt_made)
                    for late, stage in ((9, cross_normalise), (13, cross_copy), (15, cross_low)):
                        if late <= u < PAIRS and (u - late) % (HEADS // 2) == 0:
                            stage((u - late) // (HEADS // 2))
                cross_normalise(NB - 1)
                cross_copy(NB - 1)
                cross_low(NB - 1)
                for t in range(KT):
                    e.wait(product, C_CDENSE + t // 2 + 1)
                    e.done(dve.tensor_tensor(res[:, t, :], ps[:, t, 0:NT], res[:, t, :], ALU.add), res_made)
                norm_sum(3)
                norm_experts(3, 4)
                for i in range(STEPS):
                    s = i % 2
                    e.wait(tanh_mlp, i + 1)
                    if i >= 2:
                        e.wait(h_lo_made, i - 1)
                    e.done(dve.scalar_tensor_tensor(act_a[:, s, :], act_t[:, s, :], 1.0, ps[:, 4 + 2 * s, 0:NT],
                                                    ALU.add, ALU.mult), step)
                    e.fence()
                    e.done(dve.scalar_tensor_tensor(act_h[:, s, :], act_a[:, s, :], 0.5, ps[:, 5 + 2 * s, 0:NT],
                                                    ALU.mult, ALU.mult), glu_made)
                    e.wait(h_hi_made, i + 1)
                    low(h_lo[:, s, :], act_h[:, s, :], h_hi[:, s, :], h_lo_made)
                e.wait(stored, 0)
                e.wait(product, CHUNKS)
                for t in range(KT):
                    e.done(dve.tensor_tensor(y_out[:, t, :], ps[:, t, 0:NT], res[:, t, :], ALU.add), y_made)
                e.close()


def kernel(**inputs):
    import numpy as np
    import concourse.bacc as bacc
    from concourse.bass_utils import run_bass_kernel_spmd

    a = {name: np.asarray(x) for name, x in inputs.items()}

    def w(name, layer=1):
        return a[f"L{layer}_xattn_{name}"]

    def by_tile(m, n=None):
        m = m if n is None else m[:, n * P:(n + 1) * P]
        return m.reshape(-1, P, m.shape[1]).transpose(1, 0, 2)

    def flat(*blocks):
        return np.concatenate([x.reshape(P, -1) for x in blocks], axis=1)

    def padded(m, axis):
        wide = [(0, 0), (0, 0)]
        wide[axis] = (0, FT * P - INTER)
        return np.pad(m, wide)

    w_mem, w_gate = w("W_mem", 0), w("W_gate", 0).T
    qkv, dense = (w("v_qkv"), w("l_qkv")), (w("v_dense"), w("l_dense"))
    gates = [padded(w(f"{n}_gate"), 1) for n in "vl"]
    ups = [padded(w(f"{n}_up"), 1) for n in "vl"]
    downs = [padded(w(f"{n}_down"), 0) for n in "vl"]
    chunks = [flat(by_tile(w_mem, t)) for t in range(CT)]
    chunks += [flat(by_tile(w_mem.T, 2 * c), by_tile(w_mem.T, 2 * c + 1)) for c in range(KT // 2)]
    chunks += [flat(by_tile(w_gate[:DIM], t)) for t in range(KT)]
    chunks += [flat(by_tile(qkv[x], j)) for j in range(2 * KT) for x in range(EXPERTS)]
    chunks += [qkv[x][k * P:(k + 1) * P, 2 * DIM:] for k in range(KT) for x in range(EXPERTS)]
    chunks += [flat(by_tile(dense[x], t)) for t in range(KT) for x in range(EXPERTS)]
    ckv = w("ckv_w")
    chunks += [flat(by_tile(ckv, 0), by_tile(ckv, 1)), flat(by_tile(ckv[:, CDIM:]))]
    chunks += [flat(by_tile(w("cq_w"), t)) for t in range(CT)]
    cd = w("cdense_w")
    chunks += [flat(by_tile(cd, 2 * c), by_tile(cd, 2 * c + 1)) for c in range(KT // 2)]
    mlp = [None] * (3 * STEPS)
    for i in range(STEPS):
        x, f = divmod(i, FT)
        mlp[c_glu(i) - C_MLP] = flat(by_tile(gates[x], f))
        mlp[c_glu(i) + 1 - C_MLP] = flat(by_tile(ups[x], f))
        mlp[c_down(i) - C_MLP] = downs[x][f * P:(f + 1) * P]
    weights = np.stack(chunks + mlp)
    assert weights.shape == (CHUNKS, P, 512)

    angle = np.outer(np.arange(SEQ, dtype=np.float32),
                     np.float32(1) / np.float32(10000) ** (np.arange(0, HD, 2, dtype=np.float32) / np.float32(HD)))
    cos, sin = np.cos(angle), np.sin(angle)
    tables = np.stack([np.tile(np.concatenate([cos, cos], 1), (1, P // HD)),
                       np.tile(np.concatenate([-sin, sin], 1), (1, P // HD))], 1).astype(np.float32)
    after = np.triu(np.full((SEQ, SEQ), MASKED, np.float32), 1)
    causal = np.repeat(after[:, None, :], NB, 1)
    odd = (np.arange(P) // CHD % 2).astype(np.float32)

    x, mem = a["x"], a["ctx_1024"]
    arrays = {
        "x_t": x.reshape(GROUPS, NT, KT, P).transpose(0, 3, 2, 1),
        "mem_t": mem.reshape(GROUPS, NB * CTX, CT, P).transpose(0, 3, 2, 1),
        "mem_n": mem.reshape(GROUPS, NB * NKC, KC, CDIM).transpose(0, 2, 1, 3),
        "weights": weights,
        "w_gate_mem": by_tile(w_gate[DIM:]),
        "w_mem": by_tile(w_mem),
        "b_gate": w("b_gate", 0).reshape(KT, P).T,
        "norms": np.stack([n.reshape(KT, P).T for n in (
            w("norm_w", 0), w("ln_in_w"), w("ln_post_cross_w"), w("ln_post_attn_w"))], 1),
        "pos": a["pos_1xS"],
        "mask": a["mask_BxS_ik0"].reshape(GROUPS, 1, NT),
        "rope_tables": tables,
        "identity_in": np.eye(P, dtype=np.float32),
        "causal_in": causal,
        "head_parity": np.stack([1 - odd, odd], 1),
    }
    arrays = {name: np.ascontiguousarray(x) for name, x in arrays.items()}
    nc = bacc.Bacc("TRN2", target_bir_lowering=False, num_devices=1)
    args = {name: nc.dram_tensor(name, x.shape, mybir.dt.from_np(x.dtype), kind="ExternalInput").ap()
            for name, x in arrays.items()}
    out = nc.dram_tensor("out_t", (GROUPS, P, KT, NT), F32, kind="ExternalOutput").ap()
    build_xattn(nc, **args, out_t=out)
    got = run_bass_kernel_spmd(nc, [arrays], core_ids=[0]).results[0]["out_t"]
    return got.transpose(0, 3, 2, 1).reshape(BATCHES, SEQ, DIM)
```

```python
from contextlib import ExitStack

import concourse.bass as bass
from concourse import mybir

F32 = mybir.dt.float32
F32R = mybir.dt.float32r
BF16 = mybir.dt.bfloat16
I32 = mybir.dt.int32
ALU = mybir.AluOpType
ACT = mybir.ActivationFunctionType
AX_X = mybir.AxisListType.X

P = 128
BATCHES, SEQ, DIM = 32, 112, 512
CTX, CDIM = 375, 256
NB = 4
GROUPS = BATCHES // NB
NT = NB * SEQ
KT = DIM // P
CT = CDIM // P
HEADS, HD = 16, 32
CHD = 16
QUADS = HEADS // 4
KC, NKC = 125, 3
CPAD = NB * CTX + 4
CEVEN = CTX + 1
INTER = 1376
FT = -(-INTER // P)
EXPERTS = 2
EPS = 1e-6
MASKED = -3.0e38

C_U = 0
C_MC = C_U + CT
C_GATE = C_MC + KT // 2
C_QK = C_GATE + KT
C_V = C_QK + 2 * KT * EXPERTS
C_CK = C_V + KT * EXPERTS
C_DENSE = C_CK + 1
C_CV = C_DENSE + KT * EXPERTS
C_CQ = C_CV + 1
C_CDENSE = C_CQ + CT
C_MLP = C_CDENSE + KT // 2
STEPS = EXPERTS * FT
CHUNKS = C_MLP + 3 * STEPS
RING = 7
assert CHUNKS % RING == 0
CV_BANKS = (4, 5, 2, 3, 4, 5)
PE_SET, ACT_SET, DVE_SET = CT + 1, KT + CT + 4, 18
DVE_STEPS = 199


def c_glu(step):
    return C_MLP + (3 * step - 1 if step else 0)


def c_down(step):
    return C_MLP + (3 * step + 4 if step < STEPS - 1 else 3 * STEPS - 1)


class Signal:

    def __init__(self, ctx, nc, name, per_group=0, first=0):
        self.sem = ctx.enter_context(nc.semaphore(name))
        self.name, self.per_group, self.first = name, per_group, first


class Engine:

    def __init__(self, eng, group):
        self.eng, self.group, self.last, self.count = eng, group, None, {}

    def wait(self, signal, events):
        self.eng.wait_ge(signal.sem, self.group * signal.per_group + (signal.first + events))

    def done(self, instruction, signal):
        instruction.then_inc(signal.sem, 1)
        self.count[signal] = self.count.get(signal, 0) + 1
        self.last = signal

    def fence(self):
        self.wait(self.last, self.count[self.last])

    def close(self):
        wrong = {s.name: n for s, n in self.count.items() if n != s.per_group}
        assert not wrong, wrong


def split_products(pe, out, w_hi, w_lo, x_hi, x_lo, start, stop):
    first = pe.matmul(out, w_hi, x_hi, start=start, stop=False)
    pe.matmul(out, w_hi, x_lo, start=False, stop=False)
    return first, pe.matmul(out, w_lo, x_hi, start=False, stop=stop)


def cross_unit(u):
    return u // (2 * NB), u // 2 % NB, u % 2


def cross_bank(u):
    return 2 - 2 * (u % 2)


def build_xattn(nc, x_t, mem_t, mem_n, weights, w_gate_mem, w_mem, b_gate, norms, pos, mask,
                rope_tables, identity_in, causal_in, head_masks, out_t):
    with ExitStack() as ctx:
        def sb(name, shape, dt=F32):
            return ctx.enter_context(nc.sbuf_tensor(name, shape, dt))

        def signal(name, per_group=0, first=0):
            return Signal(ctx, nc, name, per_group, first)

        ps = ctx.enter_context(nc.psum_tensor("ps", [P, 8, 512], F32))

        w_raw = sb("w_raw", [P, RING, 512])
        w_hi, w_lo = sb("w_hi", [P, RING, 512], F32R), sb("w_lo", [P, RING, 512], F32R)
        v_hi, v_lo = sb("v_hi", [P, KT, NT], F32R), sb("v_lo", [P, KT, NT], F32R)
        l_hi, l_lo = sb("l_hi", [P, KT, NT], F32R), sb("l_lo", [P, KT, NT], F32R)
        m_hi, m_lo = sb("m_hi", [P, CT, CPAD], F32R), sb("m_lo", [P, CT, CPAD], F32R)
        wc_hi, wc_lo = sb("wc_hi", [P, CT, DIM], F32R), sb("wc_lo", [P, CT, DIM], F32R)
        h_hi, h_lo = sb("h_hi", [P, 2, NT], F32R), sb("h_lo", [P, 2, NT], F32R)
        x_in, res = sb("x_in", [P, KT, NT]), sb("res", [P, KT, NT])
        tt_in = sb("tt_in", [P, NB, SEQ], I32)
        is_pad, is_v, is_l = (sb(n, [P, NB, SEQ]) for n in ("is_pad", "is_v", "is_l"))
        rstd_v, rstd_l = sb("rstd_v", [P, NT]), sb("rstd_l", [P, NT])
        mean_sq, rstd_t = sb("mean_sq", [SEQ, NB]), sb("rstd_t", [SEQ, NB])
        minus_half = sb("minus_half", [SEQ, NB])
        ident = sb("ident", [P, P])
        ident_b = sb("ident_b", [P, P], BF16)
        causal = sb("causal", [SEQ, NB, SEQ], BF16)
        ones_col = sb("ones_col", [P, 1])
        cos_t, sin_t = sb("cos_t", [P, SEQ]), sb("sin_t", [P, SEQ])
        norm_w = sb("norm_w", [P, 4, KT])
        gate_b, half_b = sb("gate_b", [P, KT]), sb("half_b", [P, KT])
        head_mask = sb("head_mask", [P, P // CHD + P // HD])
        cmask, smask = head_mask[:, 0:P // CHD], head_mask[:, P // CHD:]
        max0, sum0, rsum0 = (sb(n, [SEQ, NB]) for n in ("max0", "sum0", "rsum0"))
        max_s, rsum_s = sb("max_s", [SEQ, HEADS]), sb("rsum_s", [SEQ, 2, HEADS])
        max_c, sum_c, rsum_c = (sb(n, [SEQ, 3, 2]) for n in ("max_c", "sum_c", "rsum_c"))
        ARENA = 16384
        arena = sb("arena", [P, ARENA])

        def view(at, shape, parts=P):
            n = 1
            for s in shape:
                n *= s
            assert at + n <= ARENA
            flat = arena[0:parts, at:at + n]
            if len(shape) == 1:
                return flat
            names = "abcd"[:len(shape)]
            sizes = {c: s for c, s in zip(names[1:], shape[1:])}
            return flat.rearrange(f"p ({' '.join(names)}) -> p {' '.join(names)}", **sizes)

        memn = view(0, (NB * NKC, CDIM), KC)
        memt = view(3072, (CT, NB * CTX))
        p0 = view(6072, (NB, CTX), SEQ)
        pt0 = view(7572, (2, NKC * SEQ), KC)
        mc = view(8244, (KT, NT))
        gate_t = view(10036, (KT, NT))
        fused = view(11828, (KT, NT))
        q_t, k_t = view(0, (KT, NT)), view(1792, (KT, NT))
        rot, roc = view(12800, (2, NT)), view(13696, (2, NT))
        kb = view(3584, (2, KT, 4, SEQ))
        v_n = view(7168, (NB, DIM), SEQ)
        prob = view(9216, (2, HEADS, SEQ), SEQ)
        prob_t = view(12800, (HEADS, SEQ), SEQ)
        ctx_v, ctx_l = view(14592, (2, KT, SEQ)), view(15488, (2, KT, SEQ))
        ck = view(0, (CT, NB * CTX))
        cv = view(3000, (NB * NKC, HEADS // 2, 4 * CHD), KC)
        cp = view(9144, (3, 2, CTX), SEQ)
        cpt = view(11394, (2, 2, NKC * SEQ), KC)
        act_t, act_a, act_h = view(11448, (2, NT)), view(12344, (2, NT)), view(13240, (2, NT))
        y_out = view(14136, (KT, NT))
        squares = [view(at, (KT, NT)) for at in (13620, 7488, 12162, 6072)]
        norm_v = [None, view(9280, (KT, NT)), view(13954, (KT, NT)), view(7864, (KT, NT))]
        norm_l = [None, view(11072, (KT, NT)), None, view(9656, (KT, NT))]
        wm_raw, wg_raw = view(0, (KT, CDIM)), view(1024, (KT, DIM))
        table_sb, onehot = view(3072, (2, P), SEQ), view(3328, (SEQ,), SEQ)
        pos_i, row_i = view(3440, (SEQ,), SEQ).bitcast(I32), view(3552, (SEQ,), SEQ).bitcast(I32)
        pos_f, pos_neg, row_f = (view(at, (SEQ,), SEQ) for at in (3664, 3776, 3888))
        causal_raw = view(4000, (NB, SEQ), SEQ)
        wm_hi, wm_lo = v_hi[:, :, 0:CDIM], v_lo[:, :, 0:CDIM]

        def gate_part(t, k):
            return t[:, k // 2, (k % 2) * DIM:(k % 2 + 1) * DIM]

        const_loaded, setup_loaded = signal("const_loaded"), signal("setup_loaded")
        x_loaded, mask_loaded = signal("x_loaded", 16), signal("mask_loaded", 16)
        memt_loaded, memn_loaded = signal("memt_loaded", 16), signal("memn_loaded", 16)
        w_loaded = [signal(f"w_loaded{i}", 16 * CHUNKS // RING) for i in range(RING)]
        w_hi_made, w_lo_made = signal("w_hi_made", CHUNKS), signal("w_lo_made", CHUNKS, first=1)
        product = signal("product", CHUNKS, first=RING)
        stored = signal("stored", 16, first=1)
        dve_set, pe_set, act_set, pool_set = (signal(n) for n in (
            "dve_set", "pe_set", "act_set", "pool_set"))
        s0_done, pt0_done, am_done = (signal(n, NB) for n in ("s0_done", "pt0_done", "am_done"))
        sumsq_done, rstd_done = signal("sumsq_done", 4), signal("rstd_done", 4)
        s_done, pt_done = signal("s_done", NB), signal("pt_done", NB * QUADS)
        ctx_done = signal("ctx_done", NB)
        ck_done, cv_done = signal("ck_done", 5), signal("cv_done", 6)
        PAIRS = NB * HEADS // 2
        cs_done, cpt_done = signal("cs_done", PAIRS), signal("cpt_done", PAIRS)
        co_done = signal("co_done", CT)
        x_hi_made, m_hi_made, u_hi_made = (signal("x_hi_made", 1), signal("m_hi_made", CT),
                                           signal("u_hi_made", CT))
        p0_made, am_hi_made, mc_made = (signal("p0_made", NB), signal("am_hi_made", NB),
                                        signal("mc_made", KT))
        tanh_gate, squared = signal("tanh_gate", KT), signal("squared", 4)
        norm_hi_made, ctx_hi_made = signal("norm_hi_made", 5), signal("ctx_hi_made", 2 * NB)
        v_made, exp_done, pt_made = (signal("v_made", NB), signal("exp_done", NB),
                                     signal("pt_made", NB * QUADS))
        ck_made, ck_hi_made, cq_hi_made = (signal("ck_made", 6), signal("ck_hi_made", CT),
                                           signal("cq_hi_made", CT))
        cexp_done, cpt_made = signal("cexp_done", 2 * PAIRS), signal("cpt_made", PAIRS)
        cctx_hi_made = signal("cctx_hi_made", CT)
        tanh_mlp, h_hi_made = signal("tanh_mlp", STEPS), signal("h_hi_made", STEPS)
        step = signal("step", DVE_STEPS)
        masks_made = signal("masks_made", 1, first=1)
        x_lo_made, m_lo_made, u_lo_made = (signal("x_lo_made", 1), signal("m_lo_made", CT),
                                           signal("u_lo_made", CT))
        max0_made, p0_normed, pt0_made = (signal(n, NB) for n in (
            "max0_made", "p0_normed", "pt0_made"))
        am_lo_made, fused_made = signal("am_lo_made", NB), signal("fused_made", KT, first=1)
        sq_summed, mean_made = signal("sq_summed", 4), signal("mean_made", 4)
        res_made, normed = signal("res_made", 3 * KT), signal("normed", 5, first=1)
        norm_lo_made, ctx_lo_last = signal("norm_lo_made", 5), signal("ctx_lo_last", 2)
        rotated, roped = signal("rotated", 2 * KT), signal("roped", 2 * KT)
        kb_made, s_shifted, rsum_made, ctx_split = (signal("kb_made", NB), signal("s_shifted", NB),
                                                    signal("rsum_made", NB), signal("ctx_split", 2 * NB))
        cv_made, ck_lo_made, cq_lo_made = (signal("cv_made", 12), signal("ck_lo_made", CT),
                                           signal("cq_lo_made", CT))
        quad0_made, cmax_made, cp_normed = (signal("quad0_made", 1), signal("cmax_made", PAIRS),
                                            signal("cp_normed", PAIRS))
        cctx_lo_made = signal("cctx_lo_made", CT)
        glu_made, h_lo_made = signal("glu_made", STEPS), signal("h_lo_made", STEPS)
        y_made = signal("y_made", KT, first=1)
        powered, czero_set, quad_made = (signal("powered", 4), signal("czero_set", 1),
                                         signal("quad_made", QUADS - 1))
        p_normed, ctx_lo_made = signal("p_normed", 2 * NB), signal("ctx_lo_made", 2 * (NB - 1))

        loads = [(ident, identity_in), (norm_w, norms), (gate_b, b_gate), (head_mask, head_masks)]
        setups = [(wm_raw, w_mem), (wg_raw, w_gate_mem), (table_sb, rope_tables),
                  (causal_raw, causal_in),
                  (pos_i, pos.broadcast_to([SEQ, SEQ]))]
        block = ctx.enter_context(nc.Block())

        def batch(b):
            return slice(b * SEQ, (b + 1) * SEQ)

        @block.sync
        def _(sp):
            sp.sem_inc(stored.sem, stored.first)
            for dst, src in loads:
                sp.dma_start(dst[:], src).then_inc(const_loaded.sem, 16)
            for dst, src in setups:
                sp.dma_start(dst, src).then_inc(setup_loaded.sem, 16)
            sp.wait_ge(pe_set.sem, PE_SET)
            sp.wait_ge(act_set.sem, ACT_SET)
            sp.wait_ge(dve_set.sem, DVE_SET)
            with sp.Fori(0, GROUPS) as g:
                e = Engine(sp, g)
                e.wait(masks_made, 0)
                sp.dma_start(tt_in[:].rearrange("p b s -> p (b s)"),
                             mask[g].broadcast_to([P, NT])).then_inc(mask_loaded.sem, 16)
                e.wait(fused_made, 0)
                sp.dma_start(x_in[:], x_t[g]).then_inc(x_loaded.sem, 16)
                e.wait(normed, 0)
                sp.dma_start(memt, mem_t[g]).then_inc(memt_loaded.sem, 16)
                sp.dma_start(memn, mem_n[g]).then_inc(memn_loaded.sem, 16)
                for c in range(CHUNKS):
                    e.wait(w_lo_made, max(c - RING + 1, 0))
                    sp.dma_start(w_raw[:, c % RING, :], weights[c]).then_inc(w_loaded[c % RING].sem, 16)
                e.wait(y_made, KT)
                sp.dma_start(out_t[g], y_out).then_inc(stored.sem, 16)
            sp.wait_ge(stored.sem, stored.first + 16 * GROUPS)

        @block.gpsimd
        def _(pool):
            pool.sem_inc(w_lo_made.sem, w_lo_made.first)
            pool.memset(minus_half[:], -0.5).then_inc(pool_set.sem, 1)
            pool.iota(row_i, pattern=[[0, SEQ]], base=0, channel_multiplier=1).then_inc(pool_set.sem, 1)
            pool.wait_ge(pool_set.sem, 2)
            with pool.Fori(0, GROUPS) as g:
                e = Engine(pool, g)

                def low_parts(first, end):
                    for c in range(first, end):
                        slot = c % RING
                        e.wait(w_hi_made, c + 1)
                        e.done(pool.tensor_tensor(w_lo[:, slot, :], w_raw[:, slot, :],
                                                  w_hi[:, slot, :].bitcast(F32), ALU.subtract), w_lo_made)

                def power(n):
                    e.wait(mean_made, n + 1)
                    e.done(pool.tensor_tensor(rstd_t[:], mean_sq[:], minus_half[:], ALU.pow), powered)

                low_parts(0, C_QK)
                power(0)
                power(1)
                def normalise(b):
                    e.wait(rsum_made, b + 1)
                    for half in range(2):
                        now = prob[:, b % 2, 8 * half:8 * half + 8, :]
                        e.done(pool.tensor_tensor(now, now, rsum_s[:, b % 2, 8 * half:8 * half + 8].unsqueeze(
                            2).to_broadcast([SEQ, 8, SEQ]), ALU.mult), p_normed)

                low_parts(C_QK, C_CK)
                normalise(0)
                low_parts(C_CK, C_CK + 3)
                normalise(1)
                low_parts(C_CK + 3, C_CK + RING)
                for s in range(2, NB + 1):
                    if s < NB:
                        normalise(s)
                    b = s - 2
                    e.wait(ctx_hi_made, 2 * b + 2)
                    for lo, hi, now in ((v_lo, v_hi, ctx_v), (l_lo, l_hi, ctx_l)):
                        e.done(pool.tensor_tensor(lo[:, :, batch(b)], now[:, b % 2], hi[:, :, batch(b)].bitcast(F32),
                                                  ALU.subtract), ctx_lo_made)
                low_parts(C_CK + RING, C_CV)
                e.done(pool.memset(cv[:, :, :, CHD:3 * CHD], 0.0), czero_set)
                low_parts(C_CV, C_CQ)
                power(2)
                low_parts(C_CQ, C_CDENSE)
                e.wait(cq_lo_made, CT)
                for q in range(1, QUADS):
                    if q >= 2:
                        e.wait(cs_done, 2 * NB * (q - 1))
                    for out, part in zip(((v_hi, v_lo), (l_hi, l_lo))[q % 2], (h_hi, h_lo)):
                        last = pool.tensor_tensor(
                            out[:], part[:, q // 2, :].bitcast(F32).unsqueeze(1).to_broadcast([P, 4, NT]),
                            cmask[:, 4 * (q % 2):4 * (q % 2) + 4].unsqueeze(2).to_broadcast([P, 4, NT]), ALU.mult)
                        if part is h_lo:
                            e.done(last, quad_made)
                low_parts(C_CDENSE, C_MLP)
                power(3)
                low_parts(C_MLP, CHUNKS)
                e.close()

        @block.scalar
        def _(act):
            act.wait_ge(setup_loaded.sem, 16 * len(setups))
            act.copy(wm_hi, wm_raw).then_inc(act_set.sem, 1)
            for k in range(KT):
                act.copy(gate_part(m_hi, k), wg_raw[:, k, :]).then_inc(act_set.sem, 1)
            for t in range(CT):
                act.wait_ge(pe_set.sem, t + 1)
                act.copy(wc_hi[:, t, :], ps[:, t, :]).then_inc(act_set.sem, 1)
            act.wait_ge(const_loaded.sem, 16 * len(loads))
            act.mul(half_b[:], gate_b[:], 0.5).then_inc(act_set.sem, 1)
            act.copy(ident_b[:], ident[:]).then_inc(act_set.sem, 1)
            act.copy(causal[:], causal_raw).then_inc(act_set.sem, 1)
            act.wait_ge(act_set.sem, ACT_SET)
            act.wait_ge(dve_set.sem, DVE_SET)
            with act.Fori(0, GROUPS) as g:
                e = Engine(act, g)
                made = [0]

                def high_parts(end):
                    for c in range(made[0], min(end, CHUNKS)):
                        slot = c % RING
                        act.wait_ge(w_loaded[slot].sem, g * w_loaded[slot].per_group + 16 * (c // RING + 1))
                        act.wait_ge(product.sem, g * CHUNKS + (c + 1))
                        e.done(act.copy(w_hi[:, slot, :], w_raw[:, slot, :]), w_hi_made)
                    made[0] = max(made[0], end)

                def product_of(chunk):
                    high_parts(chunk + RING)
                    e.wait(product, chunk + 1)

                high_parts(2)
                e.wait(x_loaded, 16)
                e.done(act.copy(v_hi[:], x_in[:]), x_hi_made)
                e.wait(memt_loaded, 16)
                for t in range(CT):
                    e.done(act.copy(m_hi[:, t, 0:NB * CTX], memt[:, t, :]), m_hi_made)
                for t in range(CT):
                    product_of(C_U + t)
                    e.done(act.activation(l_hi[:, t, :], ps[:, t, 0:NT], ACT.Copy,
                                          scale=float(DIM) ** -0.5), u_hi_made)
                for b in range(NB):
                    e.wait(max0_made, b + 1)
                    e.done(act.activation(p0[:, b, :], ps[0:SEQ, 2 + b, 0:CTX], ACT.Exp,
                                          bias=max0[:, b:b + 1], accum_out=sum0[:, b:b + 1]), p0_made)
                for b in range(NB):
                    e.wait(am_done, b + 1)
                    e.done(act.copy(l_hi[:, CT:2 * CT, batch(b)], ps[:, b % 2, 0:CT * SEQ].rearrange(
                        "p (t s) -> p t s", t=CT)), am_hi_made)
                for t in range(KT):
                    product_of(C_MC + t // 2)
                    e.done(act.copy(mc[:, t, :], ps[:, 2 + t, 0:NT]), mc_made)
                for t in range(KT):
                    product_of(C_GATE + t)
                    e.done(act.activation(gate_t[:, t, :], ps[:, (6 + t) % 8, 0:NT], ACT.Tanh,
                                          bias=half_b[:, t:t + 1], scale=0.5), tanh_gate)

                def square(n, source):
                    e.done(act.activation(squares[n], source, ACT.Square, scale=float(DIM) ** -0.5), squared)

                e.wait(fused_made, KT)
                e.wait(stored, 0)
                square(0, fused)
                e.wait(res_made, KT)
                e.wait(sq_summed, 1)
                square(1, res[:])
                e.wait(normed, 1)
                e.done(act.copy(v_hi[:], norm_v[1]), norm_hi_made)
                e.wait(normed, 2)
                e.done(act.copy(l_hi[:], norm_l[1]), norm_hi_made)
                for j in range(2 * KT):
                    product_of(C_QK + 2 * j + 1)
                def exponents(b):
                    e.wait(s_shifted, b + 1)
                    e.done(act.activation(prob[:, b % 2], prob[:, b % 2], ACT.Exp,
                                          scale=float(HD) ** -0.5), exp_done)

                def key_tiles(first, end):
                    for n in range(first, end):
                        if n < 5:
                            e.wait(ck_done, n + 1)
                        else:
                            e.wait(product, C_CK + 1)
                        t, c = divmod(n, 3)
                        e.done(act.copy(ck[:, t, c * 500:(c + 1) * 500], ps[:, n % 4, 0:500]), ck_made)

                product_of(C_V + 1)
                exponents(0)
                product_of(C_V + 4)
                exponents(1)
                product_of(C_CK - 1)
                for b in range(NB):
                    e.done(act.copy(v_n[:, b, :], ps[0:SEQ, 4 + b, 0:DIM]), v_made)
                high_parts(C_CK + RING)
                for s in range(2, NB + 2):
                    b = s - 2
                    for j in range(QUADS):
                        e.wait(pt_done, b * QUADS + j + 1)
                        e.done(act.copy(prob_t[:, 4 * j:4 * j + 4, :], ps[0:SEQ, 4 + j % 2, 0:NT].rearrange(
                            "p (h s) -> p h s", h=4)), pt_made)
                    if s < NB:
                        exponents(s)
                    if s == NB - 1:
                        key_tiles(0, 2)
                    if s == NB:
                        key_tiles(2, 6)
                    e.wait(ctx_split, 2 * b + 2)
                    e.done(act.copy(v_hi[:, :, batch(b)], ctx_v[:, b % 2]), ctx_hi_made)
                    e.done(act.copy(l_hi[:, :, batch(b)], ctx_l[:, b % 2]), ctx_hi_made)
                for t in range(KT):
                    product_of(C_DENSE + 2 * t + 1)
                high_parts(C_CQ + 2)
                e.wait(res_made, 2 * KT)
                square(2, res[:])
                e.wait(normed, 3)
                e.done(act.copy(l_hi[:], norm_v[2]), norm_hi_made)
                e.wait(cv_done, 6)
                for t in range(CT):
                    e.done(act.copy(m_hi[:, t, 0:NB * CTX], ck[:, t, :]), ck_hi_made)
                for t in range(CT):
                    product_of(C_CQ + t)
                    e.done(act.copy(h_hi[:, t, :], ps[:, t, 0:NT]), cq_hi_made)
                high_parts(C_CDENSE + RING - 2)

                def cross_high(t):
                    e.wait(co_done, t + 1)
                    e.done(act.copy(v_hi[:, t, :], ps[:, 6 + t, 0:NT]), cctx_hi_made)

                for s in range(PAIRS + 2):
                    if s >= 2:
                        u = s - 2
                        e.wait(cpt_done, u + 1)
                        e.done(act.copy(cpt[:, u % 2], ps[0:KC, 4:6, 0:NKC * SEQ]), cpt_made)
                    if s < PAIRS:
                        e.wait(cmax_made, s + 1)
                        if s >= 3:
                            e.wait(cpt_done, s - 2)
                        for i in range(2):
                            e.done(act.activation(cp[:, s % 3, i, :], ps[0:SEQ, cross_bank(s) + i, 0:CTX], ACT.Exp,
                                                  bias=max_c[:, s % 3, i:i + 1], scale=float(CHD) ** -0.5,
                                                  accum_out=sum_c[:, s % 3, i:i + 1]), cexp_done)
                    if s == 6 * NB + 3:
                        cross_high(0)
                cross_high(1)
                for t in range(KT // 2):
                    product_of(C_CDENSE + t)
                e.wait(res_made, 3 * KT)
                square(3, res[:])
                e.wait(normed, 4)
                e.done(act.copy(v_hi[:], norm_v[3]), norm_hi_made)
                e.wait(normed, 5)
                e.done(act.copy(l_hi[:], norm_l[3]), norm_hi_made)
                for i in range(STEPS):
                    product_of(c_glu(i) + 1)
                    e.done(act.activation(act_t[:, i % 2, :], ps[:, 4 + 2 * (i % 2), 0:NT], ACT.Tanh,
                                          scale=0.5), tanh_mlp)
                    e.wait(glu_made, i + 1)
                    if i >= 2:
                        e.wait(product, c_down(i - 2) + 1)
                    e.done(act.copy(h_hi[:, i % 2, :], act_h[:, i % 2, :]), h_hi_made)
                product_of(c_down(STEPS - 1))
                e.close()

        @block.tensor
        def _(pe):
            pe.sem_inc(product.sem, product.first)
            pe.wait_ge(act_set.sem, KT + 1)
            pe.wait_ge(dve_set.sem, KT + 1)
            for t in range(CT):
                for k in range(KT):
                    w = slice(t * P, (t + 1) * P)
                    _, last = split_products(pe, ps[:, t, :], wm_hi[:, k, w], wm_lo[:, k, w],
                                             gate_part(m_hi, k), gate_part(m_lo, k), k == 0, k == KT - 1)
                last.then_inc(pe_set.sem, 1)
            pe.wait_ge(dve_set.sem, KT + 1 + 6)
            pe.matmul(ps[:, 2, 0:SEQ], table_sb[:, 0, :], onehot, start=True, stop=True)
            pe.matmul(ps[:, 3, 0:SEQ], table_sb[:, 1, :], onehot, start=True, stop=True).then_inc(pe_set.sem, 1)
            pe.wait_ge(pool_set.sem, 1)
            pe.wait_ge(act_set.sem, ACT_SET)
            pe.wait_ge(dve_set.sem, DVE_SET)
            with pe.Fori(0, GROUPS) as g:
                e = Engine(pe, g)

                def chunk(c):
                    e.wait(w_lo_made, c + 1)
                    slot = c % RING
                    return w_hi[:, slot, :], w_lo[:, slot, :]

                def project(out, c, at, stride, tiles, x_hi, x_lo, start=True, stop=True):
                    whi, wlo = chunk(c)
                    for k in range(tiles):
                        w = slice(at + k * stride, at + k * stride + P)
                        first, last = split_products(pe, out, whi[:, w], wlo[:, w], x_hi[:, k, :], x_lo[:, k, :],
                                                     start and k == 0, stop and k == tiles - 1)
                    return last

                e.wait(x_lo_made, 1)
                for t in range(CT):
                    e.done(project(ps[:, t, 0:NT], C_U + t, 0, P, KT, v_hi, v_lo), product)
                e.wait(m_lo_made, CT)
                e.wait(u_lo_made, CT)
                for b in range(NB):
                    out = ps[0:SEQ, 2 + b, 0:CEVEN]
                    for t in range(CT):
                        m = slice(b * CTX, b * CTX + CEVEN)
                        _, last = split_products(pe, out, l_hi[:, t, batch(b)], l_lo[:, t, batch(b)],
                                                 m_hi[:, t, m], m_lo[:, t, m], t == 0, t == CT - 1)
                    e.done(last, s0_done)
                for b in range(NB):
                    e.wait(p0_normed, b + 1)
                    if b >= 2:
                        e.wait(pt0_made, b - 1)
                    for c in range(NKC):
                        last = pe.transpose(ps[0:KC, 6 + b % 2, c * SEQ:(c + 1) * SEQ],
                                            p0[:, b, c * KC:(c + 1) * KC], ident[0:SEQ, 0:SEQ])
                    e.done(last, pt0_done)
                e.wait(memn_loaded, 16)
                for b in range(NB):
                    e.wait(pt0_made, b + 1)
                    if b >= 2:
                        e.wait(am_lo_made, b - 1)
                    for t in range(CT):
                        for c in range(NKC):
                            last = pe.matmul(ps[:, b % 2, t * SEQ:(t + 1) * SEQ],
                                             memn[:, b * NKC + c, t * P:(t + 1) * P],
                                             pt0[:, b % 2, c * SEQ:(c + 1) * SEQ],
                                             start=c == 0, stop=c == NKC - 1)
                    e.done(last, am_done)
                e.wait(am_lo_made, NB)
                for t in range(KT):
                    last = project(ps[:, 2 + t, 0:NT], C_MC + t // 2, (t % 2) * CT * P, P, CT,
                                   l_hi[:, CT:], l_lo[:, CT:])
                    if t % 2:
                        e.done(last, product)
                for t in range(KT):
                    out = ps[:, (6 + t) % 8, 0:NT]
                    for k in range(CT):
                        w = slice(t * P, (t + 1) * P)
                        split_products(pe, out, wc_hi[:, k, w], wc_lo[:, k, w], l_hi[:, CT + k, :],
                                       l_lo[:, CT + k, :], k == 0, False)
                    e.done(project(out, C_GATE + t, 0, P, KT, v_hi, v_lo, start=False), product)

                def norm(n):
                    e.wait(sq_summed, n + 1)
                    for b in range(NB):
                        last = pe.matmul(ps[0:SEQ, 6, b:b + 1], squares[n][:, 0, batch(b)], ones_col[:],
                                         start=True, stop=True)
                    e.done(last, sumsq_done)

                def norm_row(n):
                    e.wait(powered, n + 1)
                    for b in range(NB):
                        last = pe.matmul(ps[:, 7, batch(b)], rstd_t[:, b:b + 1].to_broadcast([SEQ, P]),
                                         ident[0:SEQ, 0:SEQ], start=True, stop=True)
                    e.done(last, rstd_done)

                e.wait(tanh_gate, KT)
                norm(0)
                norm_row(0)
                norm(1)
                e.wait(res_made, KT)
                norm_row(1)
                for j in range(2 * KT):
                    if j >= 4:
                        e.wait(roped, j - 3)
                    e.wait(norm_lo_made, 1)
                    e.done(project(ps[:, j % 4, 0:NT], C_QK + 2 * j, 0, P, KT, v_hi, v_lo, stop=False), product)
                    e.wait(norm_lo_made, 2)
                    e.done(project(ps[:, j % 4, 0:NT], C_QK + 2 * j + 1, 0, P, KT, l_hi, l_lo, start=False), product)
                def scores(b):
                    if b:
                        e.wait(s_shifted, b)
                    for m in range(KT):
                        pe.matmul(ps[0:SEQ, m, 0:NT], ident_b[0:SEQ, 0:SEQ],
                                  causal[:].rearrange("p m s -> p (m s)"), start=True, stop=False)
                    e.wait(kb_made, b + 1)
                    for m in range(KT):
                        last = pe.matmul(ps[0:SEQ, m, 0:NT], q_t[:, m, batch(b)],
                                         kb[:, b % 2, m].rearrange("p j s -> p (j s)"), start=False, stop=True)
                    e.done(last, s_done)

                for c in range(KT * EXPERTS):
                    whi, wlo = chunk(C_V + c)
                    k, expert = divmod(c, EXPERTS)
                    xh, xl = ((v_hi, v_lo), (l_hi, l_lo))[expert]
                    for b in range(NB):
                        out = ps[0:SEQ, 4 + b, :]
                        pe.matmul(out, xh[:, k, batch(b)], whi, start=c == 0, stop=False)
                        pe.matmul(out, xh[:, k, batch(b)], wlo, start=False, stop=False)
                        last = pe.matmul(out, xl[:, k, batch(b)], whi, start=False, stop=c == KT * EXPERTS - 1)
                    e.done(last, product)
                    if c == 1:
                        e.wait(roped, 2 * KT)
                        scores(0)
                    if c == 4:
                        scores(1)

                def transposes(b, j):
                    if j % 2 == 0:
                        e.wait(p_normed, 2 * b + j // 2 + 1)
                    if b * QUADS + j >= 2:
                        e.wait(pt_made, b * QUADS + j - 1)
                    for i in range(4):
                        last = pe.transpose(ps[0:SEQ, 4 + j % 2, batch(i)], prob[:, b % 2, 4 * j + i, :],
                                            ident[0:SEQ, 0:SEQ])
                    e.done(last, pt_done)

                def context(b, j):
                    e.wait(pt_made, b * QUADS + j + 1)
                    if b >= 2 and j == 0:
                        e.wait(ctx_split, 2 * (b - 1))
                    for i in range(4):
                        h = 4 * j + i
                        last = pe.matmul(ps[HD * i:HD * i + HD, 6 + b % 2, batch(j)],
                                         v_n[:, b, h * HD:(h + 1) * HD], prob_t[:, h, :], start=True, stop=True)
                    if j == QUADS - 1:
                        e.done(last, ctx_done)

                def key_tiles(first, end):
                    whi, wlo = chunk(C_CK)
                    for n in range(first, end):
                        t, c = divmod(n, 3)
                        if n >= 4:
                            e.wait(ck_made, n - 3)
                        for k in range(CT):
                            w = slice((t * CT + k) * P, (t * CT + k + 1) * P)
                            m = slice(c * 500, (c + 1) * 500)
                            _, last = split_products(pe, ps[:, n % 4, 0:500], whi[:, w], wlo[:, w],
                                                     m_hi[:, k, m], m_lo[:, k, m], k == 0, k == CT - 1)
                        e.done(last, ck_done if n < 5 else product)

                for s in range(2, NB + 2):
                    if s < NB:
                        scores(s)
                    if s == 2:
                        e.wait(v_made, NB)
                    for j in range(QUADS + 2):
                        if j < QUADS:
                            transposes(s - 2, j)
                        if j >= 2:
                            context(s - 2, j - 2)
                    if s == NB - 1:
                        e.wait(s_shifted, NB)
                        key_tiles(0, 2)
                    if s == NB:
                        key_tiles(2, 6)
                e.wait(ck_made, 6)
                e.wait(ctx_lo_made, 2 * (NB - 1))
                e.wait(ctx_lo_last, 1)
                for t in range(KT):
                    e.done(project(ps[:, t, 0:NT], C_DENSE + 2 * t, 0, P, KT, v_hi, v_lo, stop=False), product)
                    if t == 0:
                        e.wait(ctx_lo_last, 2)
                    e.done(project(ps[:, t, 0:NT], C_DENSE + 2 * t + 1, 0, P, KT, l_hi, l_lo, start=False), product)

                norm(2)
                vhi, vlo = chunk(C_CV)
                for n in range(6):
                    if n == 2:
                        e.wait(res_made, 2 * KT)
                    if n >= 4:
                        e.wait(cv_made, 2 * (n - 3))
                    for i in range(2):
                        m = slice((2 * n + i) * KC, (2 * n + i + 1) * KC)
                        out = ps[0:KC, CV_BANKS[n], i * CDIM:(i + 1) * CDIM]
                        for k in range(CT):
                            w = slice(k * CDIM, (k + 1) * CDIM)
                            pe.matmul(out, m_hi[:, k, m], vhi[:, w], start=k == 0, stop=False)
                            pe.matmul(out, m_hi[:, k, m], vlo[:, w], start=False, stop=False)
                            last = pe.matmul(out, m_lo[:, k, m], vhi[:, w], start=False, stop=k == CT - 1)
                    e.done(last, cv_done)
                norm_row(2)
                e.wait(norm_lo_made, 3)
                for t in range(CT):
                    whi, wlo = chunk(C_CQ + t)
                    for k in range(KT):
                        w = slice(k * P, (k + 1) * P)
                        first, last = split_products(pe, ps[:, t, 0:NT], whi[:, w], wlo[:, w], l_hi[:, k, :],
                                                     l_lo[:, k, :], k == 0, k == KT - 1)
                        if t == 0 and k == 0:
                            e.done(first, product)
                    e.done(last, product)
                e.wait(ck_lo_made, CT)
                e.wait(cv_made, 12)

                def quad(u):
                    q = cross_unit(u)[0]
                    return ((v_hi, v_lo), (l_hi, l_lo))[q % 2]

                def unit_scores(u):
                    q, b, pair = cross_unit(u)
                    if u == 0:
                        e.wait(quad0_made, 1)
                    elif u == 1:
                        e.wait(cq_lo_made, CT)
                    elif u % (2 * NB) == 0:
                        e.wait(quad_made, q)
                    if u >= 2:
                        e.wait(cexp_done, 2 * (u - 1))
                    m = slice(b * CTX, b * CTX + CEVEN)
                    for i in range(2):
                        hi, lo = (part[:, 2 * pair + i, batch(b)] for part in quad(u))
                        _, last = split_products(pe, ps[0:SEQ, cross_bank(u) + i, 0:CEVEN], hi, lo,
                                                 m_hi[:, q // 2, m], m_lo[:, q // 2, m], True, True)
                    e.done(last, cs_done)

                def unit_transposes(u):
                    e.wait(cp_normed, u + 1)
                    if u:
                        e.wait(cpt_made, u)
                    for i in range(2):
                        for c in range(NKC):
                            last = pe.transpose(ps[0:KC, 4 + i, c * SEQ:(c + 1) * SEQ],
                                                cp[:, u % 3, i, c * KC:(c + 1) * KC], ident[0:SEQ, 0:SEQ])
                    e.done(last, cpt_done)

                def unit_context(u):
                    q, b, pair = cross_unit(u)
                    e.wait(cpt_made, u + 1)
                    r = 64 * (q % 2) + 32 * pair
                    for i in range(2):
                        for c in range(NKC):
                            last = pe.matmul(ps[r:r + 32, 6 + q // 2, batch(b)],
                                             cv[:, b * NKC + c, 2 * q + pair, 32 * i:32 * i + 32],
                                             cpt[:, u % 2, i, c * SEQ:(c + 1) * SEQ],
                                             start=i + c == 0, stop=i == 1 and c == NKC - 1)
                    if u % (PAIRS // 2) == PAIRS // 2 - 1:
                        e.done(last, co_done)

                for s in range(PAIRS + 3):
                    if s < PAIRS:
                        unit_scores(s)
                    if 2 <= s < PAIRS + 2:
                        unit_transposes(s - 2)
                    if s >= 3:
                        unit_context(s - 3)
                for k in range(CT):
                    e.wait(cctx_lo_made, k + 1)
                    for t in range(KT):
                        whi, wlo = chunk(C_CDENSE + t // 2)
                        w = slice(((t % 2) * CT + k) * P, ((t % 2) * CT + k + 1) * P)
                        _, last = split_products(pe, ps[:, t, 0:NT], whi[:, w], wlo[:, w], v_hi[:, k, :],
                                                 v_lo[:, k, :], k == 0, k == CT - 1)
                        if k == CT - 1 and t % 2:
                            e.done(last, product)
                norm(3)
                norm_row(3)

                def glu(i):
                    xh, xl = ((v_hi, v_lo), (l_hi, l_lo))[i // FT]
                    if i >= 2:
                        e.wait(glu_made, i - 1)
                    for up in range(2):
                        e.done(project(ps[:, 4 + 2 * (i % 2) + up, 0:NT], c_glu(i) + up, 0, P, KT, xh, xl), product)

                def down(i):
                    whi, wlo = chunk(c_down(i))
                    e.wait(h_lo_made, i + 1)
                    for t in range(KT):
                        w = slice(t * P, (t + 1) * P)
                        _, last = split_products(pe, ps[:, t, 0:NT], whi[:, w], wlo[:, w], h_hi[:, i % 2, :],
                                                 h_lo[:, i % 2, :], i == 0, i == STEPS - 1)
                    e.done(last, product)

                e.wait(norm_lo_made, 4)
                glu(0)
                for i in range(1, STEPS):
                    if i == FT:
                        e.wait(norm_lo_made, 5)
                    glu(i)
                    down(i - 1)
                down(STEPS - 1)
                e.wait(y_made, KT)
                e.close()

        @block.vector
        def _(dve):
            for begun in (masks_made, fused_made, normed, y_made):
                dve.sem_inc(begun.sem, begun.first)
            made = [0]

            def setup(instruction, wait=True):
                instruction.then_inc(dve_set.sem, 1)
                made[0] += 1
                if wait:
                    dve.wait_ge(dve_set.sem, made[0])

            dve.wait_ge(act_set.sem, KT + 1)
            setup(dve.tensor_tensor(wm_lo, wm_raw, wm_hi.bitcast(F32), ALU.subtract))
            for k in range(KT):
                setup(dve.tensor_tensor(gate_part(m_lo, k), wg_raw[:, k, :],
                                        gate_part(m_hi, k).bitcast(F32), ALU.subtract))
            dve.wait_ge(pool_set.sem, 2)
            setup(dve.tensor_copy(row_f, row_i))
            setup(dve.tensor_copy(pos_f, pos_i))
            setup(dve.tensor_scalar(pos_neg, pos_f, 0.0, float(SEQ), ALU.is_lt, ALU.mult))
            setup(dve.tensor_tensor(pos_f, pos_f, pos_neg, ALU.add))
            setup(dve.tensor_scalar(pos_f, pos_f, 0.0, float(SEQ - 1), ALU.max, ALU.min))
            setup(dve.tensor_tensor(onehot, pos_f, row_f, ALU.is_equal))
            setup(dve.memset(ones_col[:], 1.0))
            dve.wait_ge(pe_set.sem, CT + 1)
            setup(dve.tensor_copy(cos_t[:], ps[:, 2, 0:SEQ]))
            setup(dve.tensor_copy(sin_t[:], ps[:, 3, 0:SEQ]))
            dve.wait_ge(act_set.sem, KT + CT + 1)
            for t in range(CT):
                setup(dve.tensor_tensor(wc_lo[:, t, :], ps[:, t, :], wc_hi[:, t, :].bitcast(F32), ALU.subtract))
            setup(dve.memset(m_hi[:, :, NB * CTX:CPAD].bitcast(F32), 0.0))
            setup(dve.memset(m_lo[:, :, NB * CTX:CPAD].bitcast(F32), 0.0))
            assert made[0] == DVE_SET
            dve.wait_ge(const_loaded.sem, 16 * len(loads))
            with dve.Fori(0, GROUPS) as g:
                e = Engine(dve, g)

                def low(out, source, high, signal):
                    e.done(dve.tensor_tensor(out, source, high.bitcast(F32), ALU.subtract), signal)

                e.wait(mask_loaded, 16)
                e.wait(product, 0)
                e.wait(y_made, 0)
                e.done(dve.tensor_scalar(is_pad[:], tt_in[:], 1, None, ALU.is_equal), masks_made)
                e.fence()
                e.done(dve.memset(is_v[:, :, SEQ - 1:SEQ], 0.0), step)
                e.done(dve.tensor_tensor(is_v[:, :, 0:SEQ - 1], is_pad[:, :, 0:SEQ - 1],
                                         is_pad[:, :, 1:SEQ], ALU.mult), step)
                e.fence()
                e.done(dve.tensor_scalar(is_l[:], is_v[:], -1.0, 1.0, ALU.mult, ALU.add), step)
                e.wait(x_hi_made, 1)
                low(v_lo[:], x_in[:], v_hi[:], x_lo_made)
                for t in range(CT):
                    e.wait(m_hi_made, t + 1)
                    low(m_lo[:, t, 0:NB * CTX], memt[:, t, :], m_hi[:, t, 0:NB * CTX], m_lo_made)
                for t in range(CT):
                    e.wait(u_hi_made, t + 1)
                    e.done(dve.scalar_tensor_tensor(l_lo[:, t, :], ps[:, t, 0:NT], float(DIM) ** -0.5,
                                                    l_hi[:, t, :].bitcast(F32), ALU.mult, ALU.subtract), u_lo_made)
                for b in range(NB):
                    e.wait(s0_done, b + 1)
                    e.done(dve.tensor_reduce(max0[:, b:b + 1], ps[0:SEQ, 2 + b, 0:CTX], AX_X, ALU.max), step)
                    e.fence()
                    e.done(dve.tensor_scalar(max0[:, b:b + 1], max0[:, b:b + 1], -1.0, None, ALU.mult), max0_made)
                for b in range(NB):
                    e.wait(p0_made, b + 1)
                    e.done(dve.reciprocal(rsum0[:, b:b + 1], sum0[:, b:b + 1]), step)
                    e.fence()
                    e.done(dve.tensor_scalar(p0[:, b, :], p0[:, b, :], rsum0[:, b:b + 1], None, ALU.mult), p0_normed)
                for b in range(NB):
                    e.wait(pt0_done, b + 1)
                    if b >= 2:
                        e.wait(am_done, b - 1)
                    e.done(dve.tensor_copy(pt0[:, b % 2, :], ps[0:KC, 6 + b % 2, 0:NKC * SEQ]), pt0_made)
                    if b:
                        e.wait(am_hi_made, b)
                        low(l_lo[:, CT:2 * CT, batch(b - 1)], ps[:, (b - 1) % 2, 0:CT * SEQ].rearrange(
                            "p (t s) -> p t s", t=CT), l_hi[:, CT:2 * CT, batch(b - 1)], am_lo_made)
                e.wait(am_hi_made, NB)
                low(l_lo[:, CT:2 * CT, batch(NB - 1)], ps[:, (NB - 1) % 2, 0:CT * SEQ].rearrange(
                    "p (t s) -> p t s", t=CT), l_hi[:, CT:2 * CT, batch(NB - 1)], am_lo_made)
                for t in range(KT):
                    e.wait(mc_made, t + 1)
                    e.wait(tanh_gate, t + 1)
                    e.done(dve.scalar_tensor_tensor(gate_t[:, t, :], gate_t[:, t, :], 1.0, mc[:, t, :],
                                                    ALU.add, ALU.mult), step)
                    e.fence()
                    e.done(dve.scalar_tensor_tensor(fused[:, t, :], gate_t[:, t, :], 0.5, x_in[:, t, :],
                                                    ALU.mult, ALU.add), fused_made)

                def norm_sum(n):
                    sq = squares[n]
                    e.wait(squared, n + 1)
                    e.done(dve.tensor_tensor(sq[:, 0:2, :], sq[:, 0:2, :], sq[:, 2:4, :], ALU.add), step)
                    e.fence()
                    e.done(dve.tensor_tensor(sq[:, 0, :], sq[:, 0, :], sq[:, 1, :], ALU.add), sq_summed)
                    e.wait(sumsq_done, n + 1)
                    if n:
                        e.wait(powered, n)
                    e.done(dve.tensor_scalar(mean_sq[:], ps[0:SEQ, 6, 0:NB], EPS, None, ALU.add), mean_made)

                def norm_scale(out, source, n, t, row, signal):
                    e.done(dve.scalar_tensor_tensor(out[:, t, :], source[:, t, :], norm_w[:, n, t:t + 1], row,
                                                    ALU.mult, ALU.mult), signal)

                def norm_experts(n, first):
                    e.wait(rstd_done, n + 1)
                    for mask_of, row in ((is_v, rstd_v), (is_l, rstd_l)):
                        e.done(dve.tensor_tensor(row[:], ps[:, 7, 0:NT], mask_of[:].rearrange("p b s -> p (b s)"),
                                                 ALU.mult), step)
                    e.fence()
                    for out, row in ((norm_v[n], rstd_v[:]), (norm_l[n], rstd_l[:])):
                        for t in range(KT):
                            norm_scale(out, res, n, t, row, normed if t == KT - 1 else step)
                    e.wait(norm_hi_made, first)
                    low(v_lo[:], norm_v[n], v_hi[:], norm_lo_made)
                    e.wait(norm_hi_made, first + 1)
                    low(l_lo[:], norm_l[n], l_hi[:], norm_lo_made)

                norm_sum(0)
                e.wait(rstd_done, 1)
                for t in range(KT):
                    norm_scale(res, fused, 0, t, ps[:, 7, 0:NT], res_made)
                norm_sum(1)
                norm_experts(1, 1)
                for j in range(2 * KT):
                    out = (q_t, k_t)[j // KT][:, j % KT, :]
                    now, s = ps[:, j % 4, 0:NT], j % 2
                    e.wait(product, C_QK + 2 * j + 2)
                    if j >= 2:
                        e.fence()
                    e.done(dve.tensor_tensor(roc[:, s, :].rearrange("p (b s) -> p b s", b=NB),
                                             now.rearrange("p (b s) -> p b s", b=NB),
                                             cos_t[:].unsqueeze(1).to_broadcast([P, NB, SEQ]), ALU.mult), step)
                    e.done(dve.stream_shuffle(rot[:, s, :], now, [(i + HD // 2) % HD for i in range(HD)]), rotated)
                    e.fence()
                    e.done(dve.tensor_tensor(rot[:, s, :].rearrange("p (b s) -> p b s", b=NB),
                                             rot[:, s, :].rearrange("p (b s) -> p b s", b=NB),
                                             sin_t[:].unsqueeze(1).to_broadcast([P, NB, SEQ]), ALU.mult), step)
                    e.fence()
                    e.done(dve.tensor_tensor(out, rot[:, s, :], roc[:, s, :], ALU.add), roped)
                def key_blocks(b):
                    for j in range(4):
                        e.done(dve.tensor_scalar(kb[:, b % 2, :, j, :], k_t[:, :, batch(b)], smask[:, j:j + 1], None,
                                                 ALU.mult), kb_made if j == 3 else step)

                e.fence()
                key_blocks(0)
                key_blocks(1)
                for s in range(NB + 2):
                    if s < NB:
                        e.wait(s_done, s + 1)
                        now = ps[0:SEQ, 0:4, 0:NT].rearrange("p m (j s) -> p m j s", j=4)
                        e.done(dve.tensor_reduce(max_s[:].rearrange("p (m j) -> p m j", j=4), now, AX_X, ALU.max), step)
                        e.fence()
                        if s >= 2:
                            e.wait(pt_done, (s - 1) * QUADS)
                        e.done(dve.tensor_tensor(
                            prob[:, s % 2].rearrange("p (m j) s -> p m j s", j=4), now,
                            max_s[:].rearrange("p (m j) -> p m j", j=4).unsqueeze(3).to_broadcast([SEQ, KT, 4, SEQ]),
                            ALU.subtract), s_shifted)
                        if s + 2 < NB:
                            key_blocks(s + 2)
                        e.wait(exp_done, s + 1)
                        e.done(dve.tensor_reduce(rsum_s[:, s % 2, :], prob[:, s % 2], AX_X, ALU.add), step)
                        e.fence()
                        e.done(dve.reciprocal(rsum_s[:, s % 2, :], rsum_s[:, s % 2, :]), rsum_made)
                    if s >= 2:
                        b = s - 2
                        e.wait(ctx_done, b + 1)
                        if b >= 2:
                            e.wait(ctx_lo_made, 2 * (b - 1))
                        now = ps[:, 6 + b % 2, 0:NT].rearrange("p (t s) -> p t s", t=KT)
                        for out, mask_of in ((ctx_v, is_v), (ctx_l, is_l)):
                            e.done(dve.tensor_tensor(out[:, b % 2], now,
                                                     mask_of[:, b, :].unsqueeze(1).to_broadcast([P, KT, SEQ]),
                                                     ALU.mult), ctx_split)
                b = NB - 1
                e.wait(ctx_hi_made, 2 * b + 1)
                low(v_lo[:, :, batch(b)], ctx_v[:, b % 2], v_hi[:, :, batch(b)], ctx_lo_last)
                e.wait(ctx_hi_made, 2 * b + 2)
                low(l_lo[:, :, batch(b)], ctx_l[:, b % 2], l_hi[:, :, batch(b)], ctx_lo_last)
                for t in range(KT):
                    e.wait(product, C_DENSE + 2 * t + 2)
                    e.done(dve.tensor_tensor(res[:, t, :], ps[:, t, 0:NT], res[:, t, :], ALU.add), res_made)
                norm_sum(2)
                e.wait(czero_set, 1)
                for n in range(6):
                    e.wait(cv_done, n + 1)
                    now = ps[0:KC, CV_BANKS[n], :].rearrange("p (i h d) -> p i h d", i=2, h=HEADS // 2)
                    for odd in range(2):
                        e.done(dve.tensor_copy(cv[:, 2 * n:2 * n + 2, :, 3 * CHD * odd:3 * CHD * odd + CHD],
                                               now[:, :, :, CHD * odd:CHD * odd + CHD]), cv_made)
                e.wait(rstd_done, 3)
                for t in range(KT):
                    norm_scale(norm_v[2], res, 2, t, ps[:, 7, 0:NT], normed if t == KT - 1 else step)
                e.wait(norm_hi_made, 3)
                low(l_lo[:], norm_v[2], l_hi[:], norm_lo_made)
                for t in range(CT):
                    e.wait(ck_hi_made, t + 1)
                    low(m_lo[:, t, 0:NB * CTX], ck[:, t, :], m_hi[:, t, 0:NB * CTX], ck_lo_made)
                for t in range(CT):
                    e.wait(cq_hi_made, t + 1)
                    low(h_lo[:, t, :], ps[:, t, 0:NT], h_hi[:, t, :], cq_lo_made)
                    if t == 0:
                        e.fence()
                        for out, part in ((v_hi, h_hi), (v_lo, h_lo)):
                            for i in range(4):
                                e.done(dve.tensor_scalar(out[:, i, :], part[:, 0, :].bitcast(F32), cmask[:, i:i + 1],
                                                         None, ALU.mult),
                                       quad0_made if part is h_lo and i == 3 else step)

                def cross_low(t):
                    e.wait(cctx_hi_made, t + 1)
                    low(v_lo[:, t, :], ps[:, 6 + t, 0:NT], v_hi[:, t, :], cctx_lo_made)

                for s in range(PAIRS + 1):
                    if s < PAIRS:
                        e.wait(cs_done, s + 1)
                        if s >= 3:
                            e.wait(cexp_done, 2 * (s - 2))
                        e.done(dve.tensor_reduce(max_c[:, s % 3, :], ps[0:SEQ, cross_bank(s):cross_bank(s) + 2, 0:CTX],
                                                 AX_X, ALU.max), step)
                        e.fence()
                        e.done(dve.tensor_scalar(max_c[:, s % 3, :], max_c[:, s % 3, :], -float(CHD) ** -0.5, None,
                                                 ALU.mult), cmax_made)
                    if s:
                        u = (s - 1) % 3
                        e.wait(cexp_done, 2 * s)
                        e.done(dve.reciprocal(rsum_c[:, u, :], sum_c[:, u, :]), step)
                        e.fence()
                        for i in range(2):
                            e.done(dve.tensor_scalar(cp[:, u, i, :], cp[:, u, i, :], rsum_c[:, u, i:i + 1], None,
                                                     ALU.mult), cp_normed if i else step)
                    if s == 6 * NB + 4:
                        cross_low(0)
                cross_low(1)
                for t in range(KT):
                    e.wait(product, C_CDENSE + t // 2 + 1)
                    e.done(dve.tensor_tensor(res[:, t, :], ps[:, t, 0:NT], res[:, t, :], ALU.add), res_made)
                norm_sum(3)
                norm_experts(3, 4)
                for i in range(STEPS):
                    s = i % 2
                    e.wait(tanh_mlp, i + 1)
                    if i >= 2:
                        e.wait(h_lo_made, i - 1)
                    e.done(dve.scalar_tensor_tensor(act_a[:, s, :], act_t[:, s, :], 1.0, ps[:, 4 + 2 * s, 0:NT],
                                                    ALU.add, ALU.mult), step)
                    e.fence()
                    e.done(dve.scalar_tensor_tensor(act_h[:, s, :], act_a[:, s, :], 0.5, ps[:, 5 + 2 * s, 0:NT],
                                                    ALU.mult, ALU.mult), glu_made)
                    e.wait(h_hi_made, i + 1)
                    low(h_lo[:, s, :], act_h[:, s, :], h_hi[:, s, :], h_lo_made)
                e.wait(stored, 0)
                e.wait(product, CHUNKS)
                for t in range(KT):
                    e.done(dve.tensor_tensor(y_out[:, t, :], ps[:, t, 0:NT], res[:, t, :], ALU.add), y_made)
                e.close()


def kernel(**inputs):
    import numpy as np
    import concourse.bacc as bacc
    from concourse.bass_utils import run_bass_kernel_spmd

    a = {name: np.asarray(x) for name, x in inputs.items()}

    def w(name, layer=1):
        return a[f"L{layer}_xattn_{name}"]

    def by_tile(m, n=None):
        m = m if n is None else m[:, n * P:(n + 1) * P]
        return m.reshape(-1, P, m.shape[1]).transpose(1, 0, 2)

    def flat(*blocks):
        return np.concatenate([x.reshape(P, -1) for x in blocks], axis=1)

    def padded(m, axis):
        wide = [(0, 0), (0, 0)]
        wide[axis] = (0, FT * P - INTER)
        return np.pad(m, wide)

    w_mem, w_gate = w("W_mem", 0), w("W_gate", 0).T
    qkv, dense = (w("v_qkv"), w("l_qkv")), (w("v_dense"), w("l_dense"))
    gates = [padded(w(f"{n}_gate"), 1) for n in "vl"]
    ups = [padded(w(f"{n}_up"), 1) for n in "vl"]
    downs = [padded(w(f"{n}_down"), 0) for n in "vl"]
    chunks = [flat(by_tile(w_mem, t)) for t in range(CT)]
    chunks += [flat(by_tile(w_mem.T, 2 * c), by_tile(w_mem.T, 2 * c + 1)) for c in range(KT // 2)]
    chunks += [flat(by_tile(w_gate[:DIM], t)) for t in range(KT)]
    chunks += [flat(by_tile(qkv[x], j)) for j in range(2 * KT) for x in range(EXPERTS)]
    chunks += [qkv[x][k * P:(k + 1) * P, 2 * DIM:] for k in range(KT) for x in range(EXPERTS)]
    ckv = w("ckv_w")
    chunks.append(flat(by_tile(ckv, 0), by_tile(ckv, 1)))
    chunks += [flat(by_tile(dense[x], t)) for t in range(KT) for x in range(EXPERTS)]
    chunks.append(flat(by_tile(ckv[:, CDIM:])))
    chunks += [flat(by_tile(w("cq_w"), t)) for t in range(CT)]
    cd = w("cdense_w")
    chunks += [flat(by_tile(cd, 2 * c), by_tile(cd, 2 * c + 1)) for c in range(KT // 2)]
    mlp = [None] * (3 * STEPS)
    for i in range(STEPS):
        x, f = divmod(i, FT)
        mlp[c_glu(i) - C_MLP] = flat(by_tile(gates[x], f))
        mlp[c_glu(i) + 1 - C_MLP] = flat(by_tile(ups[x], f))
        mlp[c_down(i) - C_MLP] = downs[x][f * P:(f + 1) * P]
    weights = np.stack(chunks + mlp)
    assert weights.shape == (CHUNKS, P, 512)

    angle = np.outer(np.arange(SEQ, dtype=np.float32),
                     np.float32(1) / np.float32(10000) ** (np.arange(0, HD, 2, dtype=np.float32) / np.float32(HD)))
    cos, sin = np.cos(angle), np.sin(angle)
    tables = np.stack([np.tile(np.concatenate([cos, cos], 1), (1, P // HD)),
                       np.tile(np.concatenate([-sin, sin], 1), (1, P // HD))], 1).astype(np.float32)
    after = np.triu(np.full((SEQ, SEQ), MASKED, np.float32), 1)
    causal = np.repeat(after[:, None, :], NB, 1)
    head_masks = np.concatenate([np.equal.outer(np.arange(P) // width, np.arange(P // width))
                                 for width in (CHD, HD)], 1).astype(np.float32)

    x, mem = a["x"], a["ctx_1024"]
    arrays = {
        "x_t": x.reshape(GROUPS, NT, KT, P).transpose(0, 3, 2, 1),
        "mem_t": mem.reshape(GROUPS, NB * CTX, CT, P).transpose(0, 3, 2, 1),
        "mem_n": mem.reshape(GROUPS, NB * NKC, KC, CDIM).transpose(0, 2, 1, 3),
        "weights": weights,
        "w_gate_mem": by_tile(w_gate[DIM:]),
        "w_mem": by_tile(w_mem),
        "b_gate": w("b_gate", 0).reshape(KT, P).T,
        "norms": np.stack([n.reshape(KT, P).T for n in (
            w("norm_w", 0), w("ln_in_w"), w("ln_post_cross_w"), w("ln_post_attn_w"))], 1),
        "pos": a["pos_1xS"],
        "mask": a["mask_BxS_ik0"].reshape(GROUPS, 1, NT),
        "rope_tables": tables,
        "identity_in": np.eye(P, dtype=np.float32),
        "causal_in": causal,
        "head_masks": head_masks,
    }
    arrays = {name: np.ascontiguousarray(x) for name, x in arrays.items()}
    nc = bacc.Bacc("TRN2", target_bir_lowering=False, num_devices=1)
    args = {name: nc.dram_tensor(name, x.shape, mybir.dt.from_np(x.dtype), kind="ExternalInput").ap()
            for name, x in arrays.items()}
    out = nc.dram_tensor("out_t", (GROUPS, P, KT, NT), F32, kind="ExternalOutput").ap()
    build_xattn(nc, **args, out_t=out)
    got = run_bass_kernel_spmd(nc, [arrays], core_ids=[0]).results[0]["out_t"]
    return got.transpose(0, 3, 2, 1).reshape(BATCHES, SEQ, DIM)
```

```python
from contextlib import ExitStack

import concourse.bass as bass
from concourse import mybir

F32 = mybir.dt.float32
F32R = mybir.dt.float32r
BF16 = mybir.dt.bfloat16
I32 = mybir.dt.int32
ALU = mybir.AluOpType
ACT = mybir.ActivationFunctionType
AX_X = mybir.AxisListType.X

P = 128
BATCHES, SEQ, DIM = 32, 112, 512
CTX, CDIM = 375, 256
NB = 4
GROUPS = BATCHES // NB
NT = NB * SEQ
KT = DIM // P
CT = CDIM // P
HEADS, HD = 16, 32
CHD = 16
QUADS = HEADS // 4
KC, NKC = 125, 3
CPAD = NB * CTX + 4
CEVEN = CTX + 1
INTER = 1376
FT = -(-INTER // P)
EXPERTS = 2
EPS = 1e-6
MASKED = -3.0e38

C_U = 0
C_MC = C_U + CT
C_GATE = C_MC + KT // 2
C_QK = C_GATE + KT
C_V = C_QK + 2 * KT * EXPERTS
C_CK = C_V + KT * EXPERTS
C_DENSE = C_CK + 1
C_CV = C_DENSE + KT * EXPERTS
C_CQ = C_CV + 1
C_CDENSE = C_CQ + CT
C_MLP = C_CDENSE + KT // 2
STEPS = EXPERTS * FT
CHUNKS = C_MLP + 3 * STEPS
LAG = 3
RING = 7
assert CHUNKS % RING == 0
CV_BANKS = (4, 5, 2, 3, 4, 5)
PE_SET, ACT_SET, DVE_SET, POOL_SET = CT + 1, KT + CT + 4, 21, 2
NORMED = 5 * KT
DVE_STEPS = 160


def c_glu(step):
    return C_MLP + (3 * step - 1 if step else 0)


def c_down(step):
    return C_MLP + (3 * step + 4 if step < STEPS - 1 else 3 * STEPS - 1)


class Signal:

    def __init__(self, ctx, nc, name, per_group=0, first=0):
        self.sem = ctx.enter_context(nc.semaphore(name))
        self.name, self.per_group, self.first = name, per_group, first


class Engine:

    def __init__(self, group):
        self.group, self.last, self.count = group, None, {}

    def at(self, signal, events):
        return signal.sem, self.group * signal.per_group + (signal.first + events)

    def next(self, signal):
        self.count[signal] = self.count.get(signal, 0) + 1
        self.last = signal
        return signal.sem, 1

    def own(self):
        return self.at(self.last, self.count[self.last])

    def close(self):
        wrong = {s.name: n for s, n in self.count.items() if n != s.per_group}
        assert not wrong, wrong


def split_products(pe, out, w_hi, w_lo, x_hi, x_lo, start, stop):
    first = pe.matmul(out, w_hi, x_hi, start=start, stop=False)
    pe.matmul(out, w_hi, x_lo, start=False, stop=False)
    return first, pe.matmul(out, w_lo, x_hi, start=False, stop=stop)


def cross_unit(u):
    return u // (2 * NB), u // 2 % NB, u % 2


def cross_bank(u):
    return 2 - 2 * (u % 2)


def build_xattn(nc, x_t, mem_t, mem_n, weights, w_gate_mem, w_mem, b_gate, norms, pos, mask,
                rope_tables, identity_in, causal_in, head_masks, out_t):
    with ExitStack() as ctx:
        def sb(name, shape, dt=F32):
            return ctx.enter_context(nc.sbuf_tensor(name, shape, dt))

        def signal(name, per_group=0, first=0):
            return Signal(ctx, nc, name, per_group, first)

        ps = ctx.enter_context(nc.psum_tensor("ps", [P, 8, 512], F32))

        w_raw = sb("w_raw", [P, RING, 512])
        w_hi, w_lo = sb("w_hi", [P, RING, 512], F32R), sb("w_lo", [P, RING, 512], F32R)
        v_hi, v_lo = sb("v_hi", [P, KT, NT], F32R), sb("v_lo", [P, KT, NT], F32R)
        l_hi, l_lo = sb("l_hi", [P, KT, NT], F32R), sb("l_lo", [P, KT, NT], F32R)
        m_hi, m_lo = sb("m_hi", [P, CT, CPAD], F32R), sb("m_lo", [P, CT, CPAD], F32R)
        wc_hi, wc_lo = sb("wc_hi", [P, CT, DIM], F32R), sb("wc_lo", [P, CT, DIM], F32R)
        h_hi, h_lo = sb("h_hi", [P, 2, NT], F32R), sb("h_lo", [P, 2, NT], F32R)
        x_in, res = sb("x_in", [P, KT, NT]), sb("res", [P, KT, NT])
        tt_in = sb("tt_in", [P, NB, SEQ], I32)
        is_pad, is_v, is_l = (sb(n, [P, NB, SEQ]) for n in ("is_pad", "is_v", "is_l"))
        rstd_l = sb("rstd_l", [P, NT])
        mean_sq, rstd_t = sb("mean_sq", [SEQ, 2, NB]), sb("rstd_t", [SEQ, 2, NB])
        minus_half = sb("minus_half", [SEQ, NB])
        ident = sb("ident", [P, P])
        ident_b = sb("ident_b", [P, P], BF16)
        causal = sb("causal", [SEQ, NB, SEQ], BF16)
        ones_col = sb("ones_col", [P, 1])
        cos_t, sin_t = sb("cos_t", [P, SEQ]), sb("sin_t", [P, SEQ])
        norm_w = sb("norm_w", [P, 4, KT])
        norm_w00, norm_w01 = sb("norm_w00", [P, KT]), sb("norm_w01", [P, KT])
        gate_b, half_b = sb("gate_b", [P, KT]), sb("half_b", [P, KT])
        head_mask = sb("head_mask", [P, P // CHD + P // HD])
        cmask, smask = head_mask[:, 0:P // CHD], head_mask[:, P // CHD:]
        max0, sum0, rsum0 = (sb(n, [SEQ, NB]) for n in ("max0", "sum0", "rsum0"))
        max_s, rsum_s = sb("max_s", [SEQ, HEADS]), sb("rsum_s", [SEQ, 2, HEADS])
        max_c, sum_c, rsum_c = (sb(n, [SEQ, 4, 2]) for n in ("max_c", "sum_c", "rsum_c"))
        ARENA = 16384
        arena = sb("arena", [P, ARENA])

        def view(at, shape, parts=P):
            n = 1
            for s in shape:
                n *= s
            assert at + n <= ARENA
            flat = arena[0:parts, at:at + n]
            if len(shape) == 1:
                return flat
            names = "abcd"[:len(shape)]
            sizes = {c: s for c, s in zip(names[1:], shape[1:])}
            return flat.rearrange(f"p ({' '.join(names)}) -> p {' '.join(names)}", **sizes)

        memn = view(0, (NB * NKC, CDIM), KC)
        memt = view(3072, (CT, NB * CTX))
        p0 = view(6072, (NB, CTX), SEQ)
        pt0 = view(7572, (2, NKC * SEQ), KC)
        mc = view(8244, (KT, NT))
        gate_t = view(10036, (KT, NT))
        fused = view(11828, (KT, NT))
        q_t, k_t = view(0, (KT, NT)), view(1792, (KT, NT))
        rot, roc = view(12800, (2, NT)), view(13696, (2, NT))
        kb = view(3584, (2, KT, 4, SEQ))
        v_n = view(7168, (NB, DIM), SEQ)
        prob = view(9216, (2, HEADS, SEQ), SEQ)
        prob_t = view(12800, (HEADS, SEQ), SEQ)
        ctx_v, ctx_l = view(14592, (2, KT, SEQ)), view(15488, (2, KT, SEQ))
        ck = view(0, (CT, NB * CTX))
        cv = view(3000, (NB * NKC, HEADS // 2, 4 * CHD), KC)
        cp = view(9144, (4, 2, CTX), SEQ)
        cpt = view(12144, (2, 2, NKC * SEQ), KC)
        act_t, act_a, act_h = view(11448, (2, NT)), view(12344, (2, NT)), view(13240, (2, NT))
        y_out = view(14136, (KT, NT))
        squares = [view(at, (KT, NT)) for at in (13620, 0, 12162, 6072)]
        norm_v = [None, view(1792, (KT, NT)), view(13954, (KT, NT)), view(7864, (KT, NT))]
        norm_l = [None, view(3584, (KT, NT)), None, view(9656, (KT, NT))]
        wm_raw, wg_raw = view(6144, (KT, CDIM)), view(7168, (KT, DIM))
        table_sb, onehot = view(9216, (2, P), SEQ), view(9472, (SEQ,), SEQ)
        pos_i, row_i = view(9584, (SEQ,), SEQ).bitcast(I32), view(9696, (SEQ,), SEQ).bitcast(I32)
        pos_f, pos_neg, row_f = (view(at, (SEQ,), SEQ) for at in (9808, 9920, 10032))
        causal_raw = view(10144, (NB, SEQ), SEQ)
        wm_hi, wm_lo = v_hi[:, :, 0:CDIM], v_lo[:, :, 0:CDIM]

        def gate_part(t, k):
            return t[:, k // 2, (k % 2) * DIM:(k % 2 + 1) * DIM]

        const_loaded, setup_loaded = signal("const_loaded"), signal("setup_loaded")
        x_loaded, mask_loaded = signal("x_loaded", 16), signal("mask_loaded", 16)
        memt_loaded, memn_loaded = signal("memt_loaded", 16), signal("memn_loaded", 16)
        w_loaded = [signal(f"w_loaded{i}", 16 * CHUNKS // RING) for i in range(RING)]
        w_hi_made, w_lo_made = signal("w_hi_made", CHUNKS), signal("w_lo_made", CHUNKS)
        product = signal("product", CHUNKS, first=RING)
        stored = signal("stored", 16, first=1)
        dve_set, pe_set, act_set, pool_set = (signal(n) for n in (
            "dve_set", "pe_set", "act_set", "pool_set"))
        s0_done, pt0_done, am_done = (signal(n, NB) for n in ("s0_done", "pt0_done", "am_done"))
        sumsq_done, rstd_done = signal("sumsq_done", 3), signal("rstd_done", 4)
        s_done, pt_done = signal("s_done", NB), signal("pt_done", NB * QUADS)
        ctx_done = signal("ctx_done", NB)
        ck_done, cv_done = signal("ck_done", 5), signal("cv_done", 6)
        PAIRS = NB * HEADS // 2
        cs_done, cpt_done = signal("cs_done", PAIRS), signal("cpt_done", PAIRS)
        co_done, cdense_even = signal("co_done", CT), signal("cdense_even", KT // 2)
        x_hi_made, m_hi_made, u_hi_made = (signal("x_hi_made", 1), signal("m_hi_made", CT),
                                           signal("u_hi_made", CT))
        p0_made, am_hi_made, mc_made = (signal("p0_made", NB), signal("am_hi_made", NB),
                                        signal("mc_made", KT))
        tanh_gate, squared = signal("tanh_gate", KT), signal("squared", 3 * KT)
        norm_hi_made, ctx_hi_made = signal("norm_hi_made", NORMED), signal("ctx_hi_made", 2 * NB)
        v_made, exp_done, pt_made = (signal("v_made", NB), signal("exp_done", NB),
                                     signal("pt_made", NB * QUADS))
        ck_made, ck_hi_made, cq_hi_made = (signal("ck_made", 6), signal("ck_hi_made", CT),
                                           signal("cq_hi_made", CT))
        cexp_done, cpt_made = signal("cexp_done", 2 * PAIRS), signal("cpt_made", PAIRS)
        quad0_hi_made = signal("quad0_hi_made", 4)
        cpt_odd_made = signal("cpt_odd_made", PAIRS // 2)
        cctx_hi_made = signal("cctx_hi_made", CT)
        tanh_mlp, h_hi_made = signal("tanh_mlp", STEPS), signal("h_hi_made", STEPS)
        step = signal("step", DVE_STEPS)
        masks_made = signal("masks_made", 1)
        x_lo_made, m_lo_made, u_lo_made = (signal("x_lo_made", 1), signal("m_lo_made", CT),
                                           signal("u_lo_made", CT))
        max0_made, p0_normed, pt0_made = (signal(n, NB) for n in (
            "max0_made", "p0_normed", "pt0_made"))
        am_lo_made, fused_made = signal("am_lo_made", NB), signal("fused_made", KT)
        sq_summed, mean_made = signal("sq_summed", 4), signal("mean_made", 3)
        res_made, normed = signal("res_made", 3 * KT), signal("normed", NORMED)
        norm_lo_even, ctx_lo_last = signal("norm_lo_even", NORMED // 2), signal("ctx_lo_last", 2)
        rotated, roped = signal("rotated", 2 * KT), signal("roped", 2 * KT)
        rstd_read = signal("rstd_read", 1)
        p_normed_late = signal("p_normed_late", NB - 2)
        kb_made, s_shifted, rsum_made, ctx_split = (signal("kb_made", NB), signal("s_shifted", NB),
                                                    signal("rsum_made", NB), signal("ctx_split", 2 * NB))
        cv_made, ck_lo_made, cq_lo_made = (signal("cv_made", 12), signal("ck_lo_made", 1),
                                           signal("cq_lo_made", CT))
        quad0_made, cmax_made, cp_normed = (signal("quad0_made", 2), signal("cmax_made", PAIRS),
                                            signal("cp_normed", PAIRS))
        cctx_lo_made = signal("cctx_lo_made", CT)
        down_done = signal("down_done", KT - 1)
        glu_made, h_lo_made = signal("glu_made", STEPS), signal("h_lo_made", STEPS)
        y_made = signal("y_made", KT, first=1)
        powered, czero_set, quad_made = (signal("powered", 4), signal("czero_set", 1),
                                         signal("quad_made", QUADS - 1))
        norm_lo_odd, ck_lo_late = signal("norm_lo_odd", NORMED // 2), signal("ck_lo_late", 1)
        p_normed, ctx_lo_made = signal("p_normed", NB + 2), signal("ctx_lo_made", 2 * (NB - 1))

        loads = [(ident, identity_in), (norm_w, norms), (gate_b, b_gate), (head_mask, head_masks)]
        setups = [(wm_raw, w_mem), (wg_raw, w_gate_mem), (table_sb, rope_tables),
                  (causal_raw, causal_in),
                  (pos_i, pos.broadcast_to([SEQ, SEQ]))]
        block = ctx.enter_context(nc.Block())

        def batch(b):
            return slice(b * SEQ, (b + 1) * SEQ)

        norm_parts = [(v_hi, v_lo, norm_v[1]), (l_hi, l_lo, norm_l[1]), (l_hi, l_lo, norm_v[2]),
                      (v_hi, v_lo, norm_v[3]), (l_hi, l_lo, norm_l[3])]

        @block.sync
        def _(sp):
            sp.sem_inc(stored.sem, stored.first)
            for dst, src in loads:
                sp.dma_start(dst[:], src).then_inc(const_loaded.sem, 16)
            for dst, src in setups:
                sp.dma_start(dst, src).then_inc(setup_loaded.sem, 16)

            def load_inputs(group, ahead):
                for dst, src, loaded in (
                        (tt_in[:].rearrange("p b s -> p (b s)"), mask[ahead:][group].broadcast_to([P, NT]), mask_loaded),
                        (x_in[:], x_t[ahead:][group], x_loaded), (memt, mem_t[ahead:][group], memt_loaded),
                        (memn, mem_n[ahead:][group], memn_loaded)):
                    sp.dma_start(dst, src).then_inc(loaded.sem, 16)

            def load_chunk(c):
                sp.dma_start(w_raw[:, c % RING, :], weights[c % CHUNKS]).then_inc(w_loaded[c % RING].sem, 16)

            load_inputs(0, 0)
            for c in range(RING):
                load_chunk(c)
            with sp.Fori(0, GROUPS) as g:
                e = Engine(g)
                for c in range(RING, CHUNKS + RING - 1):
                    sp.wait_ge(*e.at(w_lo_made, c - RING + (1 if c < CHUNKS + RING - 2 else 2)))
                    load_chunk(c)
                    if c == C_MLP + 2 * RING:
                        load_inputs(g, 1)
                sp.wait_ge(*e.at(y_made, KT))
                load_chunk(CHUNKS + RING - 1)
                sp.dma_start(out_t[g], y_out).then_inc(stored.sem, 16)
            sp.wait_ge(stored.sem, stored.first + 16 * GROUPS)
            sp.wait_ge(mask_loaded.sem, 16 * (GROUPS + 1))
            sp.wait_ge(memn_loaded.sem, 16 * (GROUPS + 1))

        @block.gpsimd
        def _(pool):
            pool.memset(minus_half[:], -0.5).then_inc(pool_set.sem, 1)
            pool.iota(row_i, pattern=[[0, SEQ]], base=0, channel_multiplier=1).then_inc(pool_set.sem, 1)
            pool.wait_ge(pool_set.sem, POOL_SET)

            def low_part(e, c):
                slot = c % RING
                pool.wait_ge(*e.at(w_hi_made, c + 1))
                pool.tensor_tensor(w_lo[:, slot, :], w_raw[:, slot, :],
                                          w_hi[:, slot, :].bitcast(F32), ALU.subtract).then_inc(*e.next(w_lo_made))

            for c in range(RING):
                low_part(Engine(0), c)
            with pool.Fori(0, GROUPS) as g:
                e = Engine(g)

                made = [RING]

                def low_parts(end):
                    for c in range(made[0], end):
                        low_part(e, c)
                    made[0] = end

                def power(n):
                    pool.wait_ge(*e.at(mean_made, n))
                    pool.tensor_tensor(rstd_t[:, 0], mean_sq[:, 0], minus_half[:], ALU.pow).then_inc(*e.next(powered))

                def norm_lows(block, first=0, tiles=KT):
                    hi, lo, now = norm_parts[block]
                    for t in range(first + 1, first + tiles, 2):
                        pool.wait_ge(*e.at(norm_hi_made, KT * block + t + 1))
                        pool.tensor_tensor(lo[:, t, :], now[:, t, :], hi[:, t, :].bitcast(F32),
                                                  ALU.subtract).then_inc(*e.next(norm_lo_odd))

                low_parts(C_QK + 5)
                pool.wait_ge(*e.at(mean_made, 1))
                for which in (1, 0):
                    pool.tensor_tensor(rstd_t[:, which], mean_sq[:, which], minus_half[:], ALU.pow).then_inc(
                        *e.next(powered))
                norm_lows(0)
                norm_lows(1)

                def normalise(b):
                    pool.wait_ge(*e.at(rsum_made, b + 1))
                    for half in range(2 if b < 2 else 1):
                        now = prob[:, b % 2, 8 * half:8 * half + 8, :]
                        pool.tensor_tensor(now, now, rsum_s[:, b % 2, 8 * half:8 * half + 8].unsqueeze(
                            2).to_broadcast([SEQ, 8, SEQ]), ALU.mult).then_inc(*e.next(p_normed))

                low_parts(C_CK)
                normalise(0)
                low_parts(C_CK + 3)
                normalise(1)
                low_parts(C_CK + RING)
                for s in range(2, NB + 1):
                    if s < NB:
                        normalise(s)
                    b = s - 2
                    pool.wait_ge(*e.at(ctx_hi_made, 2 * b + 2))
                    for lo, hi, now in ((v_lo, v_hi, ctx_v), (l_lo, l_hi, ctx_l)):
                        pool.tensor_tensor(lo[:, :, batch(b)], now[:, b % 2], hi[:, :, batch(b)].bitcast(F32),
                                                  ALU.subtract).then_inc(*e.next(ctx_lo_made))
                low_parts(C_CV)
                pool.memset(cv[:, :, :, CHD:3 * CHD], 0.0).then_inc(*e.next(czero_set))
                low_parts(C_CQ + CT)
                power(2)
                norm_lows(2)
                low_parts(C_CDENSE)
                pool.wait_ge(*e.at(cq_lo_made, CT))
                for q in range(1, QUADS):
                    if q >= 2:
                        pool.wait_ge(*e.at(cs_done, 2 * NB * (q - 1)))
                    for out, part in zip(((v_hi, v_lo), (l_hi, l_lo))[q % 2], (h_hi, h_lo)):
                        last = pool.tensor_tensor(
                            out[:], part[:, q // 2, :].bitcast(F32).unsqueeze(1).to_broadcast([P, 4, NT]),
                            cmask[:, 4 * (q % 2):4 * (q % 2) + 4].unsqueeze(2).to_broadcast([P, 4, NT]), ALU.mult)
                        if part is h_lo:
                            last.then_inc(*e.next(quad_made))
                    if q == 1:
                        pool.wait_ge(*e.at(ck_hi_made, CT))
                        pool.tensor_tensor(m_lo[:, 1, 0:NB * CTX], ck[:, 1, :],
                                                  m_hi[:, 1, 0:NB * CTX].bitcast(F32), ALU.subtract).then_inc(*e.next(ck_lo_late))
                low_parts(C_CDENSE + RING - 2)
                power(3)
                norm_lows(3)
                low_parts(C_MLP + 3)
                low_parts(C_MLP + RING)
                for i in range(KT // 2):
                    norm_lows(4, 2 * i, 2)
                    low_parts(C_MLP + RING + 6 * (i + 1))
                low_parts(CHUNKS + RING)
                e.close()

        @block.scalar
        def _(act):
            def high_part(g, c):
                slot = c % RING
                act.wait_ge(w_loaded[slot].sem, g * w_loaded[slot].per_group + 16 * (c // RING + 1))
                act.wait_ge(product.sem, g * CHUNKS + (c + 1))
                return act.copy(w_hi[:, slot, :], w_raw[:, slot, :])

            act.wait_ge(setup_loaded.sem, 16 * len(setups))
            act.copy(wm_hi, wm_raw).then_inc(act_set.sem, 1)
            for k in range(KT):
                act.copy(gate_part(m_hi, k), wg_raw[:, k, :]).then_inc(act_set.sem, 1)
            before = Engine(0)
            for c in range(RING):
                high_part(0, c).then_inc(*before.next(w_hi_made))
            for t in range(CT):
                act.wait_ge(pe_set.sem, t + 1)
                act.copy(wc_hi[:, t, :], ps[:, t, :]).then_inc(act_set.sem, 1)
            act.wait_ge(const_loaded.sem, 16 * len(loads))
            act.mul(half_b[:], gate_b[:], 0.5).then_inc(act_set.sem, 1)
            act.copy(ident_b[:], ident[:]).then_inc(act_set.sem, 1)
            act.copy(causal[:], causal_raw).then_inc(act_set.sem, 1)
            act.wait_ge(act_set.sem, ACT_SET)
            act.wait_ge(dve_set.sem, DVE_SET)

            def x_high(e, ahead):
                act.wait_ge(*e.at(x_loaded, 16 * (ahead + 1)))
                act.copy(v_hi[:], x_in[:]).then_inc(*e.next(x_hi_made))

            def memory_high(e, ahead, t):
                act.wait_ge(*e.at(memt_loaded, 16 * (ahead + 1)))
                act.copy(m_hi[:, t, 0:NB * CTX], memt[:, t, :]).then_inc(*e.next(m_hi_made))

            x_high(before, 0)
            for t in range(CT):
                memory_high(before, 0, t)
            with act.Fori(0, GROUPS) as g:
                e = Engine(g)
                made = [RING]

                def high_parts(end):
                    for c in range(made[0], end):
                        high_part(g, c).then_inc(*e.next(w_hi_made))
                    made[0] = max(made[0], end)

                def product_of(chunk):
                    high_parts(chunk + RING)
                    act.wait_ge(*e.at(product, chunk + 1))

                for t in range(CT):
                    act.wait_ge(*e.at(product, C_U + t + 1))
                    act.activation(l_hi[:, t, :], ps[:, 4 + t, 0:NT], ACT.Copy,
                                          scale=float(DIM) ** -0.5).then_inc(*e.next(u_hi_made))
                for b in range(NB):
                    act.wait_ge(*e.at(max0_made, b + 1))
                    act.activation(p0[:, b, :], ps[0:SEQ, b, 0:CTX], ACT.Exp,
                                          bias=max0[:, b:b + 1], accum_out=sum0[:, b:b + 1]).then_inc(*e.next(p0_made))
                for b in range(NB):
                    act.wait_ge(*e.at(am_done, b + 1))
                    act.copy(l_hi[:, CT:2 * CT, batch(b)], ps[:, b % 2, 0:CT * SEQ].rearrange(
                        "p (t s) -> p t s", t=CT)).then_inc(*e.next(am_hi_made))
                for t in range(KT):
                    product_of(C_MC + t // 2)
                    act.copy(mc[:, t, :], ps[:, 2 + t, 0:NT]).then_inc(*e.next(mc_made))
                def square(block, source, t):
                    act.activation(squares[block][:, t, :], source[:, t, :], ACT.Square,
                                          scale=float(DIM) ** -0.5).then_inc(*e.next(squared))

                def norm_highs(block, first=0, tiles=KT):
                    hi, _, now = norm_parts[block]
                    for t in range(first, first + tiles):
                        act.wait_ge(*e.at(normed, KT * block + t + 1))
                        act.copy(hi[:, t, :], now[:, t, :]).then_inc(*e.next(norm_hi_made))

                def square_fused(t):
                    act.wait_ge(*e.at(fused_made, t + 1))
                    if t == 0:
                        act.wait_ge(*e.at(stored, 0))
                    square(0, fused, t)

                for t in range(KT):
                    product_of(C_GATE + t)
                    act.activation(gate_t[:, t, :], ps[:, (6 + t) % 8, 0:NT], ACT.Tanh,
                                          bias=half_b[:, t:t + 1], scale=0.5).then_inc(*e.next(tanh_gate))
                    square_fused(t)
                norm_highs(0)
                norm_highs(1)
                for j in range(2 * KT):
                    product_of(C_QK + 2 * j + 1)
                def exponents(b):
                    act.wait_ge(*e.at(s_shifted, b + 1))
                    act.activation(prob[:, b % 2], prob[:, b % 2], ACT.Exp,
                                          scale=float(HD) ** -0.5).then_inc(*e.next(exp_done))

                def key_tiles(first, end):
                    for n in range(first, end):
                        if n < 5:
                            act.wait_ge(*e.at(ck_done, n + 1))
                        else:
                            act.wait_ge(*e.at(product, C_CK + 1))
                        t, c = divmod(n, 3)
                        act.copy(ck[:, t, c * 500:(c + 1) * 500], ps[:, n % 4, 0:500]).then_inc(*e.next(ck_made))

                def context_high(b):
                    for i, (hi, now) in enumerate(((v_hi, ctx_v), (l_hi, ctx_l))):
                        act.wait_ge(*e.at(ctx_split, 2 * b + i + 1))
                        act.copy(hi[:, :, batch(b)], now[:, b % 2]).then_inc(*e.next(ctx_hi_made))

                product_of(C_V + 1)
                exponents(0)
                product_of(C_V + 4)
                exponents(1)
                product_of(C_CK - 1)
                for b in range(NB):
                    act.copy(v_n[:, b, :], ps[0:SEQ, 4 + b, 0:DIM]).then_inc(*e.next(v_made))
                high_parts(C_CK + RING)
                for s in range(2, NB + 2):
                    b = s - 2
                    for j in range(QUADS):
                        act.wait_ge(*e.at(pt_done, b * QUADS + j + 1))
                        act.copy(prob_t[:, 4 * j:4 * j + 4, :], ps[0:SEQ, 4 + j % 2, 0:NT].rearrange(
                            "p (h s) -> p h s", h=4)).then_inc(*e.next(pt_made))
                    if s < NB:
                        exponents(s)
                    if 1 <= b < NB - 1:
                        context_high(b - 1)
                    if s == NB - 1:
                        key_tiles(0, 2)
                    if s == NB:
                        key_tiles(2, 6)
                        context_high(NB - 2)
                context_high(NB - 1)
                for t in range(KT):
                    product_of(C_DENSE + 2 * t + 1)
                    act.wait_ge(*e.at(res_made, KT + t + 1))
                    square(2, res, t)
                norm_highs(2)
                high_parts(C_CQ + 1)
                act.wait_ge(*e.at(cv_done, 6))
                act.copy(m_hi[:, 0, 0:NB * CTX], ck[:, 0, :]).then_inc(*e.next(ck_hi_made))
                high_parts(C_CQ + RING)
                for t in range(CT):
                    act.wait_ge(*e.at(product, C_CQ + t + 1))
                    act.activation(h_hi[:, t, :], ps[:, t, 0:NT], ACT.Copy,
                                   scale=float(CHD) ** -0.5).then_inc(*e.next(cq_hi_made))
                    if t == 0:
                        act.wait_ge(*e.at(cq_hi_made, 1))
                        for i in range(4):
                            act.activation(v_hi[:, i, :], h_hi[:, 0, :].bitcast(F32), ACT.Copy,
                                           scale=cmask[:, i:i + 1]).then_inc(*e.next(quad0_hi_made))
                act.copy(m_hi[:, 1, 0:NB * CTX], ck[:, 1, :]).then_inc(*e.next(ck_hi_made))
                high_parts(C_CDENSE + RING - 2)

                def cross_high(t):
                    act.wait_ge(*e.at(co_done, t + 1))
                    act.copy(v_hi[:, t, :], ps[:, 6 + t, 0:NT]).then_inc(*e.next(cctx_hi_made))

                for s in range(PAIRS + LAG):
                    if s >= LAG:
                        u = s - LAG
                        act.wait_ge(*e.at(cpt_done, u + 1))
                        heads = 1 if u % 2 else 2
                        act.copy(cpt[:, u % 2, 0:heads], ps[0:KC, 4:4 + heads, 0:NKC * SEQ]).then_inc(*e.next(cpt_made))
                    if s < PAIRS:
                        act.wait_ge(*e.at(cmax_made, s + 1))
                        if s >= 4:
                            act.wait_ge(*e.at(cpt_done, s - 3))
                        for i in range(2):
                            act.activation(cp[:, s % 4, i, :], ps[0:SEQ, cross_bank(s) + i, 0:CTX], ACT.Exp,
                                           bias=max_c[:, s % 4, i:i + 1],
                                           accum_out=sum_c[:, s % 4, i:i + 1]).then_inc(*e.next(cexp_done))
                    if s == 6 * NB + 3:
                        cross_high(0)
                cross_high(1)
                for t in range(KT // 2):
                    product_of(C_CDENSE + t)
                for t in range(KT):
                    act.wait_ge(*e.at(res_made, 2 * KT + t + 1))
                    square(3, res, t)
                norm_highs(3)
                for i in range(STEPS):
                    product_of(c_glu(i))
                    act.activation(act_t[:, i % 2, :], ps[:, 4 + 2 * (i % 2), 0:NT], ACT.Tanh,
                                          scale=0.5).then_inc(*e.next(tanh_mlp))
                    act.wait_ge(*e.at(glu_made, i + 1))
                    if i >= 2:
                        act.wait_ge(*e.at(product, c_down(i - 2) + 1))
                    act.copy(h_hi[:, i % 2, :], act_h[:, i % 2, :]).then_inc(*e.next(h_hi_made))
                    if i < KT:
                        norm_highs(4, i, 1)
                    if i == FT + 1:
                        x_high(e, 1)
                    if FT + 2 <= i < FT + 2 + CT:
                        memory_high(e, 1, i - FT - 2)
                high_parts(CHUNKS + RING)
                e.close()

        @block.tensor
        def _(pe):
            pe.sem_inc(product.sem, product.first)
            pe.wait_ge(act_set.sem, KT + 1)
            pe.wait_ge(dve_set.sem, KT + 1)
            for t in range(CT):
                for k in range(KT):
                    w = slice(t * P, (t + 1) * P)
                    _, last = split_products(pe, ps[:, t, :], wm_hi[:, k, w], wm_lo[:, k, w],
                                             gate_part(m_hi, k), gate_part(m_lo, k), k == 0, k == KT - 1)
                last.then_inc(pe_set.sem, 1)
            pe.wait_ge(dve_set.sem, KT + 1 + 6)
            pe.matmul(ps[:, 2, 0:SEQ], table_sb[:, 0, :], onehot, start=True, stop=True)
            pe.matmul(ps[:, 3, 0:SEQ], table_sb[:, 1, :], onehot, start=True, stop=True).then_inc(pe_set.sem, 1)
            pe.wait_ge(pool_set.sem, POOL_SET)
            pe.wait_ge(act_set.sem, ACT_SET)
            pe.wait_ge(dve_set.sem, DVE_SET)
            with pe.Fori(0, GROUPS) as g:
                e = Engine(g)

                def chunk(c):
                    pe.wait_ge(*e.at(w_lo_made, c + 1))
                    slot = c % RING
                    return w_hi[:, slot, :], w_lo[:, slot, :]

                def project(out, c, at, stride, tiles, x_hi, x_lo, start=True, stop=True, block=None):
                    whi, wlo = chunk(c)
                    for k in range(tiles):
                        if block is not None:
                            norm_ready(block, k)
                        w = slice(at + k * stride, at + k * stride + P)
                        first, last = split_products(pe, out, whi[:, w], wlo[:, w], x_hi[:, k, :], x_lo[:, k, :],
                                                     start and k == 0, stop and k == tiles - 1)
                    return last

                def norm_ready(block, t):
                    pe.wait_ge(*e.at((norm_lo_even, norm_lo_odd)[t % 2], block * KT // 2 + t // 2 + 1))

                pe.wait_ge(*e.at(x_lo_made, 1))
                for t in range(CT):
                    project(ps[:, 4 + t, 0:NT], C_U + t, 0, P, KT, v_hi, v_lo).then_inc(*e.next(product))
                pe.wait_ge(*e.at(m_lo_made, CT))
                pe.wait_ge(*e.at(y_made, 0))
                for t in range(CT):
                    pe.wait_ge(*e.at(u_lo_made, t + 1))
                    for b in range(NB):
                        m = slice(b * CTX, b * CTX + CEVEN)
                        _, last = split_products(pe, ps[0:SEQ, b, 0:CEVEN], l_hi[:, t, batch(b)],
                                                 l_lo[:, t, batch(b)], m_hi[:, t, m], m_lo[:, t, m],
                                                 t == 0, t == CT - 1)
                        if t == CT - 1:
                            last.then_inc(*e.next(s0_done))
                for b in range(NB):
                    pe.wait_ge(*e.at(p0_normed, b + 1))
                    if b >= 2:
                        pe.wait_ge(*e.at(pt0_made, b - 1))
                    for c in range(NKC):
                        last = pe.transpose(ps[0:KC, 6 + b % 2, c * SEQ:(c + 1) * SEQ],
                                            p0[:, b, c * KC:(c + 1) * KC], ident[0:SEQ, 0:SEQ])
                    last.then_inc(*e.next(pt0_done))
                pe.wait_ge(*e.at(memn_loaded, 16))
                for b in range(NB):
                    pe.wait_ge(*e.at(pt0_made, b + 1))
                    if b >= 2:
                        pe.wait_ge(*e.at(am_lo_made, b - 1))
                    for t in range(CT):
                        for c in range(NKC):
                            last = pe.matmul(ps[:, b % 2, t * SEQ:(t + 1) * SEQ],
                                             memn[:, b * NKC + c, t * P:(t + 1) * P],
                                             pt0[:, b % 2, c * SEQ:(c + 1) * SEQ],
                                             start=c == 0, stop=c == NKC - 1)
                    last.then_inc(*e.next(am_done))
                pe.wait_ge(*e.at(am_lo_made, NB))
                for t in range(KT):
                    last = project(ps[:, 2 + t, 0:NT], C_MC + t // 2, (t % 2) * CT * P, P, CT,
                                   l_hi[:, CT:], l_lo[:, CT:])
                    if t % 2:
                        last.then_inc(*e.next(product))
                for t in range(KT):
                    out = ps[:, (6 + t) % 8, 0:NT]
                    for k in range(CT):
                        w = slice(t * P, (t + 1) * P)
                        split_products(pe, out, wc_hi[:, k, w], wc_lo[:, k, w], l_hi[:, CT + k, :],
                                       l_lo[:, CT + k, :], k == 0, False)
                    project(out, C_GATE + t, 0, P, KT, v_hi, v_lo, start=False).then_inc(*e.next(product))

                def mean_squares(block, t, bank=6, column=0):
                    for b in range(NB):
                        last = pe.matmul(ps[0:SEQ, bank, column + b:column + b + 1], squares[block][:, t, batch(b)],
                                         ones_col[:], start=True, stop=True)
                    return last

                def norm_row(n, bank, which=0):
                    pe.wait_ge(*e.at(powered, n))
                    for b in range(NB):
                        last = pe.matmul(ps[:, bank, batch(b)], rstd_t[:, which, b:b + 1].to_broadcast([SEQ, P]),
                                         ident[0:SEQ, 0:SEQ], start=True, stop=True)
                    last.then_inc(*e.next(rstd_done))

                pe.wait_ge(*e.at(tanh_gate, KT))
                for last_tile in range(2):
                    pe.wait_ge(*e.at(sq_summed, 1 + last_tile))
                    if last_tile:
                        pe.wait_ge(*e.at(squared, KT))
                    for block in range(2):
                        last = mean_squares(block, last_tile * (KT - 1), (6, 4)[last_tile], block * NB)
                last.then_inc(*e.next(sumsq_done))
                norm_row(1, 5, 1)
                norm_row(2, 7, 0)
                for j in range(2 * KT):
                    if j >= 4:
                        pe.wait_ge(*e.at(roped, j - 3))
                    for x, (hi, lo) in enumerate(((v_hi, v_lo), (l_hi, l_lo))):
                        project(ps[:, j % 4, 0:NT], C_QK + 2 * j + x, 0, P, KT, hi, lo, start=x == 0,
                                       stop=x == 1, block=x).then_inc(*e.next(product))
                pe.wait_ge(*e.at(res_made, KT))

                def scores(b):
                    if b:
                        pe.wait_ge(*e.at(s_shifted, b))
                    for m in range(KT):
                        pe.matmul(ps[0:SEQ, m, 0:NT], ident_b[0:SEQ, 0:SEQ],
                                  causal[:].rearrange("p m s -> p (m s)"), start=True, stop=False)
                    pe.wait_ge(*e.at(kb_made, b + 1))
                    for m in range(KT):
                        last = pe.matmul(ps[0:SEQ, m, 0:NT], q_t[:, m, batch(b)],
                                         kb[:, b % 2, m].rearrange("p j s -> p (j s)"), start=False, stop=True)
                    last.then_inc(*e.next(s_done))

                for c in range(KT * EXPERTS):
                    whi, wlo = chunk(C_V + c)
                    k, expert = divmod(c, EXPERTS)
                    xh, xl = ((v_hi, v_lo), (l_hi, l_lo))[expert]
                    for b in range(NB):
                        out = ps[0:SEQ, 4 + b, :]
                        pe.matmul(out, xh[:, k, batch(b)], whi, start=c == 0, stop=False)
                        pe.matmul(out, xh[:, k, batch(b)], wlo, start=False, stop=False)
                        last = pe.matmul(out, xl[:, k, batch(b)], whi, start=False, stop=c == KT * EXPERTS - 1)
                    last.then_inc(*e.next(product))
                    if c == 1:
                        pe.wait_ge(*e.at(roped, 2 * KT))
                        scores(0)
                    if c == 4:
                        scores(1)

                def transposes(b, j):
                    if j == 2 and b >= 2:
                        pe.wait_ge(*e.at(p_normed_late, b - 1))
                    elif j % 2 == 0:
                        pe.wait_ge(*e.at(p_normed, (2 * b if b < 2 else b + 2) + j // 2 + 1))
                    if b * QUADS + j >= 2:
                        pe.wait_ge(*e.at(pt_made, b * QUADS + j - 1))
                    for i in range(4):
                        last = pe.transpose(ps[0:SEQ, 4 + j % 2, batch(i)], prob[:, b % 2, 4 * j + i, :],
                                            ident[0:SEQ, 0:SEQ])
                    last.then_inc(*e.next(pt_done))

                def context(b, j):
                    pe.wait_ge(*e.at(pt_made, b * QUADS + j + 1))
                    if b >= 2 and j == 0:
                        pe.wait_ge(*e.at(ctx_split, 2 * (b - 1)))
                    for i in range(4):
                        h = 4 * j + i
                        last = pe.matmul(ps[HD * i:HD * i + HD, 6 + b % 2, batch(j)],
                                         v_n[:, b, h * HD:(h + 1) * HD], prob_t[:, h, :], start=True, stop=True)
                    if j == QUADS - 1:
                        last.then_inc(*e.next(ctx_done))

                def key_tiles(first, end):
                    whi, wlo = chunk(C_CK)
                    for n in range(first, end):
                        t, c = divmod(n, 3)
                        if n >= 4:
                            pe.wait_ge(*e.at(ck_made, n - 3))
                        for k in range(CT):
                            w = slice((t * CT + k) * P, (t * CT + k + 1) * P)
                            m = slice(c * 500, (c + 1) * 500)
                            _, last = split_products(pe, ps[:, n % 4, 0:500], whi[:, w], wlo[:, w],
                                                     m_hi[:, k, m], m_lo[:, k, m], k == 0, k == CT - 1)
                        last.then_inc(*e.next(ck_done if n < 5 else product))

                for s in range(2, NB + 2):
                    if s < NB:
                        scores(s)
                    if s == 2:
                        pe.wait_ge(*e.at(v_made, NB))
                    for j in range(QUADS + 2):
                        if j < QUADS:
                            transposes(s - 2, j)
                        if j >= 2:
                            context(s - 2, j - 2)
                    if s == NB - 1:
                        pe.wait_ge(*e.at(s_shifted, NB))
                        key_tiles(0, 2)
                    if s == NB:
                        key_tiles(2, 6)
                pe.wait_ge(*e.at(ck_made, 6))
                pe.wait_ge(*e.at(ctx_lo_made, 2 * (NB - 1)))
                pe.wait_ge(*e.at(ctx_lo_last, 1))
                for t in range(KT):
                    project(ps[:, t, 0:NT], C_DENSE + 2 * t, 0, P, KT, v_hi, v_lo, stop=False).then_inc(*e.next(product))
                    if t == 0:
                        pe.wait_ge(*e.at(ctx_lo_last, 2))
                    project(ps[:, t, 0:NT], C_DENSE + 2 * t + 1, 0, P, KT, l_hi, l_lo, start=False).then_inc(*e.next(product))

                vhi, vlo = chunk(C_CV)
                for n in range(6):
                    if n == 2:
                        pe.wait_ge(*e.at(sq_summed, 3))
                        mean_squares(2, 0).then_inc(*e.next(sumsq_done))
                    if n == 4:
                        norm_row(3, 7)
                    if n == 2:
                        pe.wait_ge(*e.at(res_made, 2 * KT))
                    if n >= 4:
                        pe.wait_ge(*e.at(cv_made, 2 * (n - 3)))
                    for i in range(2):
                        m = slice((2 * n + i) * KC, (2 * n + i + 1) * KC)
                        out = ps[0:KC, CV_BANKS[n], i * CDIM:(i + 1) * CDIM]
                        for k in range(CT):
                            w = slice(k * CDIM, (k + 1) * CDIM)
                            pe.matmul(out, m_hi[:, k, m], vhi[:, w], start=k == 0, stop=False)
                            pe.matmul(out, m_hi[:, k, m], vlo[:, w], start=False, stop=False)
                            last = pe.matmul(out, m_lo[:, k, m], vhi[:, w], start=False, stop=k == CT - 1)
                    last.then_inc(*e.next(cv_done))
                for t in range(CT):
                    whi, wlo = chunk(C_CQ + t)
                    for k in range(KT):
                        norm_ready(2, k)
                        w = slice(k * P, (k + 1) * P)
                        first, last = split_products(pe, ps[:, t, 0:NT], whi[:, w], wlo[:, w], l_hi[:, k, :],
                                                     l_lo[:, k, :], k == 0, k == KT - 1)
                        if t == 0 and k == 0:
                            first.then_inc(*e.next(product))
                    last.then_inc(*e.next(product))
                pe.wait_ge(*e.at(ck_lo_made, 1))

                def quad(u):
                    q = cross_unit(u)[0]
                    return ((v_hi, v_lo), (l_hi, l_lo))[q % 2]

                def unit_scores(u):
                    q, b, pair = cross_unit(u)
                    if u < 2:
                        pe.wait_ge(*e.at(quad0_made, u + 1))
                        pe.wait_ge(*e.at(quad0_hi_made, 2 * (u + 1)))
                    if u == 1:
                        pe.wait_ge(*e.at(cq_lo_made, CT))
                    if u == PAIRS // 2:
                        pe.wait_ge(*e.at(ck_lo_late, 1))
                    if u and u % (2 * NB) == 0:
                        pe.wait_ge(*e.at(quad_made, q))
                    if u >= 2:
                        pe.wait_ge(*e.at(cexp_done, 2 * (u - 1)))
                    m = slice(b * CTX, b * CTX + CEVEN)
                    for i in range(2):
                        hi, lo = (part[:, 2 * pair + i, batch(b)] for part in quad(u))
                        _, last = split_products(pe, ps[0:SEQ, cross_bank(u) + i, 0:CEVEN], hi, lo,
                                                 m_hi[:, q // 2, m], m_lo[:, q // 2, m], True, True)
                    last.then_inc(*e.next(cs_done))

                def unit_transposes(u):
                    pe.wait_ge(*e.at(cp_normed, u + 1))
                    if u:
                        pe.wait_ge(*e.at(cpt_made, u))
                    if u and u % 2 == 0:
                        pe.wait_ge(*e.at(cpt_odd_made, u // 2))
                    for i in range(2):
                        for c in range(NKC):
                            last = pe.transpose(ps[0:KC, 4 + i, c * SEQ:(c + 1) * SEQ],
                                                cp[:, u % 4, i, c * KC:(c + 1) * KC], ident[0:SEQ, 0:SEQ])
                    last.then_inc(*e.next(cpt_done))

                def unit_context(u):
                    q, b, pair = cross_unit(u)
                    pe.wait_ge(*e.at(cpt_made, u + 1))
                    if u % 2:
                        pe.wait_ge(*e.at(cpt_odd_made, u // 2 + 1))
                    if u == 0:
                        pe.wait_ge(*e.at(cv_made, 12))
                    r = 64 * (q % 2) + 32 * pair
                    for i in range(2):
                        for c in range(NKC):
                            last = pe.matmul(ps[r:r + 32, 6 + q // 2, batch(b)],
                                             cv[:, b * NKC + c, 2 * q + pair, 32 * i:32 * i + 32],
                                             cpt[:, u % 2, i, c * SEQ:(c + 1) * SEQ],
                                             start=i + c == 0, stop=i == 1 and c == NKC - 1)
                    if u % (PAIRS // 2) == PAIRS // 2 - 1:
                        last.then_inc(*e.next(co_done))

                for s in range(PAIRS + LAG + 1):
                    if s < PAIRS:
                        unit_scores(s)
                    if LAG <= s < PAIRS + LAG:
                        unit_transposes(s - LAG)
                    if s > LAG:
                        unit_context(s - LAG - 1)
                for k in range(CT):
                    pe.wait_ge(*e.at(cctx_lo_made, k + 1))
                    for t in range(KT):
                        whi, wlo = chunk(C_CDENSE + t // 2)
                        w = slice(((t % 2) * CT + k) * P, ((t % 2) * CT + k + 1) * P)
                        _, last = split_products(pe, ps[:, t, 0:NT], whi[:, w], wlo[:, w], v_hi[:, k, :],
                                                 v_lo[:, k, :], k == 0, k == CT - 1)
                        if k == CT - 1:
                            last.then_inc(*e.next(product if t % 2 else cdense_even))
                pe.wait_ge(*e.at(sq_summed, 4))
                mean_squares(3, 0).then_inc(*e.next(sumsq_done))
                norm_row(4, 7)

                def glu(i):
                    xh, xl = ((v_hi, v_lo), (l_hi, l_lo))[i // FT]
                    if i == 1:
                        pe.wait_ge(*e.at(rstd_read, 1))
                    if i >= 2:
                        pe.wait_ge(*e.at(glu_made, i - 1))
                    for up in range(2):
                        project(ps[:, 4 + 2 * (i % 2) + up, 0:NT], c_glu(i) + up, 0, P, KT, xh, xl, block=3 + i // FT).then_inc(*e.next(product))

                def down(i):
                    whi, wlo = chunk(c_down(i))
                    pe.wait_ge(*e.at(h_lo_made, i + 1))
                    for t in range(KT):
                        w = slice(t * P, (t + 1) * P)
                        _, last = split_products(pe, ps[:, t, 0:NT], whi[:, w], wlo[:, w], h_hi[:, i % 2, :],
                                                 h_lo[:, i % 2, :], i == 0, i == STEPS - 1)
                        if i == STEPS - 1 and t < KT - 1:
                            last.then_inc(*e.next(down_done))
                    last.then_inc(*e.next(product))

                glu(0)
                for i in range(1, STEPS):
                    glu(i)
                    down(i - 1)
                down(STEPS - 1)
                e.close()

        @block.vector
        def _(dve):
            dve.sem_inc(y_made.sem, y_made.first)
            made = [0]

            def setup(instruction, wait=True):
                instruction.then_inc(dve_set.sem, 1)
                made[0] += 1
                if wait:
                    dve.wait_ge(dve_set.sem, made[0])

            dve.wait_ge(act_set.sem, KT + 1)
            setup(dve.tensor_tensor(wm_lo, wm_raw, wm_hi.bitcast(F32), ALU.subtract))
            for k in range(KT):
                setup(dve.tensor_tensor(gate_part(m_lo, k), wg_raw[:, k, :],
                                        gate_part(m_hi, k).bitcast(F32), ALU.subtract))
            dve.wait_ge(pool_set.sem, POOL_SET)
            setup(dve.tensor_copy(row_f, row_i))
            setup(dve.tensor_copy(pos_f, pos_i))
            setup(dve.tensor_scalar(pos_neg, pos_f, 0.0, float(SEQ), ALU.is_lt, ALU.mult))
            setup(dve.tensor_tensor(pos_f, pos_f, pos_neg, ALU.add))
            setup(dve.tensor_scalar(pos_f, pos_f, 0.0, float(SEQ - 1), ALU.max, ALU.min))
            setup(dve.tensor_tensor(onehot, pos_f, row_f, ALU.is_equal))
            setup(dve.memset(ones_col[:], 1.0))
            dve.wait_ge(pe_set.sem, CT + 1)
            setup(dve.tensor_copy(cos_t[:], ps[:, 2, 0:SEQ]))
            setup(dve.tensor_copy(sin_t[:], ps[:, 3, 0:SEQ]))
            dve.wait_ge(act_set.sem, KT + CT + 1)
            for t in range(CT):
                setup(dve.tensor_tensor(wc_lo[:, t, :], ps[:, t, :], wc_hi[:, t, :].bitcast(F32), ALU.subtract))
            setup(dve.memset(m_hi[:, :, NB * CTX:CPAD].bitcast(F32), 0.0))
            setup(dve.memset(m_lo[:, :, NB * CTX:CPAD].bitcast(F32), 0.0))
            dve.wait_ge(const_loaded.sem, 16 * len(loads))
            setup(dve.tensor_tensor(norm_w00[:], norm_w[:, 0, :], norm_w[:, 0, :], ALU.mult))
            setup(dve.tensor_scalar(norm_w00[:], norm_w00[:], 1.0 / DIM, None, ALU.mult))
            setup(dve.tensor_tensor(norm_w01[:], norm_w[:, 0, :], norm_w[:, 1, :], ALU.mult))
            assert made[0] == DVE_SET

            def low(out, source, high, signal, by=None):
                dve.tensor_tensor(out, source, high.bitcast(F32), ALU.subtract).then_inc(*(by or e).next(signal))

            def x_low(e):
                dve.wait_ge(*e.at(x_hi_made, 1 + (e is not before)))
                low(v_lo[:], x_in[:], v_hi[:], x_lo_made, e)

            def memory_low(e, t):
                dve.wait_ge(*e.at(m_hi_made, t + 1 + CT * (e is not before)))
                low(m_lo[:, t, 0:NB * CTX], memt[:, t, :], m_hi[:, t, 0:NB * CTX], m_lo_made, e)

            before = Engine(0)
            x_low(before)
            for t in range(CT):
                memory_low(before, t)
            with dve.Fori(0, GROUPS) as g:
                e = Engine(g)

                for t in range(CT):
                    dve.wait_ge(*e.at(u_hi_made, t + 1))
                    dve.scalar_tensor_tensor(l_lo[:, t, :], ps[:, 4 + t, 0:NT], float(DIM) ** -0.5,
                                                    l_hi[:, t, :].bitcast(F32), ALU.mult, ALU.subtract).then_inc(*e.next(u_lo_made))
                for b in range(NB + 1):
                    if b < NB:
                        dve.wait_ge(*e.at(s0_done, b + 1))
                        dve.tensor_reduce(max0[:, b:b + 1], ps[0:SEQ, b, 0:CTX], AX_X, ALU.max,
                                          negate=True).then_inc(*e.next(max0_made))
                    if b:
                        dve.wait_ge(*e.at(p0_made, b))
                        dve.reciprocal(rsum0[:, b - 1:b], sum0[:, b - 1:b]).then_inc(*e.next(step))
                        dve.wait_ge(*e.own())
                        dve.tensor_scalar(p0[:, b - 1, :], p0[:, b - 1, :], rsum0[:, b - 1:b], None,
                                          ALU.mult).then_inc(*e.next(p0_normed))
                for b in range(NB):
                    dve.wait_ge(*e.at(pt0_done, b + 1))
                    if b >= 2:
                        dve.wait_ge(*e.at(am_done, b - 1))
                    dve.tensor_copy(pt0[:, b % 2, :], ps[0:KC, 6 + b % 2, 0:NKC * SEQ]).then_inc(*e.next(pt0_made))
                    if b:
                        dve.wait_ge(*e.at(am_hi_made, b))
                        low(l_lo[:, CT:2 * CT, batch(b - 1)], ps[:, (b - 1) % 2, 0:CT * SEQ].rearrange(
                            "p (t s) -> p t s", t=CT), l_hi[:, CT:2 * CT, batch(b - 1)], am_lo_made)
                dve.wait_ge(*e.at(am_hi_made, NB))
                low(l_lo[:, CT:2 * CT, batch(NB - 1)], ps[:, (NB - 1) % 2, 0:CT * SEQ].rearrange(
                    "p (t s) -> p t s", t=CT), l_hi[:, CT:2 * CT, batch(NB - 1)], am_lo_made)

                dve.wait_ge(*e.at(mask_loaded, 16))
                dve.tensor_scalar(is_pad[:], tt_in[:], 1, None, ALU.is_equal).then_inc(*e.next(masks_made))
                dve.wait_ge(*e.own())
                dve.memset(is_v[:, :, SEQ - 1:SEQ], 0.0).then_inc(*e.next(step))
                dve.tensor_tensor(is_v[:, :, 0:SEQ - 1], is_pad[:, :, 0:SEQ - 1],
                                         is_pad[:, :, 1:SEQ], ALU.mult).then_inc(*e.next(step))
                dve.wait_ge(*e.own())
                dve.tensor_scalar(is_l[:], is_v[:], -1.0, 1.0, ALU.mult, ALU.add).then_inc(*e.next(step))

                def add_square(block, t, signal):
                    sq = squares[block]
                    dve.tensor_tensor(sq[:, 0, :], sq[:, 0, :], sq[:, t, :], ALU.add).then_inc(*e.next(signal))

                def add_squares(t, signal):
                    dve.wait_ge(*e.at(squared, t + 1))
                    dve.wait_ge(*e.own())
                    add_square(1, t, step)
                    add_square(0, t, signal)

                for t in range(KT):
                    dve.wait_ge(*e.at(mc_made, t + 1))
                    dve.wait_ge(*e.at(tanh_gate, t + 1))
                    dve.scalar_tensor_tensor(gate_t[:, t, :], gate_t[:, t, :], 1.0, mc[:, t, :],
                                                    ALU.add, ALU.mult).then_inc(*e.next(step))
                    dve.wait_ge(*e.own())
                    dve.scalar_tensor_tensor(fused[:, t, :], gate_t[:, t, :], 0.5, x_in[:, t, :],
                                                    ALU.mult, ALU.add).then_inc(*e.next(fused_made))
                    dve.wait_ge(*e.own())
                    dve.scalar_tensor_tensor(squares[1][:, t, :], fused[:, t, :], norm_w00[:, t:t + 1],
                                             fused[:, t, :], ALU.mult, ALU.mult).then_inc(
                                                 *e.next(sq_summed if t == KT - 1 else step))
                    if 1 <= t < KT - 1:
                        add_squares(t, sq_summed if t == KT - 2 else step)

                def mean(n):
                    dve.wait_ge(*e.at(sumsq_done, n))
                    dve.wait_ge(*e.at(powered, n))
                    dve.tensor_scalar(mean_sq[:, 0], ps[0:SEQ, 6, 0:NB], EPS, None, ALU.add).then_inc(*e.next(mean_made))

                def norm_tile(block, source, weight, t, row):
                    now = norm_parts[block][2]
                    dve.scalar_tensor_tensor(now[:, t, :], source[:, t, :], weight[:, t:t + 1], row,
                                                    ALU.mult, ALU.mult).then_inc(*e.next(normed))

                def norm_low(block, t):
                    hi, lo, now = norm_parts[block]
                    dve.wait_ge(*e.at(norm_hi_made, KT * block + t + 1))
                    low(lo[:, t, :], now[:, t, :], hi[:, t, :], norm_lo_even)

                def norm_tiles(block, source, weight, row):
                    for t in range(KT):
                        norm_tile(block, source, weight, t, row)
                        if t % 2:
                            norm_low(block, t - 1)

                def before_norm(block, source, weight, mask_of, t):
                    dve.scalar_tensor_tensor(norm_parts[block][2][:, t, :], source[:, t, :], weight[:, t:t + 1],
                                             mask_of[:].rearrange("p b s -> p (b s)"), ALU.mult,
                                             ALU.mult).then_inc(*e.next(step))

                def finish_norm(block, bank):
                    for t in range(KT):
                        now = norm_parts[block][2][:, t, :]
                        dve.tensor_tensor(now, now, ps[:, bank, 0:NT], ALU.mult).then_inc(*e.next(normed))
                        if t % 2:
                            norm_low(block, t - 1)

                def mask_row(row, mask_of, bank, made=step):
                    dve.tensor_tensor(row[:], ps[:, bank, 0:NT], mask_of[:].rearrange("p b s -> p (b s)"),
                                             ALU.mult).then_inc(*e.next(made))

                def residual(n, t):
                    dve.tensor_tensor(res[:, t, :], ps[:, t, 0:NT], res[:, t, :], ALU.add).then_inc(*e.next(res_made))
                    if t >= 2:
                        dve.wait_ge(*e.at(squared, KT * (n - 1) + t))
                        dve.wait_ge(*e.own())
                        add_square(n, t - 1, step)
                    if t == KT - 1:
                        dve.wait_ge(*e.at(squared, KT * n))
                        dve.wait_ge(*e.own())
                        add_square(n, t, sq_summed)

                for t in range(KT):
                    before_norm(0, fused, norm_w01, is_v, t)
                dve.wait_ge(*e.at(sumsq_done, 1))
                dve.tensor_copy(mean_sq[:, 1], ps[0:SEQ, 6, NB:2 * NB]).then_inc(*e.next(step))
                dve.tensor_scalar(mean_sq[:, 0], ps[0:SEQ, 6, 0:NB], EPS, None, ALU.add).then_inc(*e.next(step))
                dve.wait_ge(*e.own())
                dve.tensor_tensor(mean_sq[:], mean_sq[:], ps[0:SEQ, 4, 0:2 * NB].rearrange("p (n b) -> p n b", n=2),
                                  ALU.add).then_inc(*e.next(step))
                dve.wait_ge(*e.own())
                dve.scalar_tensor_tensor(mean_sq[:, 1], mean_sq[:, 0], EPS, mean_sq[:, 1],
                                         ALU.mult, ALU.add).then_inc(*e.next(mean_made))
                for t in range(KT):
                    before_norm(1, fused, norm_w01, is_l, t)
                dve.wait_ge(*e.own())
                dve.wait_ge(*e.at(rstd_done, 1))
                finish_norm(0, 5)
                finish_norm(1, 5)
                dve.wait_ge(*e.at(rstd_done, 2))
                for t in range(KT):
                    dve.scalar_tensor_tensor(res[:, t, :], fused[:, t, :], norm_w[:, 0, t:t + 1],
                                                    ps[:, 7, 0:NT], ALU.mult, ALU.mult).then_inc(*e.next(res_made))
                dve.wait_ge(*e.own())
                for j in range(2 * KT):
                    out = (q_t, k_t)[j // KT][:, j % KT, :]
                    now, s = ps[:, j % 4, 0:NT], j % 2
                    dve.wait_ge(*e.at(product, C_QK + 2 * j + 2))
                    if j >= 2:
                        dve.wait_ge(*e.own())
                    dve.tensor_tensor(roc[:, s, :].rearrange("p (b s) -> p b s", b=NB),
                                             now.rearrange("p (b s) -> p b s", b=NB),
                                             cos_t[:].unsqueeze(1).to_broadcast([P, NB, SEQ]), ALU.mult).then_inc(*e.next(step))
                    dve.stream_shuffle(rot[:, s, :], now, [(i + HD // 2) % HD for i in range(HD)]).then_inc(*e.next(rotated))
                    dve.wait_ge(*e.own())
                    dve.tensor_tensor(rot[:, s, :].rearrange("p (b s) -> p b s", b=NB),
                                             rot[:, s, :].rearrange("p (b s) -> p b s", b=NB),
                                             sin_t[:].unsqueeze(1).to_broadcast([P, NB, SEQ]), ALU.mult).then_inc(*e.next(step))
                    dve.wait_ge(*e.own())
                    dve.tensor_tensor(out, rot[:, s, :], roc[:, s, :], ALU.add).then_inc(*e.next(roped))
                def key_blocks(b):
                    for j in range(4):
                        dve.tensor_scalar(kb[:, b % 2, :, j, :], k_t[:, :, batch(b)], smask[:, j:j + 1], None,
                                                 ALU.mult).then_inc(*e.next(kb_made if j == 3 else step))

                dve.wait_ge(*e.own())
                key_blocks(0)
                key_blocks(1)
                for s in range(NB + 3):
                    if s < NB:
                        dve.wait_ge(*e.at(s_done, s + 1))
                        now = ps[0:SEQ, 0:4, 0:NT].rearrange("p m (j s) -> p m j s", j=4)
                        dve.tensor_reduce(max_s[:].rearrange("p (m j) -> p m j", j=4), now, AX_X, ALU.max).then_inc(*e.next(step))
                        dve.wait_ge(*e.own())
                        if s >= 2:
                            dve.wait_ge(*e.at(pt_done, (s - 1) * QUADS))
                        dve.tensor_tensor(
                            prob[:, s % 2].rearrange("p (m j) s -> p m j s", j=4), now,
                            max_s[:].rearrange("p (m j) -> p m j", j=4).unsqueeze(3).to_broadcast([SEQ, KT, 4, SEQ]),
                            ALU.subtract).then_inc(*e.next(s_shifted))
                        if s + 2 < NB:
                            key_blocks(s + 2)
                    if 2 <= s - 1 < NB:
                        u = (s - 1) % 2
                        dve.wait_ge(*e.at(rsum_made, s))
                        dve.tensor_tensor(
                            prob[:, u, 8:, :], prob[:, u, 8:, :],
                            rsum_s[:, u, 8:].unsqueeze(2).to_broadcast([SEQ, 8, SEQ]),
                            ALU.mult).then_inc(*e.next(p_normed_late))
                    if s >= 3:
                        b = s - 3
                        dve.wait_ge(*e.at(ctx_done, b + 1))
                        if b >= 2:
                            dve.wait_ge(*e.at(ctx_lo_made, 2 * (b - 1)))
                        now = ps[:, 6 + b % 2, 0:NT].rearrange("p (t s) -> p t s", t=KT)
                        for out, mask_of in ((ctx_v, is_v), (ctx_l, is_l)):
                            dve.tensor_tensor(out[:, b % 2], now,
                                                     mask_of[:, b, :].unsqueeze(1).to_broadcast([P, KT, SEQ]),
                                                     ALU.mult).then_inc(*e.next(ctx_split))
                    if s < NB:
                        dve.wait_ge(*e.at(exp_done, s + 1))
                        dve.tensor_reduce(rsum_s[:, s % 2, :], prob[:, s % 2], AX_X, ALU.add).then_inc(*e.next(step))
                        dve.wait_ge(*e.own())
                        dve.reciprocal(rsum_s[:, s % 2, :], rsum_s[:, s % 2, :]).then_inc(*e.next(rsum_made))
                b = NB - 1
                dve.wait_ge(*e.at(ctx_hi_made, 2 * b + 1))
                low(v_lo[:, :, batch(b)], ctx_v[:, b % 2], v_hi[:, :, batch(b)], ctx_lo_last)
                dve.wait_ge(*e.at(ctx_hi_made, 2 * b + 2))
                low(l_lo[:, :, batch(b)], ctx_l[:, b % 2], l_hi[:, :, batch(b)], ctx_lo_last)
                for t in range(KT):
                    dve.wait_ge(*e.at(product, C_DENSE + 2 * t + 2))
                    residual(2, t)
                dve.wait_ge(*e.at(czero_set, 1))
                for n in range(6):
                    if n == 2:
                        mean(2)
                    if n == 4:
                        dve.wait_ge(*e.at(rstd_done, 3))
                        norm_tiles(2, res, norm_w[:, 2, :], ps[:, 7, 0:NT])
                    dve.wait_ge(*e.at(cv_done, n + 1))
                    now = ps[0:KC, CV_BANKS[n], :].rearrange("p (i h d) -> p i h d", i=2, h=HEADS // 2)
                    for odd in range(2):
                        dve.tensor_copy(cv[:, 2 * n:2 * n + 2, :, 3 * CHD * odd:3 * CHD * odd + CHD],
                                               now[:, :, :, CHD * odd:CHD * odd + CHD]).then_inc(*e.next(cv_made))
                dve.wait_ge(*e.at(ck_hi_made, 1))
                low(m_lo[:, 0, 0:NB * CTX], ck[:, 0, :], m_hi[:, 0, 0:NB * CTX], ck_lo_made)
                def query_low(t):
                    dve.wait_ge(*e.at(cq_hi_made, t + 1))
                    dve.scalar_tensor_tensor(h_lo[:, t, :], ps[:, t, 0:NT], float(CHD) ** -0.5,
                                             h_hi[:, t, :].bitcast(F32), ALU.mult, ALU.subtract).then_inc(
                                                 *e.next(cq_lo_made))

                query_low(0)
                dve.wait_ge(*e.own())
                for i in range(4):
                    dve.tensor_scalar(v_lo[:, i, :], h_lo[:, 0, :].bitcast(F32), cmask[:, i:i + 1], None,
                                      ALU.mult).then_inc(*e.next(quad0_made if i % 2 else step))
                query_low(1)

                def cross_low(t):
                    dve.wait_ge(*e.at(cctx_hi_made, t + 1))
                    low(v_lo[:, t, :], ps[:, 6 + t, 0:NT], v_hi[:, t, :], cctx_lo_made)

                for s in range(PAIRS + LAG):
                    if s < PAIRS:
                        dve.wait_ge(*e.at(cs_done, s + 1))
                        if s >= 4:
                            dve.wait_ge(*e.at(cexp_done, 2 * (s - 3)))
                        dve.tensor_reduce(max_c[:, s % 4, :], ps[0:SEQ, cross_bank(s):cross_bank(s) + 2, 0:CTX],
                                          AX_X, ALU.max, negate=True).then_inc(*e.next(cmax_made))
                    if s >= LAG and (s - LAG) % 2:
                        dve.wait_ge(*e.at(cpt_done, s - LAG + 1))
                        dve.tensor_copy(cpt[:, 1, 1], ps[0:KC, 5, 0:NKC * SEQ]).then_inc(*e.next(cpt_odd_made))
                    if 1 <= s <= PAIRS:
                        u = (s - 1) % 4
                        dve.wait_ge(*e.at(cexp_done, 2 * s))
                        dve.reciprocal(rsum_c[:, u, :], sum_c[:, u, :]).then_inc(*e.next(step))
                        dve.wait_ge(*e.own())
                        for i in range(2):
                            dve.tensor_scalar(cp[:, u, i, :], cp[:, u, i, :], rsum_c[:, u, i:i + 1], None,
                                              ALU.mult).then_inc(*e.next(cp_normed if i else step))
                    if s == 6 * NB + 4:
                        cross_low(0)
                cross_low(1)
                for t in range(KT):
                    if t % 2:
                        dve.wait_ge(*e.at(product, C_CDENSE + t // 2 + 1))
                    else:
                        dve.wait_ge(*e.at(cdense_even, t // 2 + 1))
                    residual(3, t)
                for t in range(2):
                    before_norm(3, res, norm_w[:, 3, :], is_v, t)
                mean(3)
                for t in range(2, KT):
                    before_norm(3, res, norm_w[:, 3, :], is_v, t)
                dve.wait_ge(*e.own())
                dve.wait_ge(*e.at(rstd_done, 4))
                finish_norm(3, 7)
                mask_row(rstd_l, is_l, 7, rstd_read)
                dve.wait_ge(*e.own())
                for i in range(STEPS):
                    s = i % 2
                    dve.wait_ge(*e.at(tanh_mlp, i + 1))
                    if i >= 2:
                        dve.wait_ge(*e.at(h_lo_made, i - 1))
                    dve.scalar_tensor_tensor(act_a[:, s, :], act_t[:, s, :], 1.0, ps[:, 4 + 2 * s, 0:NT],
                                             ALU.add, ALU.mult).then_inc(*e.next(step))
                    dve.wait_ge(*e.own())
                    dve.wait_ge(*e.at(product, c_glu(i) + 2))
                    dve.scalar_tensor_tensor(act_h[:, s, :], act_a[:, s, :], 0.5, ps[:, 5 + 2 * s, 0:NT],
                                             ALU.mult, ALU.mult).then_inc(*e.next(glu_made))
                    dve.wait_ge(*e.at(h_hi_made, i + 1))
                    low(h_lo[:, s, :], act_h[:, s, :], h_hi[:, s, :], h_lo_made)
                    if i < KT:
                        norm_tile(4, res, norm_w[:, 3, :], i, rstd_l[:])
                        if i % 2:
                            norm_low(4, i - 1)
                    if i == FT + 2:
                        x_low(e)
                    if FT + 3 <= i < FT + 3 + CT:
                        memory_low(e, i - FT - 3)
                dve.wait_ge(*e.at(stored, 0))
                for t in range(KT):
                    if t < KT - 1:
                        dve.wait_ge(*e.at(down_done, t + 1))
                    else:
                        dve.wait_ge(*e.at(product, CHUNKS))
                    dve.tensor_tensor(y_out[:, t, :], ps[:, t, 0:NT], res[:, t, :], ALU.add).then_inc(*e.next(y_made))
                e.close()


def kernel(**inputs):
    import numpy as np
    import concourse.bacc as bacc
    from concourse.bass_utils import run_bass_kernel_spmd

    a = {name: np.asarray(x) for name, x in inputs.items()}

    def w(name, layer=1):
        return a[f"L{layer}_xattn_{name}"]

    def by_tile(m, n=None):
        m = m if n is None else m[:, n * P:(n + 1) * P]
        return m.reshape(-1, P, m.shape[1]).transpose(1, 0, 2)

    def flat(*blocks):
        return np.concatenate([x.reshape(P, -1) for x in blocks], axis=1)

    def padded(m, axis):
        wide = [(0, 0), (0, 0)]
        wide[axis] = (0, FT * P - INTER)
        return np.pad(m, wide)

    w_mem, w_gate = w("W_mem", 0), w("W_gate", 0).T
    qkv, dense = (w("v_qkv"), w("l_qkv")), (w("v_dense"), w("l_dense"))
    gates = [padded(w(f"{n}_gate"), 1) for n in "vl"]
    ups = [padded(w(f"{n}_up"), 1) for n in "vl"]
    downs = [padded(w(f"{n}_down"), 0) for n in "vl"]
    chunks = [flat(by_tile(w_mem, t)) for t in range(CT)]
    chunks += [flat(by_tile(w_mem.T, 2 * c), by_tile(w_mem.T, 2 * c + 1)) for c in range(KT // 2)]
    chunks += [flat(by_tile(w_gate[:DIM], t)) for t in range(KT)]
    chunks += [flat(by_tile(qkv[x], j)) for j in range(2 * KT) for x in range(EXPERTS)]
    chunks += [qkv[x][k * P:(k + 1) * P, 2 * DIM:] for k in range(KT) for x in range(EXPERTS)]
    ckv = w("ckv_w")
    chunks.append(flat(by_tile(ckv, 0), by_tile(ckv, 1)))
    chunks += [flat(by_tile(dense[x], t)) for t in range(KT) for x in range(EXPERTS)]
    chunks.append(flat(by_tile(ckv[:, CDIM:])))
    chunks += [flat(by_tile(w("cq_w"), t)) for t in range(CT)]
    cd = w("cdense_w")
    chunks += [flat(by_tile(cd, 2 * c), by_tile(cd, 2 * c + 1)) for c in range(KT // 2)]
    mlp = [None] * (3 * STEPS)
    for i in range(STEPS):
        x, f = divmod(i, FT)
        mlp[c_glu(i) - C_MLP] = flat(by_tile(gates[x], f))
        mlp[c_glu(i) + 1 - C_MLP] = flat(by_tile(ups[x], f))
        mlp[c_down(i) - C_MLP] = downs[x][f * P:(f + 1) * P]
    weights = np.stack(chunks + mlp)
    assert weights.shape == (CHUNKS, P, 512)

    angle = np.outer(np.arange(SEQ, dtype=np.float32),
                     np.float32(1) / np.float32(10000) ** (np.arange(0, HD, 2, dtype=np.float32) / np.float32(HD)))
    cos, sin = np.cos(angle), np.sin(angle)
    tables = np.stack([np.tile(np.concatenate([cos, cos], 1), (1, P // HD)),
                       np.tile(np.concatenate([-sin, sin], 1), (1, P // HD))], 1).astype(np.float32)
    after = np.triu(np.full((SEQ, SEQ), MASKED, np.float32), 1)
    causal = np.repeat(after[:, None, :], NB, 1)
    head_masks = np.concatenate([np.equal.outer(np.arange(P) // width, np.arange(P // width))
                                 for width in (CHD, HD)], 1).astype(np.float32)

    x, mem = a["x"], a["ctx_1024"]
    arrays = {
        "x_t": x.reshape(GROUPS, NT, KT, P).transpose(0, 3, 2, 1),
        "mem_t": mem.reshape(GROUPS, NB * CTX, CT, P).transpose(0, 3, 2, 1),
        "mem_n": mem.reshape(GROUPS, NB * NKC, KC, CDIM).transpose(0, 2, 1, 3),
        "weights": weights,
        "w_gate_mem": by_tile(w_gate[DIM:]),
        "w_mem": by_tile(w_mem),
        "b_gate": w("b_gate", 0).reshape(KT, P).T,
        "norms": np.stack([n.reshape(KT, P).T for n in (
            w("norm_w", 0), w("ln_in_w"), w("ln_post_cross_w"), w("ln_post_attn_w"))], 1),
        "pos": a["pos_1xS"],
        "mask": a["mask_BxS_ik0"].reshape(GROUPS, 1, NT),
        "rope_tables": tables,
        "identity_in": np.eye(P, dtype=np.float32),
        "causal_in": causal,
        "head_masks": head_masks,
    }
    for name in ("x_t", "mem_t", "mem_n", "mask"):
        arrays[name] = np.concatenate([arrays[name], arrays[name][:1]])
    arrays = {name: np.ascontiguousarray(x) for name, x in arrays.items()}
    nc = bacc.Bacc("TRN2", target_bir_lowering=False, num_devices=1)
    args = {name: nc.dram_tensor(name, x.shape, mybir.dt.from_np(x.dtype), kind="ExternalInput").ap()
            for name, x in arrays.items()}
    out = nc.dram_tensor("out_t", (GROUPS, P, KT, NT), F32, kind="ExternalOutput").ap()
    build_xattn(nc, **args, out_t=out)
    got = run_bass_kernel_spmd(nc, [arrays], core_ids=[0]).results[0]["out_t"]
    return got.transpose(0, 3, 2, 1).reshape(BATCHES, SEQ, DIM)
```
